# Optimizing a Trainium2 kernel written in Bass

```python
import numpy as np
import jax
import jax.numpy as jnp

def _softmax(x, axis=-1):
    return jax.nn.softmax(x, axis=axis)

def _gelu(x):
    return jax.nn.gelu(x, approximate=True)

def _silu(x):
    return jax.nn.silu(x)

def _sigmoid(x):
    return jax.nn.sigmoid(x)

def _layernorm(x, axis=-1, eps=1e-05):
    m = jnp.mean(x, axis=axis, keepdims=True)
    v = jnp.var(x, axis=axis, keepdims=True)
    return (x - m) / jnp.sqrt(v + eps)

def _scatter_add(tgt, idx, src, axis=0):
    return tgt.at[idx].add(src)

def _segment_sum(src, seg, n):
    return jax.ops.segment_sum(src, seg, n)
kernel_name = 'mk_gnn_ffn_d1_gnn_r32_6bc6be'

def setup_inputs(seed: int=0):
    np.random.seed(seed)
    _w = jnp.asarray

    def _rec_inputs():
        import jax
        import jax.numpy as jnp
        _gk = jax.random.key(seed)
        x = -0.0003713 + 1 * jax.random.normal(jax.random.fold_in(_gk, 1), (3125, 256), jnp.float32)
        src = jax.random.randint(jax.random.fold_in(_gk, 2), (50000,), 0, 3125, jnp.int32)
        dst = jax.random.randint(jax.random.fold_in(_gk, 3), (50000,), 0, 3125, jnp.int32)
        _o = jnp.argsort(dst, stable=True)
        src = src[_o]
        dst = dst[_o]
        return (x, src, dst)
    x, src, dst = _rec_inputs()

    def _L0_gnn_setup():
        import jax, jax.numpy as jnp
        import numpy as np
        HEAD = 8
        D = 128
        GIN = 256
        GOUT = 256
        N = 50000
        E = 25000

        def gt_layer(edge_index, embeds, qT, kT, vT, ln_s, ln_b):
            rows, cols = (edge_index[0], edge_index[1])
            n, d = embeds.shape
            hd = d // HEAD
            rowE = embeds[rows]
            colE = embeds[cols]
            q = (rowE @ qT).reshape(-1, HEAD, hd)
            k = (colE @ kT).reshape(-1, HEAD, hd)
            v = (colE @ vT).reshape(-1, HEAD, hd)
            att = jnp.clip(jnp.einsum('ehd,ehd->eh', q, k), -10.0, 10.0)
            expAtt = jnp.exp(att)
            attNorm = jax.ops.segment_sum(expAtt, rows, num_segments=n)[rows]
            att = expAtt / (attNorm + 1e-08)
            res = (att[..., None] * v).reshape(-1, d)
            agg = jax.ops.segment_sum(res, rows, num_segments=n)
            out = agg + embeds
            mu = jnp.mean(out, axis=-1, keepdims=True)
            var = jnp.mean((out - mu) ** 2, axis=-1, keepdims=True)
            return (out - mu) / jnp.sqrt(var + 1e-06) * ln_s + ln_b
        key = jax.random.key(seed)
        ks = jax.random.split(key, 16)

        def xavier(k, shape):
            lim = np.sqrt(6.0 / (shape[0] + shape[1]))
            return jax.random.uniform(k, shape, jnp.float32, -lim, lim)
        inp = {'x': jax.random.normal(ks[0], (N, GIN), jnp.float32), 'edge_index': jax.random.randint(ks[1], (2, E), 0, N, jnp.int64), 'W_P_w': xavier(ks[2], (GIN, D)), 'W_P_b': jnp.zeros((D,), jnp.float32), 'W_pos': jax.random.uniform(ks[3], (1, D), jnp.float32, -0.02, 0.02), 'q1': xavier(ks[4], (D, D)), 'k1': xavier(ks[5], (D, D)), 'v1': xavier(ks[6], (D, D)), 'ln1_s': jnp.ones((D,), jnp.float32), 'ln1_b': jnp.zeros((D,), jnp.float32), 'q2': xavier(ks[7], (D, D)), 'k2': xavier(ks[8], (D, D)), 'v2': xavier(ks[9], (D, D)), 'ln2_s': jnp.ones((D,), jnp.float32), 'ln2_b': jnp.zeros((D,), jnp.float32), 'inv_w': xavier(ks[10], (D, GOUT)), 'inv_b': jnp.zeros((GOUT,), jnp.float32)}
        return inp
    _L0_gnn_all = _L0_gnn_setup()
    _L0_gnn_in = {k: v for k, v in _L0_gnn_all.items() if k in ('W_P_w', 'W_P_b', 'W_pos', 'q1', 'k1', 'v1', 'ln1_s', 'ln1_b', 'q2', 'k2', 'v2', 'ln2_s', 'ln2_b', 'inv_w', 'inv_b')}
    del _L0_gnn_all

    def _L0_ffn_setup():
        import jax, jax.numpy as jnp
        import numpy as np
        B, N, D = (16, 128, 256)
        NUM_EXPERTS, TOP_K, HEADS = (4, 2, 4)
        N_EDGES = 32768
        LN_EPS = 1e-05

        def _layernorm(x, g, b):
            mu = x.mean(-1, keepdims=True)
            var = ((x - mu) ** 2).mean(-1, keepdims=True)
            return (x - mu) * jax.lax.rsqrt(var + LN_EPS) * g + b

        def _forward(x, edge_index, W_gat, att_src, att_dst, b_gat, ln_gamma, ln_beta, W1, b1, W2, b2):
            Bc, Nc, Dc = x.shape
            M = Bc * Nc
            x_flat = x.reshape(M, Dc)
            h = (x_flat @ W_gat).reshape(M, HEADS, NUM_EXPERTS)
            loops = jnp.arange(M, dtype=edge_index.dtype)
            src = jnp.concatenate([edge_index[0], loops])
            dst = jnp.concatenate([edge_index[1], loops])
            a_src = (h * att_src).sum(-1)
            a_dst = (h * att_dst).sum(-1)
            e = jax.nn.leaky_relu(a_src[src] + a_dst[dst], negative_slope=0.2)
            e_max = jax.ops.segment_max(e, dst, num_segments=M)
            ee = jnp.exp(e - e_max[dst])
            denom = jax.ops.segment_sum(ee, dst, num_segments=M)
            alpha = ee / (denom[dst] + 1e-16)
            msg = h[src] * alpha[:, :, None]
            agg = jax.ops.segment_sum(msg, dst, num_segments=M).reshape(M, HEADS * NUM_EXPERTS) + b_gat
            scores = _layernorm(agg, ln_gamma, ln_beta).reshape(M, HEADS, NUM_EXPERTS).mean(1)
            scores = scores.reshape(Bc, Nc, NUM_EXPERTS)
            topk_s, topk_i = jax.lax.top_k(scores, TOP_K)
            w = jax.nn.softmax(topk_s, axis=-1)
            out = jnp.zeros_like(x)
            for ei in range(NUM_EXPERTS):
                g = jnp.where(topk_i == ei, w, 0.0).sum(-1)
                hh = jax.nn.gelu(x @ W1[ei] + b1[ei], approximate=False)
                out = out + g[..., None] * (hh @ W2[ei] + b2[ei])
            return out
        key = jax.random.key(seed)
        ks = jax.random.split(key, 8)
        s = 0.05
        return {'x': jax.random.normal(ks[0], (B, N, D), jnp.float32), 'W_gat': jax.random.normal(ks[1], (D, HEADS * NUM_EXPERTS), jnp.float32) * s, 'att_src': jax.random.normal(ks[2], (HEADS, NUM_EXPERTS), jnp.float32) * s, 'att_dst': jax.random.normal(ks[3], (HEADS, NUM_EXPERTS), jnp.float32) * s, 'b_gat': jnp.zeros((HEADS * NUM_EXPERTS,), jnp.float32), 'ln_gamma': jnp.ones((HEADS * NUM_EXPERTS,), jnp.float32), 'ln_beta': jnp.zeros((HEADS * NUM_EXPERTS,), jnp.float32), 'W1': jax.random.normal(ks[4], (NUM_EXPERTS, D, 2 * D), jnp.float32) * s, 'b1': jnp.zeros((NUM_EXPERTS, 2 * D), jnp.float32), 'W2': jax.random.normal(ks[5], (NUM_EXPERTS, 2 * D, D), jnp.float32) * s, 'b2': jnp.zeros((NUM_EXPERTS, D), jnp.float32), 'edge_index': jax.random.randint(ks[6], (2, N_EDGES), 0, B * N, jnp.int32)}
    _L0_ffn_all = _L0_ffn_setup()
    _L0_ffn_in = {k: v for k, v in _L0_ffn_all.items() if k in ('W_gat', 'att_src', 'att_dst', 'b_gat', 'ln_gamma', 'ln_beta', 'W1', 'b1', 'W2', 'b2', 'edge_index')}
    del _L0_ffn_all
    return {'x': x, 'src': src, 'dst': dst, 'L0_gnn_W_P_w': _L0_gnn_in['W_P_w'], 'L0_gnn_W_P_b': _L0_gnn_in['W_P_b'], 'L0_gnn_W_pos': _L0_gnn_in['W_pos'], 'L0_gnn_q1': _L0_gnn_in['q1'], 'L0_gnn_k1': _L0_gnn_in['k1'], 'L0_gnn_v1': _L0_gnn_in['v1'], 'L0_gnn_ln1_s': _L0_gnn_in['ln1_s'], 'L0_gnn_ln1_b': _L0_gnn_in['ln1_b'], 'L0_gnn_q2': _L0_gnn_in['q2'], 'L0_gnn_k2': _L0_gnn_in['k2'], 'L0_gnn_v2': _L0_gnn_in['v2'], 'L0_gnn_ln2_s': _L0_gnn_in['ln2_s'], 'L0_gnn_ln2_b': _L0_gnn_in['ln2_b'], 'L0_gnn_inv_w': _L0_gnn_in['inv_w'], 'L0_gnn_inv_b': _L0_gnn_in['inv_b'], 'L0_ffn_W_gat': _L0_ffn_in['W_gat'], 'L0_ffn_att_src': _L0_ffn_in['att_src'], 'L0_ffn_att_dst': _L0_ffn_in['att_dst'], 'L0_ffn_b_gat': _L0_ffn_in['b_gat'], 'L0_ffn_ln_gamma': _L0_ffn_in['ln_gamma'], 'L0_ffn_ln_beta': _L0_ffn_in['ln_beta'], 'L0_ffn_W1': _L0_ffn_in['W1'], 'L0_ffn_b1': _L0_ffn_in['b1'], 'L0_ffn_W2': _L0_ffn_in['W2'], 'L0_ffn_b2': _L0_ffn_in['b2'], 'L0_ffn_edge_index': _L0_ffn_in['edge_index']}

def reference(x, src, dst, L0_gnn_W_P_w, L0_gnn_W_P_b, L0_gnn_W_pos, L0_gnn_q1, L0_gnn_k1, L0_gnn_v1, L0_gnn_ln1_s, L0_gnn_ln1_b, L0_gnn_q2, L0_gnn_k2, L0_gnn_v2, L0_gnn_ln2_s, L0_gnn_ln2_b, L0_gnn_inv_w, L0_gnn_inv_b, L0_ffn_W_gat, L0_ffn_att_src, L0_ffn_att_dst, L0_ffn_b_gat, L0_ffn_ln_gamma, L0_ffn_ln_beta, L0_ffn_W1, L0_ffn_b1, L0_ffn_W2, L0_ffn_b2, L0_ffn_edge_index):
    import jax
    import jax.numpy as jnp

    def _L0_gnn_ref(x, edge_index, W_P_w, W_P_b, W_pos, q1, k1, v1, ln1_s, ln1_b, q2, k2, v2, ln2_s, ln2_b, inv_w, inv_b):
        import jax, jax.numpy as jnp
        import numpy as np
        HEAD = 8
        D = 128
        GIN = 256
        GOUT = 256
        N = 50000
        E = 25000

        def gt_layer(edge_index, embeds, qT, kT, vT, ln_s, ln_b):
            rows, cols = (edge_index[0], edge_index[1])
            n, d = embeds.shape
            hd = d // HEAD
            rowE = embeds[rows]
            colE = embeds[cols]
            q = (rowE @ qT).reshape(-1, HEAD, hd)
            k = (colE @ kT).reshape(-1, HEAD, hd)
            v = (colE @ vT).reshape(-1, HEAD, hd)
            att = jnp.clip(jnp.einsum('ehd,ehd->eh', q, k), -10.0, 10.0)
            expAtt = jnp.exp(att)
            attNorm = jax.ops.segment_sum(expAtt, rows, num_segments=n)[rows]
            att = expAtt / (attNorm + 1e-08)
            res = (att[..., None] * v).reshape(-1, d)
            agg = jax.ops.segment_sum(res, rows, num_segments=n)
            out = agg + embeds
            mu = jnp.mean(out, axis=-1, keepdims=True)
            var = jnp.mean((out - mu) ** 2, axis=-1, keepdims=True)
            return (out - mu) / jnp.sqrt(var + 1e-06) * ln_s + ln_b
        z = x @ W_P_w + W_P_b
        embeds = z + W_pos
        embeds = gt_layer(edge_index, embeds, q1, k1, v1, ln1_s, ln1_b)
        embeds = gt_layer(edge_index, embeds, q2, k2, v2, ln2_s, ln2_b)
        return embeds @ inv_w + inv_b

    def _L0_ffn_ref(x, W_gat, att_src, att_dst, b_gat, ln_gamma, ln_beta, W1, b1, W2, b2, edge_index):
        import jax, jax.numpy as jnp
        import numpy as np
        B, N, D = (16, 128, 256)
        NUM_EXPERTS, TOP_K, HEADS = (4, 2, 4)
        N_EDGES = 32768
        LN_EPS = 1e-05

        def _layernorm(x, g, b):
            mu = x.mean(-1, keepdims=True)
            var = ((x - mu) ** 2).mean(-1, keepdims=True)
            return (x - mu) * jax.lax.rsqrt(var + LN_EPS) * g + b

        def _forward(x, edge_index, W_gat, att_src, att_dst, b_gat, ln_gamma, ln_beta, W1, b1, W2, b2):
            Bc, Nc, Dc = x.shape
            M = Bc * Nc
            x_flat = x.reshape(M, Dc)
            h = (x_flat @ W_gat).reshape(M, HEADS, NUM_EXPERTS)
            loops = jnp.arange(M, dtype=edge_index.dtype)
            src = jnp.concatenate([edge_index[0], loops])
            dst = jnp.concatenate([edge_index[1], loops])
            a_src = (h * att_src).sum(-1)
            a_dst = (h * att_dst).sum(-1)
            e = jax.nn.leaky_relu(a_src[src] + a_dst[dst], negative_slope=0.2)
            e_max = jax.ops.segment_max(e, dst, num_segments=M)
            ee = jnp.exp(e - e_max[dst])
            denom = jax.ops.segment_sum(ee, dst, num_segments=M)
            alpha = ee / (denom[dst] + 1e-16)
            msg = h[src] * alpha[:, :, None]
            agg = jax.ops.segment_sum(msg, dst, num_segments=M).reshape(M, HEADS * NUM_EXPERTS) + b_gat
            scores = _layernorm(agg, ln_gamma, ln_beta).reshape(M, HEADS, NUM_EXPERTS).mean(1)
            scores = scores.reshape(Bc, Nc, NUM_EXPERTS)
            topk_s, topk_i = jax.lax.top_k(scores, TOP_K)
            w = jax.nn.softmax(topk_s, axis=-1)
            out = jnp.zeros_like(x)
            for ei in range(NUM_EXPERTS):
                g = jnp.where(topk_i == ei, w, 0.0).sum(-1)
                hh = jax.nn.gelu(x @ W1[ei] + b1[ei], approximate=False)
                out = out + g[..., None] * (hh @ W2[ei] + b2[ei])
            return out
        return _forward(x, edge_index, W_gat, att_src, att_dst, b_gat, ln_gamma, ln_beta, W1, b1, W2, b2)
    edge_index = jnp.stack([src, dst])
    x = x + _L0_gnn_ref(_layernorm(x, axis=-1), edge_index, L0_gnn_W_P_w, L0_gnn_W_P_b, L0_gnn_W_pos, L0_gnn_q1, L0_gnn_k1, L0_gnn_v1, L0_gnn_ln1_s, L0_gnn_ln1_b, L0_gnn_q2, L0_gnn_k2, L0_gnn_v2, L0_gnn_ln2_s, L0_gnn_ln2_b, L0_gnn_inv_w, L0_gnn_inv_b)
    x = x + _L0_ffn_ref(_layernorm(x, axis=-1)[None], L0_ffn_W_gat, L0_ffn_att_src, L0_ffn_att_dst, L0_ffn_b_gat, L0_ffn_ln_gamma, L0_ffn_ln_beta, L0_ffn_W1, L0_ffn_b1, L0_ffn_W2, L0_ffn_b2, L0_ffn_edge_index)[0]
    return x

_drawn_inputs = setup_inputs


def setup_inputs(seed=0):
    import zlib

    import numpy as np

    out = dict(_drawn_inputs(seed))
    spreads = {'L0_gnn_W_P_b': (0.0, 0.1),
     'L0_gnn_ln1_s': (1.0, 0.2),
     'L0_gnn_ln1_b': (0.0, 0.1),
     'L0_gnn_ln2_s': (1.0, 0.2),
     'L0_gnn_ln2_b': (0.0, 0.1),
     'L0_gnn_inv_b': (0.0, 0.1),
     'L0_ffn_b_gat': (0.0, 0.1),
     'L0_ffn_ln_gamma': (1.0, 0.2),
     'L0_ffn_ln_beta': (0.0, 0.1),
     'L0_ffn_b1': (0.0, 0.1),
     'L0_ffn_b2': (0.0, 0.1)}
    factors = {'L0_ffn_att_dst': 10.059}
    for name, (base, spread) in spreads.items():
        noise = np.random.default_rng([zlib.crc32(name.encode()), seed]).standard_normal(out[name].shape)
        drawn = base * np.exp(spread * noise) if base else spread * noise
        out[name] = jnp.asarray(drawn.astype(out[name].dtype))
    for name, factor in factors.items():
        out[name] = (out[name] * factor).astype(out[name].dtype)
    return out
```

```python
import concourse.bass as bass
from concourse import mybir
from contextlib import ExitStack



def graph_block_kernel(nc, x, src, dst, W_P_w, W_P_b, W_pos, q1, k1, v1, ln1_s, ln1_b,
                       q2, k2, v2, ln2_s, ln2_b, inv_w, inv_b,
                       W_gat, att_src, att_dst, b_gat, ln_gamma, ln_beta, W1, b1, W2, b2,
                       ffn_edges, out):
    f32, f16, i32 = mybir.dt.float32, mybir.dt.float16, mybir.dt.int32
    ALU = mybir.AluOpType
    ACT = mybir.ActivationFunctionType
    AX = mybir.AxisListType
    ds = bass.ds

    N, DM = x.shape
    NP, NT = 125, 25
    H, HD = 8, 16
    D = H * HD
    DV = D + H
    CH = 5
    NCH = NT // CH
    G = 4
    R1 = 4
    R2 = 10
    RB = 5
    E1, E2 = src.shape[0], ffn_edges.shape[1]
    P1, P2 = 125, 128
    J1, J2 = E1 // P1, E2 // P2
    most = lambda edges, unit: -(-((edges + NT * 127) // 128) // unit) * unit
    T1, T2 = most(E1, G * R1), most(E2, G * R2)
    IT1, IT2 = T1 // (G * R1), T2 // (G * R2)
    U = 4
    NX, HG = 4, 4
    NF = NX * HG
    DG = NF + HG
    FF = W1.shape[2]
    FC = FF // 128
    NQ = NX * FC
    HALF = (CH * NP + 1) // 2
    MID = N // 2
    RND = 12582912.0
    BIG = 1e30
    assert N == NP * NT and J1 % (2 * U) == 0 and J2 % (2 * U) == 0

    node = lambda ap: ap.rearrange("(p t) d -> p t d", t=NT)
    flat = lambda ap: ap.rearrange("p a d -> p (a d)")
    kv_tab = nc.dram_tensor("kv_tab", (N, 2 * D), f32, kind="Internal").ap()
    gate_tab = nc.dram_tensor("gate_tab", (N, DG), f32, kind="Internal").ap()

    ctx = ExitStack()
    with ctx:
        def sb(name, shape, dt=f32):
            return ctx.enter_context(nc.sbuf_tensor(name, shape, dt))

        def sem(name):
            return ctx.enter_context(nc.semaphore(name))

        X = sb("X", [NP, NT, DM])
        AGG = sb("AGG", [NP, NT, DV])
        idx = [sb("idx1", [128, T1 + R1 * G], i32), sb("idx2", [128, T2 + RB * G], i32)]
        loc = [sb("loc1", [128, T1 + G]), sb("loc2", [128, T2 + G])]
        tmap = [sb("tmap1", [1, T1 + 2 * G], i32), sb("tmap2", [1, T2 + 2 * G], i32)]
        ident = sb("ident", [128, 128])
        before = sb("before", [128, 128])
        upto = sb("upto", [128, 128])
        before128 = sb("before128", [128, NT])
        ones = sb("ones", [128, 128])
        zeros16 = sb("zeros16", [128, 128], f16)
        iota_n = sb("iota_n", [128, NP])
        iota_l = sb("iota_l", [128, 128], f16)
        iota_t = sb("iota_t", [128, T1], f16)
        diff_i = sb("diff_i", [128, 128], i32)

        region_a = sb("region_a", [128, NT * J1])
        counts = region_a[:, :]
        w1_sb = region_a[:, 0:2 * NX * FF].rearrange("p (k f) -> p k f", k=2)
        w2_sb = region_a[:, 2 * NX * FF:2 * NX * FF + NQ * DM].rearrange("p (c n) -> p c n", n=DM)
        region_b = sb("region_b", [128, NT * 2 * D])
        hot = region_b[:, 0:NT * J1 // 2].bitcast(f16)
        kv_st = region_b[0:NP, :].rearrange("p (t d) -> p t d", t=NT)
        yT = region_b[:, 0:2 * N].rearrange("p (k n) -> p k n", k=2)
        region_c = sb("region_c", [128, NT * 2 * D])
        Q = region_c[0:NP, 0:NT * D].rearrange("p (t d) -> p t d", t=NT)
        EMB = region_c[0:NP, NT * D:2 * NT * D].rearrange("p (t d) -> p t d", t=NT)
        GAT = region_c[:, 0:T2 * DG].rearrange("p (t d) -> p t d", d=DG)
        hid = region_c[:, 0:2 * FC * CH * NP].rearrange("p (r f n) -> p r f n", r=2, f=FC)
        region_k = sb("region_k", [128, R1 * G * 2 * D])
        kv = region_k[:, :].rearrange("p (r j d) -> p r j d", r=R1, j=G)
        masks = region_k[:, 0:2 * G * HG * NP].rearrange("p (r j h n) -> p r j h n", r=2, j=G, h=HG)

        def parts(region, *sizes):
            at = 0
            for n in sizes:
                yield region[:, at:at + n]
                at += n

        kp, kt, pay, pos, tcol, key1, pay1, key2, pay2, column, past = parts(
            region_c, J1, J1, J1, J1, J1, J1, J1, J2, J2, T1, T1)
        key_i = [key1[0:P1, :].bitcast(i32), key2[0:P2, :].bitcast(i32)]
        pay_i = [pay1[0:P1, :].bitcast(i32), pay2[0:P2, :].bitcast(i32)]
        column_i = column.bitcast(i32)
        past = past[0:NT - 1, :]
        cend = sb("cend", [128, NT + 1])
        cnt = sb("cnt", [128, NT])
        base = sb("base", [128, NT])
        tiles = sb("tiles", [NT, 1])
        tiles_b = sb("tiles_b", [NT, 128])
        ends = sb("ends", [NT, 1])
        hotT, hotL = parts(region_k, U * T1, 2 * U * 128)
        hotT = hotT.bitcast(f16).rearrange("p (r u t) -> p r u t", r=2, u=U)
        hotL = hotL.bitcast(f16).rearrange("p (r u m l) -> p r u m l", r=2, u=U, m=2)

        wP = sb("wP", [128, 2, D])
        wqkv = sb("wqkv", [128, 2, 3 * D])
        winv = sb("winv", [128, DM])
        wgat = sb("wgat", [128, 2, NF])
        bP = sb("bP", [NP, D])
        bPos = sb("bPos", [NP, D])
        ln_s = sb("ln_s", [NP, 2, D])
        ln_b = sb("ln_b", [NP, 2, D])
        binv = sb("binv", [NP, DM])
        gvec = sb("gvec", [NP, 5, NF])
        b1r = sb("b1r", [NQ, 128])
        b1c = sb("b1c", [128, NQ])
        b2b = sb("b2b", [NP, NX, DM])
        st6 = sb("st6", [NP, CH, 6])
        mv = sb("mv", [NP, CH, 2])
        std = sb("std", [NP, CH])
        rden = sb("rden", [NP, CH, H])
        xn = sb("xn", [NP, CH, DM])
        xnT = sb("xnT", [128, CH, 2, NP])
        e5 = sb("e5", [NP, CH, D])
        eT = sb("eT", [128, CH, NP])

        ix = sb("ix", [128, RB, G], i32)
        S = sb("S", [128, 2, G, NP])
        ST = sb("ST", [NP, 2, G, 128])
        prod = sb("prod", [128, G, D])
        logit = sb("logit", [128, G, H])
        att = sb("att", [128, 2, G, H])
        vals = sb("vals", [128, 2, G, DV])

        hn = sb("hn", [NP, NT, DG])
        adm = sb("adm", [NP, NT, 2, HG])
        mx = sb("mx", [NP, NT, HG])
        selfe = sb("selfe", [NP, NT, HG])
        tmx = sb("tmx", [NP, G, HG])
        rows = sb("rows", [128, RB, G, DG])
        msg = sb("msg", [128, 2, G, DG])
        t16, t16b, score, rank, t4, e4, gate, t1, t1b = parts(
            region_k[0:NP, :], NT * NF, NT * NF, NT * NX, NT * NX, NT * NX, NT * NX, NT * NX, NT, NT)
        t16, t16b = (a.rearrange("p (t d) -> p t d", t=NT) for a in (t16, t16b))
        score, rank, t4, e4, gate = (a.rearrange("p (t d) -> p t d", t=NT) for a in (score, rank, t4, e4, gate))

        PS = ctx.enter_context(nc.psum_tensor("PS", [128, 8, 512], f32))
        bank = lambda i: PS[:, i, :]

        s_lists, s_x, s_w, s_w12 = sem("s_lists"), sem("s_x"), sem("s_w"), sem("s_w12")
        s_iota = sem("s_iota")
        s_const = sem("s_const")
        s_phase = sem("s_phase")
        s_b1 = sem("s_b1")
        s_held_dve, s_held_pool = sem("s_held_dve"), sem("s_held_pool")
        s_dve = sem("s_dve")
        D_ = [{k: sem(f"s_{k}{i}") for k in ("cnt", "total", "tiles", "base", "past", "map", "hot", "dealt", "all")}
              for i in range(2)]
        NS = [{k: sem(f"s_{k}{i}") for k in ("var", "std", "norm", "xT", "xTc", "emb", "e5", "eT", "eTc", "proj",
                                             "projc", "kvst", "tab", "keep", "own", "yvar", "ystd", "h", "hc")} for i in range(3)]
        ES = [{k: sem(f"s_e{k}{i}") for k in ("S", "tr", "ST", "q", "clip", "exp", "vals", "agg", "slot", "own", "zero")}
              for i in range(2)]
        s_kv = [[sem(f"s_kv{i}_{r}") for r in range(R1)] for i in range(2)]
        GS = {k: sem(f"s_g{k}") for k in ("mask", "head", "tr", "red", "slot", "own", "S", "tr2", "ST", "look", "e", "exp", "msg",
                                          "agg", "own2", "zero", "tab", "diff", "self", "var", "std", "s", "sexp")}
        s_rows = [sem(f"s_rows{r}") for r in range(RB)]
        MS = {k: sem(f"s_m{k}") for k in ("hid", "gelu", "out", "acc", "own", "fin")}
        s_out = sem("s_out")

        ENGINES = 5
        N_WEIGHTS = 7 + 2 * 5 + 5 + NX

        def meet(eng, n):
            eng.drain()
            eng.sem_inc(s_phase, 1)
            eng.wait_ge(s_phase, ENGINES * n)

        class Count:

            def __init__(self, eng, semaphore, before=0):
                self.eng, self.sem, self.before, self.n = eng, semaphore, before, 0

            def did(self, ins):
                ins.then_inc(self.sem, 1)
                self.n += 1

            def wait(self):
                self.eng.wait_ge(self.sem, self.before + self.n)

        CREDIT = 2
        slot_free = lambda c, k: c * CH + (k + 1 if k >= 2 else 2 - k)

        block = ctx.enter_context(nc.Block())

        @block.sync
        def _(sp):
            for i, (key, other) in enumerate(((src, dst), (ffn_edges[1, :], ffn_edges[0, :]))):
                j = (J1, J2)[i]
                sp.dma_start(key_i[i][:, :], key.rearrange("(p j) -> p j", j=j)).then_inc(s_lists, 16)
                sp.dma_start(pay_i[i][:, :], other.rearrange("(p j) -> p j", j=j)).then_inc(s_lists, 16)
            sp.dma_start(X[:, :, :], node(x)).then_inc(s_x, 16)
            weights = [(wP[:, :, :], W_P_w.rearrange("(k p) n -> p k n", k=2)), (winv[:, :], inv_w),
                       (wgat[:, :, :], W_gat.rearrange("(k p) n -> p k n", k=2)),
                       (bP[:, :], W_P_b[None, :].broadcast_to([NP, D])), (bPos[:, :], W_pos.broadcast_to([NP, D])),
                       (binv[:, :], inv_b[None, :].broadcast_to([NP, DM])),
                       (b1r[:, :], b1.rearrange("e (c p) -> (e c) p", p=128))]
            for l, (q, k, v, s, b) in enumerate(((q1, k1, v1, ln1_s, ln1_b), (q2, k2, v2, ln2_s, ln2_b))):
                weights += [(wqkv[:, l, m * D:(m + 1) * D], w) for m, w in enumerate((q, k, v))]
                weights += [(ln_s[:, l, :], s[None, :].broadcast_to([NP, D])), (ln_b[:, l, :], b[None, :].broadcast_to([NP, D]))]
            weights += [(gvec[:, i, :], v[None, :].broadcast_to([NP, NF])) for i, v in enumerate(
                (att_src.rearrange("h e -> (h e)"), att_dst.rearrange("h e -> (h e)"), b_gat, ln_gamma, ln_beta))]
            weights += [(b2b[:, e, :], b2[e:e + 1, :].broadcast_to([NP, DM])) for e in range(NX)]
            assert len(weights) == N_WEIGHTS
            for to, of in weights:
                sp.dma_start(to, of).then_inc(s_w, 16)
            for l in range(2):
                with sp.Fori(0, NCH) as c:
                    sp.wait_ge(NS[l]["kvst"], c + 1)
                    sp.dma_start(node(kv_tab)[:, ds(c * CH, CH), :], kv_st[:, ds(c * CH, CH), :]).then_inc(NS[l]["tab"], 16)
                sp.wait_ge(NS[l]["tab"], 16 * NCH)
                meet(sp, 1 + 2 * l)
                meet(sp, 2 + 2 * l)
            for e in range(NX):
                for k in range(2):
                    sp.dma_start(w1_sb[:, k, e * FF:(e + 1) * FF], W1[e, k * 128:(k + 1) * 128, :]).then_inc(s_w12, 16)
                sp.dma_start(w2_sb[:, e * FC:(e + 1) * FC, :], W2[e, :, :].rearrange("(c p) n -> p c n", p=128)).then_inc(s_w12, 16)
            sp.wait_ge(GS["diff"], 1)
            sp.dma_start(node(gate_tab), hn[:, :, :]).then_inc(GS["tab"], 16)
            sp.wait_ge(GS["tab"], 16)
            meet(sp, 5)
            meet(sp, 6)
            meet(sp, 7)
            with sp.Fori(0, NCH) as c:
                sp.wait_ge(MS["fin"], c + 1)
                sp.dma_start(node(out)[:, ds(c * CH, CH), :], X[:, ds(c * CH, CH), :]).then_inc(s_out, 16)
            sp.wait_ge(s_out, 16 * NCH)

        @block.gpsimd
        def _(pool):
            nc.gpsimd.iota(column_i[:, :], pattern=[[1, T1]], base=0, channel_multiplier=0).then_inc(s_iota, 1)
            nc.gpsimd.iota(diff_i[:, :], pattern=[[-1, 128]], base=0, channel_multiplier=1).then_inc(s_iota, 1)
            for l in range(2):
                meet(pool, 1 + 2 * l)
                with pool.Fori(0, IT1) as it:
                    for r in range(R1):
                        pool.wait_ge(ES[l]["slot"], it * R1 + r + 1)
                        pool.sem_inc(s_held_pool, 1)
                        for j in range(G):
                            nc.gpsimd.indirect_dma_start(
                                out=kv[:, r, j, :], out_offset=None, in_=kv_tab,
                                in_offset=bass.IndirectOffsetOnAxis(ap=ix[:, r, j:j + 1], axis=0),
                            ).then_inc(s_kv[l][r], 16)
                meet(pool, 2 + 2 * l)
            meet(pool, 5)
            with pool.Fori(0, IT2) as it:
                for k in range(R2):
                    pool.wait_ge(GS["slot"], it * R2 + k + 1)
                    pool.sem_inc(s_held_pool, 1)
                    for j in range(G):
                        nc.gpsimd.indirect_dma_start(
                            out=rows[:, k % RB, j, :], out_offset=None, in_=gate_tab,
                            in_offset=bass.IndirectOffsetOnAxis(ap=ix[:, k % RB, j:j + 1], axis=0),
                        ).then_inc(s_rows[k % RB], 16)
            meet(pool, 6)
            meet(pool, 7)

        @block.scalar
        def _(act):
            def node_stage(l):
                s = NS[l]
                for name in ("xTc", "eTc", "projc")[:3 if l < 2 else 2]:
                    act.sem_inc(s[name], CREDIT)
                if l < 2:
                    act.sem_inc(s["keep"], 1)
                with act.Fori(0, NCH) as c:
                    act.wait_ge(s["var"], c + 1)
                    nc.scalar.activation(std[:, :], mv[:, :, 1], ACT.Sqrt).then_inc(s["std"], 1)
                    if l == 0:
                        for k in range(CH):
                            act.wait_ge(s["xT"], c * CH + k + 1)
                            nc.scalar.copy(xnT[:, k, :, :], bank(k % 2)[:, 0:2 * NP].rearrange("p (a n) -> p a n", a=2)).then_inc(s["xTc"], 1)
                    for k in range(CH):
                        act.wait_ge(s["eT"], c * CH + k + 1)
                        nc.scalar.copy(eT[:, k, :], bank(4 + k % 2)[:, 0:NP]).then_inc(s["eTc"], 1)
                    if l < 2:
                        nc.scalar.copy(EMB[:, ds(c * CH, CH), :], e5[:, :, :]).then_inc(s["keep"], 1)
                        for k in range(CH):
                            act.wait_ge(s["proj"], c * CH + k + 1)
                            nc.scalar.copy(flat(Q[:, ds(c * CH + k, 1), :]), bank(6 + k % 2)[0:NP, 0:D])
                            nc.scalar.copy(flat(kv_st[:, ds(c * CH + k, 1), :]), bank(6 + k % 2)[0:NP, D:3 * D]).then_inc(s["projc"], 1)
                        act.wait_ge(s["projc"], (c + 1) * CH + CREDIT)
                        act.sem_inc(s["kvst"], 1)
                    else:
                        act.wait_ge(s["yvar"], c + 1)
                        nc.scalar.activation(std[:, :], mv[:, :, 1], ACT.Sqrt).then_inc(s["ystd"], 1)
                        for k in range(CH):
                            act.wait_ge(s["xT"], c * CH + k + 1)
                            nc.scalar.copy(xnT[:, k, :, :], bank(k % 2)[:, 0:2 * NP].rearrange("p (a n) -> p a n", a=2)).then_inc(s["xTc"], 1)
                        act.wait_ge(s["xTc"], (c + 1) * CH + CREDIT)
                        nc.scalar.copy(yT[:, :, ds(c * CH * NP, CH * NP)].rearrange("p a (k n) -> p k a n", k=CH), xnT[:, :, :, :]).then_inc(s["keep"], 1)

            for l in range(2):
                node_stage(l)
                meet(act, 1 + 2 * l)
                e = ES[l]

                def keep_transposed(par, n):
                    act.wait_ge(e["tr"], n)
                    nc.scalar.copy(ST[:, par, :, :].rearrange("p j n -> p (j n)"), bank(par)[0:NP, :]).then_inc(e["ST"], 1)

                keep_transposed(0, 1)
                with act.Fori(0, IT1) as it:
                    for r in range(R1):
                        g = it * R1 + r
                        keep_transposed((r + 1) % 2, g + 2)
                        act.wait_ge(e["clip"], g + 1)
                        nc.scalar.activation(vals[:, r % 2, :, D:DV], att[:, r % 2, :, :], ACT.Exp).then_inc(e["exp"], 1)
                meet(act, 2 + 2 * l)
            node_stage(2)
            meet(act, 5)
            act.sem_inc(GS["head"], 1)
            with act.Fori(0, IT2) as it:
                for k in range(R2):
                    g = it * R2 + k
                    act.wait_ge(GS["mask"], g + 1)
                    act.wait_ge(s_rows[k % RB], (it * (R2 // RB) + k // RB + 1) * 16 * G)
                    act.wait_ge(GS["tr"], g + 1)
                    for j in range(G):
                        for h in range(HG):
                            last = nc.scalar.activation(masks[:, k % 2, j, h, :], S[:, k % 2, j, :], ACT.Identity,
                                                        bias=rows[:, k % RB, j, NF + h:NF + h + 1])
                    nc.scalar.copy(GAT[:, ds(g * G, G), :], rows[:, k % RB, :, :]).then_inc(GS["head"], 1)
            meet(act, 6)
            act.wait_ge(GS["diff"], 2)
            nc.scalar.activation(selfe[:, :, :], selfe[:, :, :], ACT.Exp).then_inc(GS["self"], 1)

            def keep_transposed2(par, n):
                act.wait_ge(GS["tr2"], n)
                nc.scalar.copy(ST[:, par, :, :].rearrange("p j n -> p (j n)"), bank(par)[0:NP, :]).then_inc(GS["ST"], 1)

            keep_transposed2(0, 1)
            with act.Fori(0, IT2) as it:
                for k in range(R2):
                    g = it * R2 + k
                    keep_transposed2((k + 1) % 2, g + 2)
                    act.wait_ge(GS["e"], g + 1)
                    nc.scalar.activation(msg[:, k % 2, :, NF:DG], att[:, k % 2, :, 0:HG], ACT.Exp).then_inc(GS["exp"], 1)
            act.wait_ge(GS["var"], 1)
            nc.scalar.activation(t1b[:, :], t1[:, :], ACT.Sqrt).then_inc(GS["std"], 1)
            act.wait_ge(GS["s"], 1)
            nc.scalar.activation(e4[:, :, :], t4[:, :, :], ACT.Exp).then_inc(GS["sexp"], 1)
            meet(act, 7)
            act.sem_inc(MS["gelu"], 2)
            with act.Fori(0, NCH) as c:
                for q in range(NQ):
                    ex, f = q // FC, q % FC
                    act.wait_ge(MS["hid"], c * NQ + q + 1)
                    if f == 0:
                        act.wait_ge(MS["out"], (c * NX + ex + 1) * CH)
                    nc.scalar.activation(hid[:, ex % 2, f, 0:HALF], PS[:, 2 * (q % 2), 0:HALF], ACT.Gelu, bias=b1c[:, q:q + 1])
                    nc.scalar.activation(hid[:, ex % 2, f, HALF:CH * NP], PS[:, 2 * (q % 2) + 1, 0:CH * NP - HALF], ACT.Gelu,
                                         bias=b1c[:, q:q + 1]).then_inc(MS["gelu"], 1)

        @block.tensor
        def _(pe):
            def count_tiles(i):
                P, T, s = (P1, P2)[i], (T1, T2)[i], D_[i]
                pe.wait_ge(s["cnt"], 1)
                nc.tensor.matmul(bank(4)[0:NT, 0:1], cnt[0:P, :], ones[0:P, 0:1], start=True, stop=True).then_inc(s["total"], 1)
                pe.wait_ge(s["tiles"], 1)
                nc.tensor.matmul(bank(5)[0:NT, 0:1], upto[0:NT, 0:NT], tiles[:, :], start=True, stop=True)
                nc.tensor.matmul(bank(6)[0:P, 0:NT], before[0:P, 0:P], cnt[0:P, :], start=True, stop=False)
                nc.tensor.matmul(bank(6)[0:P, 0:NT], tiles_b[:, 0:P], before128[0:NT, :], start=False, stop=True).then_inc(s["base"], 1)
                pe.wait_ge(s["past"], 1)
                nc.tensor.matmul(bank(7)[0:1, 0:T], ones[0:NT - 1, 0:1], past[:, 0:T], start=True, stop=True).then_inc(s["map"], 1)

            def deal(i):
                P, J, T, s = (P1, P2)[i], (J1, J2)[i], (T1, T2)[i], D_[i]
                acc = [bank(2 * i)[:, 0:T], bank(2 * i + 1)[:, 0:T]]
                pe.sem_inc(s["dealt"], 2)
                for a in acc:
                    nc.tensor.matmul(a, zeros16[:, :], iota_t[:, 0:T], start=True, stop=False)
                with pe.Fori(0, J // (2 * U)) as it:
                    for par in range(2):
                        pe.wait_ge(s["hot"], it * 2 + par + 1)
                        for u in range(U):
                            for m in range(2):
                                last = nc.tensor.matmul(acc[m], hotL[0:P, par, u, m, :], hotT[0:P, par, u, 0:T], start=False, stop=False)
                        last.then_inc(s["dealt"], 1)
                for a in acc:
                    last = nc.tensor.matmul(a, zeros16[:, :], iota_t[:, 0:T], start=False, stop=True)
                last.then_inc(s["all"], 1)

            def transposed_x(l, c, k):
                s = NS[l]
                pe.wait_ge(s["norm"], c * CH + k + 1)
                pe.wait_ge(s["xTc"], slot_free(c, k))
                for a in range(2):
                    last = nc.tensor.transpose(bank(k % 2)[:, a * NP:(a + 1) * NP], xn[:, k, a * 128:(a + 1) * 128], ident[0:NP, 0:NP])
                last.then_inc(s["xT"], 1)

            def node_stage(l):
                s = NS[l]
                with pe.Fori(0, NCH) as c:
                    if l == 0:
                        for k in range(CH):
                            transposed_x(l, c, k)
                        for k in range(CH):
                            pe.wait_ge(s["xTc"], c * CH + k + 1 + CREDIT)
                            pe.wait_ge(s["e5"], slot_free(c, k))
                            for a in range(2):
                                last = nc.tensor.matmul(bank(2 + k % 2)[0:NP, 0:D], xnT[:, k, a, :], wP[:, a, :], start=(a == 0), stop=(a == 1))
                            last.then_inc(s["emb"], 1)
                    for k in range(CH):
                        pe.wait_ge(s["e5"], c * CH + k + 1 + CREDIT)
                        pe.wait_ge(s["eTc"], slot_free(c, k))
                        nc.tensor.transpose(bank(4 + k % 2)[:, 0:NP], e5[:, k, :], ident[0:NP, 0:NP]).then_inc(s["eT"], 1)
                    for k in range(CH):
                        pe.wait_ge(s["eTc"], c * CH + k + 1 + CREDIT)
                        pe.wait_ge(s["projc"], slot_free(c, k))
                        w = wqkv[:, l, :] if l < 2 else winv[:, :]
                        nc.tensor.matmul(bank(6 + k % 2)[0:NP, 0:w.shape[1]], eT[:, k, :], w, start=True, stop=True).then_inc(s["proj"], 1)
                    if l == 2:
                        for k in range(CH):
                            transposed_x(l, c, k)
                        for k in range(CH):
                            pe.wait_ge(s["xTc"], c * CH + k + 1 + CREDIT)
                            pe.wait_ge(s["hc"], slot_free(c, k))
                            for a in range(2):
                                last = nc.tensor.matmul(bank(2 + k % 2)[0:NP, 0:NF], xnT[:, k, a, :], wgat[:, a, :], start=(a == 0), stop=(a == 1))
                            last.then_inc(s["h"], 1)

            pe.wait_ge(s_const, 1)
            for i in range(2):
                count_tiles(i)
                deal(i)
            pe.wait_ge(s_w, 16 * N_WEIGHTS)
            nc.tensor.transpose(bank(7)[:, 0:NQ], b1r[:, :], ident[0:NQ, 0:NQ]).then_inc(s_b1, 1)
            for l in range(2):
                node_stage(l)
                meet(pe, 1 + 2 * l)
                e = ES[l]

                def fetch_q(par, group, n_S, n_ST, wait_slot=True):
                    pe.wait_ge(e["S"], n_S)
                    for j in range(G):
                        last = nc.tensor.transpose(bank(par)[0:NP, j * 128:(j + 1) * 128], S[:, par, j, :], ident[:, :])
                    last.then_inc(e["tr"], 1)
                    _, at = nc.values_load_multi_w_load_instructions(
                        tmap[0][0:1, ds(group * G + G, G)], engines=[nc.tensor.engine], min_val=0, max_val=NT - 1,
                        skip_runtime_bounds_check_because="it counts up to 24 comparisons")
                    pe.wait_ge(e["ST"], n_ST)
                    for j in range(G):
                        last = nc.tensor.matmul(bank(2 + par)[:, j * 128:(j + 1) * 128], ST[:, par, j, :], flat(Q[:, ds(at[j], 1), :]), start=True, stop=True)
                    last.then_inc(e["q"], 1)

                pe.sem_inc(e["agg"], 1)
                pe.wait_ge(e["zero"], 1)
                fetch_q(0, 0, 1, 1)
                with pe.Fori(0, IT1) as it:
                    for r in range(R1):
                        g = it * R1 + r
                        fetch_q((r + 1) % 2, g + 1, g + 2, g + 2)
                        pe.wait_ge(e["vals"], g + 1)
                        for j in range(G):
                            b = bank(4 + 2 * (r % 2) + j // 2)
                            last = nc.tensor.matmul(b[0:NP, (j % 2) * DV:(j % 2 + 1) * DV], S[:, r % 2, j, :], vals[:, r % 2, j, :], start=True, stop=True)
                        last.then_inc(e["agg"], 1)
                meet(pe, 2 + 2 * l)
            node_stage(2)
            meet(pe, 5)
            pe.sem_inc(GS["tr"], 2)
            with pe.Fori(0, IT2) as it:
                for k in range(R2):
                    g = it * R2 + k
                    pe.wait_ge(GS["head"], g + 2)
                    pe.wait_ge(GS["red"], g + 1)
                    for j in range(G):
                        for h in range(HG):
                            last = nc.tensor.transpose(bank(4 * (k % 2) + j)[0:NP, h * 128:(h + 1) * 128], masks[:, k % 2, j, h, :], ident[:, :])
                    last.then_inc(GS["tr"], 1)
            meet(pe, 6)

            def look_up(par, group, n):
                pe.wait_ge(GS["S"], n)
                for j in range(G):
                    last = nc.tensor.transpose(bank(par)[0:NP, j * 128:(j + 1) * 128], S[:, par, j, :], ident[:, :])
                last.then_inc(GS["tr2"], 1)
                _, at = nc.values_load_multi_w_load_instructions(
                    tmap[1][0:1, ds(group * G + G, G)], engines=[nc.tensor.engine], min_val=0, max_val=NT - 1,
                    skip_runtime_bounds_check_because="it counts up to 24 comparisons")
                pe.wait_ge(GS["ST"], n)
                for j in range(G):
                    last = nc.tensor.matmul(bank(2 + par)[:, j * 2 * HG:(j + 1) * 2 * HG], ST[:, par, j, :],
                                            adm[:, ds(at[j], 1), :, :].rearrange("p a b h -> p (a b h)"), start=True, stop=True)
                last.then_inc(GS["look"], 1)

            pe.sem_inc(GS["agg"], 1)
            pe.wait_ge(GS["zero"], 1)
            look_up(0, 0, 1)
            with pe.Fori(0, IT2) as it:
                for k in range(R2):
                    g = it * R2 + k
                    look_up((k + 1) % 2, g + 1, g + 2)
                    pe.wait_ge(GS["msg"], g + 1)
                    for j in range(G):
                        last = nc.tensor.matmul(bank(4 + k % 2)[0:NP, j * DG:(j + 1) * DG], S[:, k % 2, j, :], msg[:, k % 2, j, :], start=True, stop=True)
                    last.then_inc(GS["agg"], 1)
            meet(pe, 7)
            pe.wait_ge(s_w12, 16 * 3 * NX)
            pe.sem_inc(MS["out"], 2 * CH)
            with pe.Fori(0, NCH) as c:
                def hidden(ex):
                    for f in range(FC):
                        q = ex * FC + f
                        pe.wait_ge(MS["gelu"], c * NQ + q + 1)
                        for h, (at, n) in enumerate(((0, HALF), (HALF, CH * NP - HALF))):
                            for a in range(2):
                                last = nc.tensor.matmul(PS[:, 2 * (q % 2) + h, 0:n], w1_sb[:, a, q * 128:(q + 1) * 128],
                                                        yT[:, a, ds(c * CH * NP + at, n)], start=(a == 0), stop=(a == 1))
                        last.then_inc(MS["hid"], 1)

                def back(ex):
                    pe.wait_ge(MS["gelu"], c * NQ + (ex + 1) * FC + 2)
                    for k in range(CH):
                        pe.wait_ge(MS["acc"], (c * NX + ex) * CH + k + 1)
                        for f in range(FC):
                            last = nc.tensor.matmul(bank(4 + (ex * CH + k) % 4)[0:NP, 0:DM], hid[:, ex % 2, f, k * NP:(k + 1) * NP],
                                                    w2_sb[:, ex * FC + f, :], start=(f == 0), stop=(f == FC - 1))
                        last.then_inc(MS["out"], 1)

                hidden(0)
                for ex in range(NX):
                    if ex + 1 < NX:
                        hidden(ex + 1)
                    back(ex)

        @block.vector
        def _(dve):
            v = nc.vector
            own = Count(dve, s_dve)

            dve.wait_ge(s_iota, 2)
            v.tensor_copy(iota_t[:, :], column_i[:, :])
            v.tensor_copy(iota_l[:, :], column_i[:, 0:128])
            v.tensor_copy(iota_n[:, :], column_i[:, 0:NP])
            v.tensor_scalar(before[:, :], diff_i[:, :], 0.0, None, ALU.is_lt)
            v.tensor_scalar(before128[:, :], diff_i[:, 0:NT], 0.0, 128.0, ALU.is_lt, ALU.mult)
            v.tensor_scalar(upto[:, :], diff_i[:, :], 0.0, None, ALU.is_le)
            v.tensor_scalar(ident[:, :], diff_i[:, :], 0.0, None, ALU.is_equal)
            v.memset(zeros16[:, :], 0.0)
            v.memset(cend[:, 0:1], 0.0)
            for i, T in enumerate((T1, T2)):
                v.memset(tmap[i][:, :], 0)
                v.memset(idx[i][:, T:], 0)
                v.memset(loc[i][:, T:], -1.0)
            v.memset(ones[:, :], 1.0).then_inc(s_const, 1)
            dve.wait_ge(s_const, 1)

            def rint(ap):
                own.wait()
                own.did(v.tensor_scalar(ap, ap, RND, RND, ALU.add, ALU.subtract))
                own.wait()

            dve.wait_ge(s_lists, 64)
            for i in range(2):
                P, J, T, s = (P1, P2)[i], (J1, J2)[i], (T1, T2)[i], D_[i]
                key, p_, t_, y_, c_, z_ = (a[0:P, 0:J] for a in (pos, kp, kt, pay, tcol, counts))
                hot_p = hot[0:P, 0:NT * J]
                cnt_p = counts[0:P, 0:NT * J]
                by_tile = lambda a: a.rearrange("p (b j) -> p b j", b=NT)
                own.did(v.tensor_copy(key, key_i[i][:, :]))
                own.wait()
                own.did(v.tensor_scalar(p_, key, -float(NT // 2), 1.0 / NT, ALU.add, ALU.mult))
                rint(p_)
                own.did(v.scalar_tensor_tensor(t_, p_, -float(NT), key, ALU.mult, ALU.add))
                own.wait()
                own.did(v.tensor_tensor(by_tile(hot_p), t_[:, None, :].broadcast_to([P, NT, J]),
                                        iota_n[0:P, 0:NT][:, :, None].broadcast_to([P, NT, J]), ALU.is_equal))
                own.wait()
                own.did(v.tensor_tensor_scan(cnt_p, hot_p, hot_p, 0.0, ALU.add, ALU.max))
                own.wait()
                own.did(v.tensor_copy(cend[0:P, 1:NT + 1], by_tile(cnt_p)[:, :, J - 1]))
                own.wait()
                v.tensor_tensor(cnt[0:P, :], cend[0:P, 1:NT + 1], cend[0:P, 0:NT], ALU.subtract).then_inc(s["cnt"], 1)
                dve.wait_ge(s["total"], 1)
                own.did(v.tensor_scalar(tiles[:, :], bank(4)[0:NT, 0:1], 63.5, 1.0 / 128, ALU.add, ALU.mult))
                rint(tiles[:, :])
                v.tensor_scalar(tiles_b[:, :], ones[0:NT, :], tiles[:, 0:1], None, ALU.mult).then_inc(s["tiles"], 1)
                dve.wait_ge(s["base"], 1)
                own.did(v.tensor_copy(ends[:, :], bank(5)[0:NT, 0:1]))
                own.did(v.scalar_tensor_tensor(base[0:P, :], bank(6)[0:P, 0:NT], -1.0, cend[0:P, 0:NT], ALU.add, ALU.subtract))
                own.wait()
                v.tensor_scalar(past[:, 0:T], iota_t[0:NT - 1, 0:T], ends[0:NT - 1, 0:1], None, ALU.is_ge).then_inc(s["past"], 1)
                own.did(v.tensor_tensor(by_tile(cnt_p), by_tile(cnt_p), base[0:P, :][:, :, None].broadcast_to([P, NT, J]), ALU.add))
                own.wait()
                own.did(v.tensor_tensor(cnt_p, cnt_p, hot_p, ALU.mult))
                own.wait()
                own.did(v.tensor_reduce(key, cnt_p.rearrange("p (b j) -> p j b", b=NT), AX.X, ALU.add))
                own.wait()
                own.did(v.tensor_scalar(c_, key, -63.5, 1.0 / 128, ALU.add, ALU.mult))
                rint(c_)
                own.did(v.scalar_tensor_tensor(key, c_, -128.0, key, ALU.mult, ALU.add))
                own.did(v.tensor_scalar(y_, pay_i[i][:, :], -float(MID), None, ALU.add))
                own.did(v.tensor_scalar(p_, p_, 1.0, None, ALU.add))
                dve.wait_ge(s["map"], 1)
                own.did(v.tensor_copy(tmap[i][0:1, G:G + T], bank(7)[0:1, 0:T]))
                own.wait()
                with dve.Fori(0, J // (2 * U)) as it:
                    for par in range(2):
                        dve.wait_ge(s["dealt"], it * 2 + par + 1)
                        for u in range(U):
                            j = (it * 2 + par) * U + u
                            v.tensor_scalar(hotT[0:P, par, u, 0:T], iota_t[0:P, 0:T], tcol[0:P, ds(j, 1)], None, ALU.is_equal)
                            v.tensor_scalar(hotL[0:P, par, u, 0, :], iota_l[0:P, :], pos[0:P, ds(j, 1)], pay[0:P, ds(j, 1)], ALU.is_equal, ALU.mult)
                            last = v.tensor_scalar(hotL[0:P, par, u, 1, :], iota_l[0:P, :], pos[0:P, ds(j, 1)], kp[0:P, ds(j, 1)], ALU.is_equal, ALU.mult)
                        last.then_inc(s["hot"], 1)
                dve.wait_ge(s["all"], 1)
                own.did(v.tensor_scalar(idx[i][:, 0:T], bank(2 * i)[:, 0:T], float(MID), None, ALU.add))
                own.did(v.tensor_scalar(loc[i][:, 0:T], bank(2 * i + 1)[:, 0:T], -1.0, None, ALU.add))
            own.wait()

            def layer_norm(o, s, var, std_done, source, width, eps, to, norm=None):
                if o.n:
                    o.wait()
                dve.sem_inc(s_held_dve, 1)
                for k in range(CH):
                    o.did(v.bn_stats(st6[:, k, :], source(k)))
                o.wait()
                dve.sem_inc(s_held_dve, 1)
                for k in range(CH):
                    o.did(v.bn_aggr(mv[:, k, :], st6[:, k, :]))
                o.wait()
                v.tensor_scalar(mv[:, :, 1], mv[:, :, 1], eps, None, ALU.add).then_inc(s[var], 1)
                dve.wait_ge(s[std_done], o.round + 1)
                o.did(v.reciprocal(std[:, :], std[:, :]))
                o.wait()
                for k in range(CH):
                    last = v.tensor_scalar(to(k), source(k), mv[:, k, 0:1], std[:, k:k + 1], ALU.subtract, ALU.mult)
                    if norm:
                        last.then_inc(s[norm], 1)
                    else:
                        o.did(last)

            OWN = [11, 4 + 16 + 1, 4 + 16 + 1 + 1 + 11]

            def node_stage(l):
                s = NS[l]
                dve.sem_inc(s["e5"], CREDIT)
                if l == 2:
                    dve.sem_inc(s["projc"], CREDIT)
                    dve.sem_inc(s["hc"], CREDIT)
                with dve.Fori(0, NCH) as c:
                    o = Count(dve, s["own"], c * OWN[l])
                    o.round = c
                    if l == 0:
                        layer_norm(o, s, "var", "std", lambda k: flat(X[:, ds(c * CH + k, 1), :]), DM, 1e-5, lambda k: xn[:, k, :], "norm")
                        dve.wait_ge(s["keep"], c + 1)
                        for k in range(CH):
                            dve.wait_ge(s["emb"], c * CH + k + 1)
                            v.tensor_tensor(e5[:, k, :], bank(2 + k % 2)[0:NP, 0:D], bP[:, :], ALU.add).then_inc(s["e5"], 1)
                    else:
                        sums = AGG[:, ds(c * CH, CH), 0:D].rearrange("p t (h d) -> p t h d", h=H)
                        e5h = e5[:, :, :].rearrange("p t (h d) -> p t h d", h=H)
                        o.did(v.tensor_scalar(rden[:, :, :], AGG[:, ds(c * CH, CH), D:DV], 1e-8, None, ALU.add))
                        o.wait()
                        o.did(v.reciprocal(rden[:, :, :], rden[:, :, :]))
                        o.wait()
                        if l == 1:
                            dve.wait_ge(s["keep"], c + 1)
                        o.did(v.tensor_tensor(e5h, sums, rden[:, :, :][:, :, :, None].broadcast_to([NP, CH, H, HD]), ALU.mult))
                        o.wait()
                        o.did(v.tensor_tensor(e5[:, :, :], e5[:, :, :], EMB[:, ds(c * CH, CH), :], ALU.add))
                        layer_norm(o, s, "var", "std", lambda k: e5[:, k, :], D, 1e-6, lambda k: e5[:, k, :])
                        o.wait()
                        o.did(v.tensor_tensor(e5[:, :, :], e5[:, :, :], ln_s[:, l - 1, :][:, None, :].broadcast_to([NP, CH, D]), ALU.mult))
                        o.wait()
                        v.tensor_tensor(e5[:, :, :], e5[:, :, :], ln_b[:, l - 1, :][:, None, :].broadcast_to([NP, CH, D]), ALU.add).then_inc(s["e5"], CH)
                    if l == 2:
                        for k in range(CH):
                            xk = flat(X[:, ds(c * CH + k, 1), :])
                            dve.wait_ge(s["proj"], c * CH + k + 1)
                            v.tensor_tensor(xk, bank(6 + k % 2)[0:NP, 0:DM], xk, ALU.add).then_inc(s["projc"], 1)
                        dve.wait_ge(s["projc"], (c + 1) * CH + CREDIT)
                        xc = X[:, ds(c * CH, CH), :]
                        o.did(v.tensor_tensor(xc, xc, binv[:, :][:, None, :].broadcast_to([NP, CH, DM]), ALU.add))
                        layer_norm(o, s, "yvar", "ystd", lambda k: flat(X[:, ds(c * CH + k, 1), :]), DM, 1e-5, lambda k: xn[:, k, :], "norm")
                        for k in range(CH):
                            dve.wait_ge(s["h"], c * CH + k + 1)
                            v.tensor_copy(flat(hn[:, ds(c * CH + k, 1), 0:NF]), bank(2 + k % 2)[0:NP, 0:NF]).then_inc(s["hc"], 1)
                    assert o.n == OWN[l], (l, o.n)

            dve.wait_ge(s_x, 16)
            dve.wait_ge(s_w, 16 * N_WEIGHTS)
            own.did(v.tensor_tensor(bP[:, :], bP[:, :], bPos[:, :], ALU.add))
            dve.wait_ge(s_b1, 1)
            own.did(v.tensor_copy(b1c[:, :], bank(7)[:, 0:NQ]))
            own.wait()
            for l in range(2):
                node_stage(l)
                e = ES[l]

                def build_S(par, group):
                    v.tensor_tensor(S[:, par, :, :], iota_n[:, :][:, None, :].broadcast_to([128, G, NP]),
                                    loc[0][:, ds(group * G, G)][:, :, None].broadcast_to([128, G, NP]), ALU.is_equal).then_inc(e["S"], 1)

                def stage_indices(r, group):
                    v.tensor_copy(ix[:, r, :], idx[0][:, ds(group * G, G)]).then_inc(e["slot"], 1)

                def add_sums(o, par, group):
                    _, at = nc.values_load_multi_w_load_instructions(
                        tmap[0][0:1, ds(group * G + G, G)], engines=[v.engine], min_val=0, max_val=NT - 1,
                        skip_runtime_bounds_check_because="it counts up to 24 comparisons")
                    for j in range(G):
                        a = flat(AGG[:, ds(at[j], 1), :])
                        o.did(v.tensor_tensor(a, bank(4 + 2 * par + j // 2)[0:NP, (j % 2) * DV:(j % 2 + 1) * DV], a, ALU.add))
                        o.wait()

                meet(dve, 1 + 2 * l)
                v.memset(PS[0:NP, 6:8, 0:2 * DV], 0.0)
                v.memset(AGG[:, :, :], 0.0).then_inc(e["zero"], 1)
                for r in range(R1):
                    stage_indices(r, r)
                build_S(0, 0)
                PER = 2 + G
                with dve.Fori(0, IT1) as it:
                    for r in range(R1):
                        g, par = it * R1 + r, r % 2
                        o = Count(dve, e["own"], g * PER)
                        dve.wait_ge(e["agg"], g + 1)
                        build_S(1 - par, g + 1)
                        dve.wait_ge(e["q"], g + 1)
                        dve.wait_ge(s_kv[l][r], (it + 1) * 16 * G)
                        o.did(v.tensor_tensor(prod[:, :, :], bank(2 + par).rearrange("p (j d) -> p j d", j=G), kv[:, r, :, 0:D], ALU.mult))
                        o.wait()
                        o.did(v.tensor_reduce(logit[:, :, :], prod[:, :, :].rearrange("p j (h d) -> p j h d", h=H), AX.X, ALU.add))
                        o.wait()
                        v.tensor_scalar(att[:, par, :, :], logit[:, :, :], 10.0, -10.0, ALU.min, ALU.max).then_inc(e["clip"], 1)
                        if r == 0:
                            dve.wait_ge(e["zero"], 1)
                        add_sums(o, 1 - par, g - 1)
                        dve.wait_ge(e["exp"], g + 1)
                        v.tensor_tensor(vals[:, par, :, 0:D].rearrange("p j (h d) -> p j h d", h=H),
                                        kv[:, r, :, D:2 * D].rearrange("p j (h d) -> p j h d", h=H),
                                        vals[:, par, :, D:DV][:, :, :, None].broadcast_to([128, G, H, HD]), ALU.mult).then_inc(e["vals"], 1)
                        stage_indices(r, g + R1)
                        assert o.n == PER
                dve.wait_ge(e["agg"], T1 // G + 1)
                add_sums(Count(dve, e["own"], T1 // G * PER), (T1 // G - 1) % 2, T1 // G - 1)
                meet(dve, 2 + 2 * l)

            node_stage(2)
            h_ = hn[:, :, 0:NF]
            a_src, a_dst, top = hn[:, :, NF:DG], adm[:, :, 0, :], adm[:, :, 1, :]
            over = lambda a, n=NF: a[:, None, :].broadcast_to([NP, NT, n])
            by_head = lambda a: a.rearrange("p t (h e) -> p t h e", h=HG)
            dve.wait_ge(NS[2]["hc"], NT + CREDIT)
            own.did(v.tensor_tensor(t16[:, :, :], h_, over(gvec[:, 0, :]), ALU.mult))
            own.did(v.tensor_tensor(t16b[:, :, :], h_, over(gvec[:, 1, :]), ALU.mult))
            own.wait()
            own.did(v.tensor_reduce(a_dst, by_head(t16b[:, :, :]), AX.X, ALU.add))
            v.tensor_reduce(a_src, by_head(t16[:, :, :]), AX.X, ALU.add).then_inc(GS["diff"], 1)
            dve.wait_ge(GS["diff"], 1)
            own.did(v.tensor_copy(mx[:, :, :], a_src))
            own.wait()
            meet(dve, 5)

            def mask_group(par, group):
                for j in range(G):
                    last = v.tensor_scalar(S[:, par, j, :], iota_n[:, :], loc[1][:, ds(group * G + j, 1)], -BIG, ALU.not_equal, ALU.mult)
                last.then_inc(GS["mask"], 1)

            def stage_rows(k, group):
                v.tensor_copy(ix[:, k, :], idx[1][:, ds(group * G, G)]).then_inc(GS["slot"], 1)

            dve.sem_inc(GS["red"], 2)
            for k in range(RB):
                stage_rows(k, k)
            mask_group(0, 0)
            with dve.Fori(0, IT2) as it:
                for k in range(R2):
                    g, par = it * R2 + k, k % 2
                    o = Count(dve, GS["own"], g * G)
                    dve.wait_ge(GS["head"], g + 1)
                    mask_group(1 - par, g + 1)
                    dve.wait_ge(GS["tr"], g + 3)
                    v.tensor_reduce(tmx[:, :, :].rearrange("p j h -> p (j h)"),
                                    PS[0:NP, 4 * par:4 * par + G, :].rearrange("p j (h n) -> p (j h) n", h=HG), AX.X, ALU.max).then_inc(GS["red"], 1)
                    _, at = nc.values_load_multi_w_load_instructions(
                        tmap[1][0:1, ds(g * G + G, G)], engines=[v.engine], min_val=0, max_val=NT - 1,
                        skip_runtime_bounds_check_because="it counts up to 24 comparisons")
                    dve.wait_ge(GS["red"], g + 3)
                    for j in range(G):
                        m = flat(mx[:, ds(at[j], 1), :])
                        o.did(v.tensor_tensor(m, tmx[:, j, :], m, ALU.max))
                        o.wait()
                    stage_rows(k % RB, g + RB)
            def leaky_sum(to, a):
                own.did(v.tensor_tensor(t4[:, :, :], a, a_dst, ALU.add))
                own.wait()
                own.did(v.scalar_tensor_tensor(to, t4[:, :, :], 0.2, t4[:, :, :], ALU.mult, ALU.max))
                own.wait()

            leaky_sum(top, mx[:, :, :])
            leaky_sum(selfe[:, :, :], a_src)
            v.tensor_tensor(selfe[:, :, :], selfe[:, :, :], top, ALU.subtract).then_inc(GS["diff"], 1)
            meet(dve, 6)

            GAG = AGG[:, :, 0:DG]
            dve.wait_ge(GS["self"], 1)
            own.did(v.tensor_tensor(by_head(GAG[:, :, 0:NF]), by_head(h_), selfe[:, :, :][:, :, :, None].broadcast_to([NP, NT, HG, NX]), ALU.mult))
            own.did(v.tensor_copy(GAG[:, :, NF:DG], selfe[:, :, :]))
            v.memset(PS[0:NP, 5, 0:G * DG], 0.0).then_inc(GS["zero"], 1)
            own.wait()

            def gate_S(par, group):
                v.tensor_tensor(S[:, par, :, :], iota_n[:, :][:, None, :].broadcast_to([128, G, NP]),
                                loc[1][:, ds(group * G, G)][:, :, None].broadcast_to([128, G, NP]), ALU.is_equal).then_inc(GS["S"], 1)

            def gate_sums(o, par, group):
                _, at = nc.values_load_multi_w_load_instructions(
                    tmap[1][0:1, ds(group * G + G, G)], engines=[v.engine], min_val=0, max_val=NT - 1,
                    skip_runtime_bounds_check_because="it counts up to 24 comparisons")
                for j in range(G):
                    a = flat(AGG[:, ds(at[j], 1), 0:DG])
                    o.did(v.tensor_tensor(a, bank(4 + par)[0:NP, j * DG:(j + 1) * DG], a, ALU.add))
                    o.wait()

            gate_S(0, 0)
            PER2 = 3 + G
            with dve.Fori(0, IT2) as it:
                for k in range(R2):
                    g, par = it * R2 + k, k % 2
                    o = Count(dve, GS["own2"], g * PER2)
                    got = bank(2 + par)[:, 0:G * 2 * HG].rearrange("p (j a h) -> p j a h", j=G, a=2)
                    dve.wait_ge(GS["agg"], g + 1)
                    gate_S(1 - par, g + 1)
                    dve.wait_ge(GS["look"], g + 1)
                    o.did(v.tensor_tensor(logit[:, :, 0:HG], GAT[:, ds(g * G, G), NF:DG], got[:, :, 0, :], ALU.add))
                    o.wait()
                    o.did(v.scalar_tensor_tensor(logit[:, :, HG:H], logit[:, :, 0:HG], 0.2, logit[:, :, 0:HG], ALU.mult, ALU.max))
                    o.wait()
                    o.did(v.tensor_tensor(logit[:, :, 0:HG], logit[:, :, HG:H], got[:, :, 1, :], ALU.subtract))
                    o.wait()
                    v.tensor_scalar(att[:, par, :, 0:HG], logit[:, :, 0:HG], 0.0, None, ALU.min).then_inc(GS["e"], 1)
                    gate_sums(o, 1 - par, g - 1)
                    dve.wait_ge(GS["exp"], g + 1)
                    v.tensor_tensor(msg[:, par, :, 0:NF].rearrange("p j (h e) -> p j h e", h=HG),
                                    GAT[:, ds(g * G, G), 0:NF].rearrange("p j (h e) -> p j h e", h=HG),
                                    msg[:, par, :, NF:DG][:, :, :, None].broadcast_to([128, G, HG, NX]), ALU.mult).then_inc(GS["msg"], 1)
                    assert o.n == PER2
            dve.wait_ge(GS["agg"], T2 // G + 1)
            gate_sums(Count(dve, GS["own2"], T2 // G * PER2), (T2 // G - 1) % 2, T2 // G - 1)

            t, tb = t16[:, :, :], t16b[:, :, :]
            wide = lambda a, n=NF: a[:, :, None].broadcast_to([NP, NT, n])
            own.did(v.tensor_scalar(t4[:, :, :], GAG[:, :, NF:DG], 1e-16, None, ALU.add))
            own.wait()
            own.did(v.reciprocal(t4[:, :, :], t4[:, :, :]))
            own.wait()
            own.did(v.tensor_tensor(by_head(t), by_head(GAG[:, :, 0:NF]), t4[:, :, :][:, :, :, None].broadcast_to([NP, NT, HG, NX]), ALU.mult))
            own.wait()
            own.did(v.tensor_tensor(t, t, over(gvec[:, 2, :]), ALU.add))
            own.wait()
            own.did(v.tensor_reduce(t1[:, :], t, AX.X, ALU.add))
            own.wait()
            own.did(v.tensor_scalar(t1[:, :], t1[:, :], 1.0 / NF, None, ALU.mult))
            own.wait()
            own.did(v.tensor_tensor(t, t, wide(t1[:, :]), ALU.subtract))
            own.wait()
            own.did(v.tensor_tensor(tb, t, t, ALU.mult))
            own.wait()
            own.did(v.tensor_reduce(t1[:, :], tb, AX.X, ALU.add))
            own.wait()
            v.tensor_scalar(t1[:, :], t1[:, :], 1.0 / NF, 1e-5, ALU.mult, ALU.add).then_inc(GS["var"], 1)
            dve.wait_ge(GS["std"], 1)
            own.did(v.reciprocal(t1b[:, :], t1b[:, :]))
            own.wait()
            own.did(v.tensor_tensor(t, t, wide(t1b[:, :]), ALU.mult))
            own.wait()
            own.did(v.tensor_tensor(t, t, over(gvec[:, 3, :]), ALU.mult))
            own.wait()
            own.did(v.tensor_tensor(t, t, over(gvec[:, 4, :]), ALU.add))
            own.wait()
            own.did(v.tensor_reduce(score[:, :, :], t.rearrange("p t (h e) -> p t e h", h=HG), AX.X, ALU.add))
            own.wait()
            own.did(v.tensor_scalar(score[:, :, :], score[:, :, :], 1.0 / HG, None, ALU.mult))
            own.did(v.memset(rank[:, :, :], 0.0))
            own.wait()
            own.did(v.tensor_reduce(t1[:, :], score[:, :, :], AX.X, ALU.max))
            for j in range(NX):
                sj = score[:, :, j]
                own.did(v.tensor_tensor(gate[:, :, :], wide(sj, NX), score[:, :, :], ALU.is_gt))
                own.wait()
                own.did(v.tensor_tensor(rank[:, :, :], rank[:, :, :], gate[:, :, :], ALU.add))
                own.wait()
                if j + 1 < NX:
                    own.did(v.tensor_tensor(gate[:, :, j + 1:], wide(sj, NX - 1 - j), score[:, :, j + 1:], ALU.is_equal))
                    own.wait()
                    own.did(v.tensor_tensor(rank[:, :, j + 1:], rank[:, :, j + 1:], gate[:, :, j + 1:], ALU.add))
                    own.wait()
            v.tensor_tensor(t4[:, :, :], score[:, :, :], wide(t1[:, :], NX), ALU.subtract).then_inc(GS["s"], 1)
            dve.wait_ge(GS["sexp"], 1)
            own.did(v.scalar_tensor_tensor(gate[:, :, :], rank[:, :, :], 1.5, e4[:, :, :], ALU.is_lt, ALU.mult))
            own.wait()
            own.did(v.tensor_reduce(t1[:, :], gate[:, :, :], AX.X, ALU.add))
            own.wait()
            own.did(v.reciprocal(t1[:, :], t1[:, :]))
            own.wait()
            own.did(v.tensor_tensor(gate[:, :, :], gate[:, :, :], wide(t1[:, :], NX), ALU.mult))
            own.wait()
            meet(dve, 7)

            dve.sem_inc(MS["acc"], 4)
            with dve.Fori(0, NCH) as c:
                o = Count(dve, MS["own"], c * NX * CH)
                for ex in range(NX):
                    for k in range(CH):
                        xk = flat(X[:, ds(c * CH + k, 1), :])
                        o.did(v.scalar_tensor_tensor(xk, b2b[:, ex, :], flat(gate[:, ds(c * CH + k, 1), ex:ex + 1]), xk, ALU.mult, ALU.add))
                    o.wait()
                for ex in range(NX):
                    for k in range(CH):
                        xk = flat(X[:, ds(c * CH + k, 1), :])
                        dve.wait_ge(MS["out"], (c * NX + ex) * CH + k + 1 + 2 * CH)
                        v.scalar_tensor_tensor(xk, bank(4 + (ex * CH + k) % 4)[0:NP, 0:DM],
                                               flat(gate[:, ds(c * CH + k, 1), ex:ex + 1]), xk, ALU.mult, ALU.add).then_inc(MS["acc"], 1)
                    dve.wait_ge(MS["acc"], (c * NX + ex + 1) * CH + 4)
                dve.sem_inc(MS["fin"], 1)


_INS = ['x', 'src', 'dst', 'L0_gnn_W_P_w', 'L0_gnn_W_P_b', 'L0_gnn_W_pos', 'L0_gnn_q1', 'L0_gnn_k1', 'L0_gnn_v1',
        'L0_gnn_ln1_s', 'L0_gnn_ln1_b', 'L0_gnn_q2', 'L0_gnn_k2', 'L0_gnn_v2', 'L0_gnn_ln2_s', 'L0_gnn_ln2_b',
        'L0_gnn_inv_w', 'L0_gnn_inv_b', 'L0_ffn_W_gat', 'L0_ffn_att_src', 'L0_ffn_att_dst', 'L0_ffn_b_gat',
        'L0_ffn_ln_gamma', 'L0_ffn_ln_beta', 'L0_ffn_W1', 'L0_ffn_b1', 'L0_ffn_W2', 'L0_ffn_b2', 'L0_ffn_edge_index']


def kernel(**inputs):
    import numpy as np
    import concourse.bacc as bacc
    from concourse.bass_utils import run_bass_kernel_spmd

    nc = bacc.Bacc("TRN2", target_bir_lowering=False, num_devices=1)
    arrays, args = {}, []
    for name in _INS:
        a = np.ascontiguousarray(inputs[name])
        arrays[f"in_{name}"] = a
        args.append(nc.dram_tensor(f"in_{name}", a.shape, mybir.dt.from_np(a.dtype), kind="ExternalInput").ap())
    out = nc.dram_tensor("out", inputs["x"].shape, mybir.dt.float32, kind="ExternalOutput").ap()
    graph_block_kernel(nc, *args, out)
    r = run_bass_kernel_spmd(nc, [arrays], core_ids=[0])
    return r.results[0]["out"]
```

```python
import concourse.bass as bass
from concourse import mybir
from contextlib import ExitStack



def graph_block_kernel(nc, x, src, dst, W_P_w, W_P_b, W_pos, q1, k1, v1, ln1_s, ln1_b,
                       q2, k2, v2, ln2_s, ln2_b, inv_w, inv_b,
                       W_gat, att_src, att_dst, b_gat, ln_gamma, ln_beta, W1, b1, W2, b2,
                       ffn_edges, out):
    f32, f16, bf16, i32 = mybir.dt.float32, mybir.dt.float16, mybir.dt.bfloat16, mybir.dt.int32
    ALU = mybir.AluOpType
    ACT = mybir.ActivationFunctionType
    AX = mybir.AxisListType
    ds = bass.ds

    N, DM = x.shape
    NP, NT = 125, 25
    H, HD = 8, 16
    D = H * HD
    DV = D + H
    CH = 5
    NCH = NT // CH
    G = 4
    GP = G // 2
    R1, RB1 = 10, 5
    R2, RB = 4, 4
    PAIR = 256
    E1, E2 = src.shape[0], ffn_edges.shape[1]
    P1, P2 = 125, 128
    J1, J2 = E1 // P1, E2 // P2
    most = lambda edges, unit: -(-2 * ((edges + NT * (PAIR - 1)) // PAIR) // unit) * unit
    T1, T2 = most(E1, G * R1), most(E2, G * R2)
    IT1, IT2 = T1 // (G * R1), T2 // (G * R2)
    U = 4
    NX, HG = 4, 4
    NF = NX * HG
    DG = NF + HG
    FF = W1.shape[2]
    FC = FF // 128
    NQ = NX * FC
    HALF = (CH * NP + 1) // 2
    MID = N // 2
    RND = 12582912.0
    BIG = 1e30
    assert N == NP * NT and J1 % (2 * U) == 0 and J2 % (2 * U) == 0

    node = lambda ap: ap.rearrange("(p t) d -> p t d", t=NT)
    flat = lambda ap: ap.rearrange("p a d -> p (a d)")
    kv_tab = nc.dram_tensor("kv_tab", (N, 2 * D), f32, kind="Internal").ap()
    gate_tab = nc.dram_tensor("gate_tab", (N, DG), f32, kind="Internal").ap()

    ctx = ExitStack()
    with ctx:
        def sb(name, shape, dt=f32):
            return ctx.enter_context(nc.sbuf_tensor(name, shape, dt))

        def sem(name):
            return ctx.enter_context(nc.semaphore(name))

        X = sb("X", [NP, NT, DM])
        AGG = sb("AGG", [NP, NT, DV])
        idx = [sb("idx1", [128, T1 + RB1 * G], i32), sb("idx2", [128, T2 + RB * G], i32)]
        loc = [sb("loc1", [128, T1 + 2 * G]), sb("loc2", [128, T2 + 2 * G])]
        tmap = [sb("tmap1", [1, T1 // 2 + GP], i32), sb("tmap2", [1, T2 // 2 + GP], i32)]
        ident = sb("ident", [128, 128])
        ident16 = sb("ident16", [128, 128], bf16)
        before = sb("before", [128, 128])
        upto = sb("upto", [128, 128])
        before256 = sb("before256", [128, NT])
        ones = sb("ones", [128, 128])
        zeros16 = sb("zeros16", [128, 128], f16)
        iota_n = sb("iota_n", [128, NP])
        iota_l = sb("iota_l", [128, 128], f16)
        iota_t = sb("iota_t", [128, T1], f16)
        diff_i = sb("diff_i", [128, 128], i32)

        region_a = sb("region_a", [128, NT * J1])
        counts = region_a[:, :]
        w1_sb = region_a[:, 0:2 * NX * FF].rearrange("p (k f) -> p k f", k=2)
        w2_sb = region_a[:, 2 * NX * FF:2 * NX * FF + NQ * DM].rearrange("p (c n) -> p c n", n=DM)
        region_b = sb("region_b", [128, NT * 2 * D])
        hot = region_b[:, 0:NT * J1 // 2].bitcast(f16)
        kv_st = region_b[0:NP, :].rearrange("p (t d) -> p t d", t=NT)
        yT = region_b[:, 0:2 * N].rearrange("p (k n) -> p k n", k=2)
        region_c = sb("region_c", [128, NT * 2 * D])
        Q = region_c[0:NP, 0:NT * D].rearrange("p (t d) -> p t d", t=NT)
        EMB = region_c[0:NP, NT * D:2 * NT * D].rearrange("p (t d) -> p t d", t=NT)
        GAT = region_c[:, 0:T2 * DG].rearrange("p (t d) -> p t d", d=DG)
        hid = region_c[:, 0:2 * FC * CH * NP].rearrange("p (r f n) -> p r f n", r=2, f=FC)
        region_k = sb("region_k", [128, RB1 * G * 2 * D])
        kv = region_k[:, :].rearrange("p (r j d) -> p r j d", r=RB1, j=G)
        masks = region_k[:, 0:2 * G * HG * NP].rearrange("p (r j h n) -> p r j h n", r=2, j=G, h=HG)

        def parts(region, *sizes):
            at = 0
            for n in sizes:
                yield region[:, at:at + n]
                at += n

        kp, kt, pay, pos, tcol, key1, pay1, key2, pay2, column, past = parts(
            region_c, J1, J1, J1, J1, J1, J1, J1, J2, J2, T1, T1)
        key_i = [key1[0:P1, :].bitcast(i32), key2[0:P2, :].bitcast(i32)]
        pay_i = [pay1[0:P1, :].bitcast(i32), pay2[0:P2, :].bitcast(i32)]
        column_i = column.bitcast(i32)
        past = past[0:NT - 1, :]
        cend = sb("cend", [128, NT + 1])
        cnt = sb("cnt", [128, NT])
        base = sb("base", [128, NT])
        tiles = sb("tiles", [NT, 1])
        tiles_b = sb("tiles_b", [NT, 128])
        ends = sb("ends", [NT, 1])
        hotT, hotL = parts(region_k, U * T1, 2 * U * 128)
        hotT = hotT.bitcast(f16).rearrange("p (r u t) -> p r u t", r=2, u=U)
        hotL = hotL.bitcast(f16).rearrange("p (r u m l) -> p r u m l", r=2, u=U, m=2)

        wP = sb("wP", [128, 2, D])
        wqkv = sb("wqkv", [128, 2, 3 * D])
        winv = sb("winv", [128, DM])
        wgat = sb("wgat", [128, 2, NF])
        bP = sb("bP", [NP, D])
        bPos = sb("bPos", [NP, D])
        ln_s = sb("ln_s", [NP, 2, D])
        ln_b = sb("ln_b", [NP, 2, D])
        binv = sb("binv", [NP, DM])
        gvec = sb("gvec", [NP, 5, NF])
        b1r = sb("b1r", [NQ, 128])
        b1c = sb("b1c", [128, NQ])
        b2b = sb("b2b", [NP, NX, DM])
        st6 = sb("st6", [NP, CH, 6])
        mv = sb("mv", [NP, CH, 2])
        std = sb("std", [NP, CH])
        rden = sb("rden", [NP, CH, H])
        behind = 2 * NX * FF + NQ * DM
        xn = region_a[0:NP, behind:behind + CH * DM].rearrange("p (k d) -> p k d", k=CH)
        region_s = sb("region_s", [128, 2 * CH * NP + CH * D + CH * NP])
        xnT, e5, eT = parts(region_s, 2 * CH * NP, CH * D, CH * NP)
        xnT = xnT.rearrange("p (k a n) -> p k a n", k=CH, a=2)
        e5 = e5[0:NP, :].rearrange("p (k d) -> p k d", k=CH)
        eT = eT.rearrange("p (k n) -> p k n", k=CH)

        ix = sb("ix", [128, max(RB1, RB), G], i32)
        RS = max(RB1, RB)
        S = region_s[:, 0:RS * G * NP].rearrange("p (r j n) -> p r j n", r=RS, j=G)
        ST = sb("ST", [NP, 2, G, 128])
        prod = region_a[:, behind + CH * DM:behind + CH * DM + G * D].rearrange("p (j d) -> p j d", j=G)
        logit = sb("logit", [128, G, H])
        att = sb("att", [128, 2, G, H])
        vals = sb("vals", [128, 2, G, DV])

        hn = sb("hn", [NP, NT, DG])
        adm = sb("adm", [NP, NT, 2, HG])
        mx = sb("mx", [NP, NT, HG])
        selfe = sb("selfe", [NP, NT, HG])
        tmx = sb("tmx", [NP, GP, HG])
        rows = sb("rows", [128, RB, G, DG])
        msg = sb("msg", [128, 2, G, DG])
        t16, t16b, score, rank, t4, e4, gate, t1, t1b = parts(
            region_k[0:NP, :], NT * NF, NT * NF, NT * NX, NT * NX, NT * NX, NT * NX, NT * NX, NT, NT)
        t16, t16b = (a.rearrange("p (t d) -> p t d", t=NT) for a in (t16, t16b))
        score, rank, t4, e4, gate = (a.rearrange("p (t d) -> p t d", t=NT) for a in (score, rank, t4, e4, gate))

        PS = ctx.enter_context(nc.psum_tensor("PS", [128, 8, 512], f32))
        bank = lambda i: PS[:, i, :]
        bank16 = lambda i: PS[:, i, :].bitcast(bf16)
        S16 = S[:, :, :, :].bitcast(bf16).rearrange("p r j (n two) -> p r j n two", two=2)[:, :, :, :, 1]

        s_lists, s_x, s_w, s_w12 = sem("s_lists"), sem("s_x"), sem("s_w"), sem("s_w12")
        s_iota = sem("s_iota")
        s_const = sem("s_const")
        s_phase = sem("s_phase")
        s_b1 = sem("s_b1")
        s_held_dve, s_held_pool = sem("s_held_dve"), sem("s_held_pool")
        s_dve = sem("s_dve")
        D_ = [{k: sem(f"s_{k}{i}") for k in ("cnt", "total", "tiles", "base", "past", "map", "hot", "dealt", "all")}
              for i in range(2)]
        NS = [{k: sem(f"s_{k}{i}") for k in ("var", "std", "norm", "xT", "xTc", "emb", "e5", "eT", "eTc", "proj",
                                             "projc", "kvst", "tab", "keep", "own", "yvar", "ystd", "h", "hc")} for i in range(3)]
        ES = [{k: sem(f"s_e{k}{i}") for k in ("S", "tr", "ST", "q", "clip", "exp", "vals", "agg", "sum", "slot", "own", "zero")}
              for i in range(2)]
        s_kv = [[sem(f"s_kv{i}_{r}") for r in range(RB1)] for i in range(2)]
        GS = {k: sem(f"s_g{k}") for k in ("mask", "head", "tr", "red", "slot", "own", "S", "tr2", "ST", "look", "e", "exp", "msg",
                                          "agg", "sum", "own2", "zero", "tab", "diff", "self", "var", "std", "s", "sexp")}
        s_rows = [sem(f"s_rows{r}") for r in range(RB)]
        MS = {k: sem(f"s_m{k}") for k in ("hid", "gelu", "out", "acc", "own", "fin")}
        s_out = sem("s_out")

        ENGINES = 5
        N_WEIGHTS = 7 + 2 * 5 + 5 + NX

        def meet(eng, n):
            eng.drain()
            eng.sem_inc(s_phase, 1)
            eng.wait_ge(s_phase, ENGINES * n)

        class Count:

            def __init__(self, eng, semaphore, before=0):
                self.eng, self.sem, self.before, self.n = eng, semaphore, before, 0

            def did(self, ins):
                ins.then_inc(self.sem, 1)
                self.n += 1

            def wait(self):
                self.eng.wait_ge(self.sem, self.before + self.n)

        CREDIT = 2
        slot_free = lambda c, k: c * CH + (k + 1 if k >= 2 else 2 - k)

        block = ctx.enter_context(nc.Block())

        @block.sync
        def _(sp):
            for i, (key, other) in enumerate(((src, dst), (ffn_edges[1, :], ffn_edges[0, :]))):
                j = (J1, J2)[i]
                sp.dma_start(key_i[i][:, :], key.rearrange("(p j) -> p j", j=j)).then_inc(s_lists, 16)
                sp.dma_start(pay_i[i][:, :], other.rearrange("(p j) -> p j", j=j)).then_inc(s_lists, 16)
            sp.dma_start(X[:, :, :], node(x)).then_inc(s_x, 16)
            weights = [(wP[:, :, :], W_P_w.rearrange("(k p) n -> p k n", k=2)), (winv[:, :], inv_w),
                       (wgat[:, :, :], W_gat.rearrange("(k p) n -> p k n", k=2)),
                       (bP[:, :], W_P_b[None, :].broadcast_to([NP, D])), (bPos[:, :], W_pos.broadcast_to([NP, D])),
                       (binv[:, :], inv_b[None, :].broadcast_to([NP, DM])),
                       (b1r[:, :], b1.rearrange("e (c p) -> (e c) p", p=128))]
            for l, (q, k, v, s, b) in enumerate(((q1, k1, v1, ln1_s, ln1_b), (q2, k2, v2, ln2_s, ln2_b))):
                weights += [(wqkv[:, l, m * D:(m + 1) * D], w) for m, w in enumerate((q, k, v))]
                weights += [(ln_s[:, l, :], s[None, :].broadcast_to([NP, D])), (ln_b[:, l, :], b[None, :].broadcast_to([NP, D]))]
            weights += [(gvec[:, i, :], v[None, :].broadcast_to([NP, NF])) for i, v in enumerate(
                (att_src.rearrange("h e -> (h e)"), att_dst.rearrange("h e -> (h e)"), b_gat, ln_gamma, ln_beta))]
            weights += [(b2b[:, e, :], b2[e:e + 1, :].broadcast_to([NP, DM])) for e in range(NX)]
            assert len(weights) == N_WEIGHTS
            for to, of in weights:
                sp.dma_start(to, of).then_inc(s_w, 16)
            for l in range(2):
                with sp.Fori(0, NCH) as c:
                    sp.wait_ge(NS[l]["kvst"], c + 1)
                    sp.dma_start(node(kv_tab)[:, ds(c * CH, CH), :], kv_st[:, ds(c * CH, CH), :]).then_inc(NS[l]["tab"], 16)
                sp.wait_ge(NS[l]["tab"], 16 * NCH)
                meet(sp, 1 + 2 * l)
                meet(sp, 2 + 2 * l)
            for e in range(NX):
                for k in range(2):
                    sp.dma_start(w1_sb[:, k, e * FF:(e + 1) * FF], W1[e, k * 128:(k + 1) * 128, :]).then_inc(s_w12, 16)
                sp.dma_start(w2_sb[:, e * FC:(e + 1) * FC, :], W2[e, :, :].rearrange("(c p) n -> p c n", p=128)).then_inc(s_w12, 16)
            sp.wait_ge(GS["diff"], 1)
            sp.dma_start(node(gate_tab), hn[:, :, :]).then_inc(GS["tab"], 16)
            sp.wait_ge(GS["tab"], 16)
            meet(sp, 5)
            meet(sp, 6)
            meet(sp, 7)
            with sp.Fori(0, NCH) as c:
                sp.wait_ge(MS["fin"], c + 1)
                sp.dma_start(node(out)[:, ds(c * CH, CH), :], X[:, ds(c * CH, CH), :]).then_inc(s_out, 16)
            sp.wait_ge(s_out, 16 * NCH)

        @block.gpsimd
        def _(pool):
            nc.gpsimd.iota(column_i[:, :], pattern=[[1, T1]], base=0, channel_multiplier=0).then_inc(s_iota, 1)
            nc.gpsimd.iota(diff_i[:, :], pattern=[[-1, 128]], base=0, channel_multiplier=1).then_inc(s_iota, 1)
            for l in range(2):
                meet(pool, 1 + 2 * l)
                with pool.Fori(0, IT1) as it:
                    for r in range(R1):
                        pool.wait_ge(ES[l]["slot"], it * R1 + r + 1)
                        pool.sem_inc(s_held_pool, 1)
                        for j in range(G):
                            nc.gpsimd.indirect_dma_start(
                                out=kv[:, r % RB1, j, :], out_offset=None, in_=kv_tab,
                                in_offset=bass.IndirectOffsetOnAxis(ap=ix[:, r % RB1, j:j + 1], axis=0),
                            ).then_inc(s_kv[l][r % RB1], 16)
                meet(pool, 2 + 2 * l)
            meet(pool, 5)
            with pool.Fori(0, IT2) as it:
                for k in range(R2):
                    pool.wait_ge(GS["slot"], it * R2 + k + 1)
                    pool.sem_inc(s_held_pool, 1)
                    for j in range(G):
                        nc.gpsimd.indirect_dma_start(
                            out=rows[:, k % RB, j, :], out_offset=None, in_=gate_tab,
                            in_offset=bass.IndirectOffsetOnAxis(ap=ix[:, k % RB, j:j + 1], axis=0),
                        ).then_inc(s_rows[k % RB], 16)
            meet(pool, 6)
            meet(pool, 7)

        @block.scalar
        def _(act):
            def keep_sums(act, tmap_, g, e, sums, first_bank, width):
                _, at = nc.values_load_multi_w_load_instructions(
                    tmap_[0:1, ds(g * GP, GP)], engines=[nc.scalar.engine], min_val=0, max_val=NT - 1,
                    skip_runtime_bounds_check_because="it counts up to 24 comparisons")
                for u in range(GP):
                    act.wait_ge(e["agg"], g * GP + u + 1 + 2 * GP)
                    nc.scalar.copy(flat(sums[:, ds(at[u], 1), :]), bank(first_bank + u)[0:NP, 0:width]).then_inc(e["sum"], 1)

            def node_stage(l):
                s = NS[l]
                for name in ("xTc", "eTc", "projc")[:3 if l < 2 else 2]:
                    act.sem_inc(s[name], CREDIT)
                if l < 2:
                    act.sem_inc(s["keep"], 1)
                with act.Fori(0, NCH) as c:
                    act.wait_ge(s["var"], c + 1)
                    nc.scalar.activation(std[:, :], mv[:, :, 1], ACT.Sqrt).then_inc(s["std"], 1)
                    if l == 0:
                        for k in range(CH):
                            act.wait_ge(s["xT"], c * CH + k + 1)
                            nc.scalar.copy(xnT[:, k, :, :], bank(k % 2)[:, 0:2 * NP].rearrange("p (a n) -> p a n", a=2)).then_inc(s["xTc"], 1)
                    for k in range(CH):
                        act.wait_ge(s["eT"], c * CH + k + 1)
                        nc.scalar.copy(eT[:, k, :], bank(4 + k % 2)[:, 0:NP]).then_inc(s["eTc"], 1)
                    if l < 2:
                        nc.scalar.copy(EMB[:, ds(c * CH, CH), :], e5[:, :, :]).then_inc(s["keep"], 1)
                        for k in range(CH):
                            act.wait_ge(s["proj"], c * CH + k + 1)
                            nc.scalar.copy(flat(Q[:, ds(c * CH + k, 1), :]), bank(6 + k % 2)[0:NP, 0:D])
                            nc.scalar.copy(flat(kv_st[:, ds(c * CH + k, 1), :]), bank(6 + k % 2)[0:NP, D:3 * D]).then_inc(s["projc"], 1)
                        act.wait_ge(s["projc"], (c + 1) * CH + CREDIT)
                        act.sem_inc(s["kvst"], 1)
                    else:
                        act.wait_ge(s["yvar"], c + 1)
                        nc.scalar.activation(std[:, :], mv[:, :, 1], ACT.Sqrt).then_inc(s["ystd"], 1)
                        for k in range(CH):
                            act.wait_ge(s["xT"], c * CH + k + 1)
                            nc.scalar.copy(xnT[:, k, :, :], bank(k % 2)[:, 0:2 * NP].rearrange("p (a n) -> p a n", a=2)).then_inc(s["xTc"], 1)
                        act.wait_ge(s["xTc"], (c + 1) * CH + CREDIT)
                        nc.scalar.copy(yT[:, :, ds(c * CH * NP, CH * NP)].rearrange("p a (k n) -> p k a n", k=CH), xnT[:, :, :, :]).then_inc(s["keep"], 1)

            for l in range(2):
                node_stage(l)
                meet(act, 1 + 2 * l)
                e = ES[l]

                def keep_transposed(par, n):
                    act.wait_ge(e["tr"], n)
                    nc.scalar.copy(ST[:, par, :, :].rearrange("p j n -> p (j n)"), bank16(par)[0:NP, 0:G * 128]).then_inc(e["ST"], 1)

                act.sem_inc(e["sum"], 1)
                keep_transposed(0, 1)
                keep_transposed(1, 2)
                with act.Fori(0, IT1) as it:
                    for r in range(R1):
                        g = it * R1 + r
                        act.wait_ge(e["clip"], g + 1)
                        nc.scalar.activation(vals[:, r % 2, :, D:DV], att[:, r % 2, :, :], ACT.Exp).then_inc(e["exp"], 1)
                        keep_transposed(r % 2, g + 3)
                        keep_sums(act, tmap[0], g, e, AGG, 4, DV)
                meet(act, 2 + 2 * l)
            node_stage(2)
            meet(act, 5)
            act.sem_inc(GS["head"], 1)
            with act.Fori(0, IT2) as it:
                for k in range(R2):
                    g = it * R2 + k
                    act.wait_ge(GS["mask"], g + 1)
                    act.wait_ge(s_rows[k % RB], (it * (R2 // RB) + k // RB + 1) * 16 * G)
                    act.wait_ge(GS["tr"], g + 1)
                    for j in range(G):
                        for h in range(HG):
                            last = nc.scalar.activation(masks[:, k % 2, j, h, :], S[:, k % 2, j, :], ACT.Identity,
                                                        bias=rows[:, k % RB, j, NF + h:NF + h + 1])
                    nc.scalar.copy(GAT[:, ds(g * G, G), :], rows[:, k % RB, :, :]).then_inc(GS["head"], 1)
            meet(act, 6)
            act.wait_ge(GS["diff"], 2)
            nc.scalar.activation(selfe[:, :, :], selfe[:, :, :], ACT.Exp).then_inc(GS["self"], 1)

            def keep_transposed2(par, n):
                act.wait_ge(GS["tr2"], n)
                nc.scalar.copy(ST[:, par, :, :].rearrange("p j n -> p (j n)"), bank16(par)[0:NP, 0:G * 128]).then_inc(GS["ST"], 1)

            act.sem_inc(GS["sum"], 1)
            keep_transposed2(0, 1)
            keep_transposed2(1, 2)
            with act.Fori(0, IT2) as it:
                for k in range(R2):
                    g = it * R2 + k
                    act.wait_ge(GS["e"], g + 1)
                    nc.scalar.activation(msg[:, k % 2, :, NF:DG], att[:, k % 2, :, 0:HG], ACT.Exp).then_inc(GS["exp"], 1)
                    keep_transposed2(k % 2, g + 3)
                    keep_sums(act, tmap[1], g, GS, AGG[:, :, 0:DG], 4, DG)
            act.wait_ge(GS["var"], 1)
            nc.scalar.activation(t1b[:, :], t1[:, :], ACT.Sqrt).then_inc(GS["std"], 1)
            act.wait_ge(GS["s"], 1)
            nc.scalar.activation(e4[:, :, :], t4[:, :, :], ACT.Exp).then_inc(GS["sexp"], 1)
            meet(act, 7)
            act.sem_inc(MS["gelu"], 2)
            with act.Fori(0, NCH) as c:
                for q in range(NQ):
                    ex, f = q // FC, q % FC
                    act.wait_ge(MS["hid"], c * NQ + q + 1)
                    if f == 0:
                        act.wait_ge(MS["out"], (c * NX + ex + 1) * CH)
                    nc.scalar.activation(hid[:, ex % 2, f, 0:HALF], PS[:, 2 * (q % 2), 0:HALF], ACT.Gelu, bias=b1c[:, q:q + 1])
                    nc.scalar.activation(hid[:, ex % 2, f, HALF:CH * NP], PS[:, 2 * (q % 2) + 1, 0:CH * NP - HALF], ACT.Gelu,
                                         bias=b1c[:, q:q + 1]).then_inc(MS["gelu"], 1)

        @block.tensor
        def _(pe):
            def count_tiles(i):
                P, T, s = (P1, P2)[i], (T1, T2)[i], D_[i]
                pe.wait_ge(s["cnt"], 1)
                nc.tensor.matmul(bank(4)[0:NT, 0:1], cnt[0:P, :], ones[0:P, 0:1], start=True, stop=True).then_inc(s["total"], 1)
                pe.wait_ge(s["tiles"], 1)
                nc.tensor.matmul(bank(5)[0:NT, 0:1], upto[0:NT, 0:NT], tiles[:, :], start=True, stop=True)
                nc.tensor.matmul(bank(6)[0:P, 0:NT], before[0:P, 0:P], cnt[0:P, :], start=True, stop=False)
                nc.tensor.matmul(bank(6)[0:P, 0:NT], tiles_b[:, 0:P], before256[0:NT, :], start=False, stop=True).then_inc(s["base"], 1)
                pe.wait_ge(s["past"], 1)
                nc.tensor.matmul(bank(7)[0:1, 0:T // 2], ones[0:NT - 1, 0:1], past[:, 0:T // 2], start=True, stop=True).then_inc(s["map"], 1)

            def deal(i):
                P, J, T, s = (P1, P2)[i], (J1, J2)[i], (T1, T2)[i], D_[i]
                acc = [bank(2 * i)[:, 0:T], bank(2 * i + 1)[:, 0:T]]
                pe.sem_inc(s["dealt"], 2)
                for a in acc:
                    nc.tensor.matmul(a, zeros16[:, :], iota_t[:, 0:T], start=True, stop=False)
                with pe.Fori(0, J // (2 * U)) as it:
                    for par in range(2):
                        pe.wait_ge(s["hot"], it * 2 + par + 1)
                        for u in range(U):
                            for m in range(2):
                                last = nc.tensor.matmul(acc[m], hotL[0:P, par, u, m, :], hotT[0:P, par, u, 0:T], start=False, stop=False)
                        last.then_inc(s["dealt"], 1)
                for a in acc:
                    last = nc.tensor.matmul(a, zeros16[:, :], iota_t[:, 0:T], start=False, stop=True)
                last.then_inc(s["all"], 1)

            def transposed_x(l, c, k):
                s = NS[l]
                pe.wait_ge(s["norm"], c * CH + k + 1)
                pe.wait_ge(s["xTc"], slot_free(c, k))
                for a in range(2):
                    last = nc.tensor.transpose(bank(k % 2)[:, a * NP:(a + 1) * NP], xn[:, k, a * 128:(a + 1) * 128], ident[0:NP, 0:NP])
                last.then_inc(s["xT"], 1)

            def node_stage(l):
                s = NS[l]
                with pe.Fori(0, NCH) as c:
                    if l == 0:
                        for k in range(CH):
                            transposed_x(l, c, k)
                        for k in range(CH):
                            pe.wait_ge(s["xTc"], c * CH + k + 1 + CREDIT)
                            pe.wait_ge(s["e5"], slot_free(c, k))
                            for a in range(2):
                                last = nc.tensor.matmul(bank(2 + k % 2)[0:NP, 0:D], xnT[:, k, a, :], wP[:, a, :], start=(a == 0), stop=(a == 1))
                            last.then_inc(s["emb"], 1)
                    for k in range(CH):
                        pe.wait_ge(s["e5"], c * CH + k + 1 + CREDIT)
                        pe.wait_ge(s["eTc"], slot_free(c, k))
                        nc.tensor.transpose(bank(4 + k % 2)[:, 0:NP], e5[:, k, :], ident[0:NP, 0:NP]).then_inc(s["eT"], 1)
                    for k in range(CH):
                        pe.wait_ge(s["eTc"], c * CH + k + 1 + CREDIT)
                        pe.wait_ge(s["projc"], slot_free(c, k))
                        w = wqkv[:, l, :] if l < 2 else winv[:, :]
                        nc.tensor.matmul(bank(6 + k % 2)[0:NP, 0:w.shape[1]], eT[:, k, :], w, start=True, stop=True).then_inc(s["proj"], 1)
                    if l == 2:
                        for k in range(CH):
                            transposed_x(l, c, k)
                        for k in range(CH):
                            pe.wait_ge(s["xTc"], c * CH + k + 1 + CREDIT)
                            pe.wait_ge(s["hc"], slot_free(c, k))
                            for a in range(2):
                                last = nc.tensor.matmul(bank(2 + k % 2)[0:NP, 0:NF], xnT[:, k, a, :], wgat[:, a, :], start=(a == 0), stop=(a == 1))
                            last.then_inc(s["h"], 1)

            def node_tiles(tmap_, first, n):
                return nc.values_load_multi_w_load_instructions(
                    tmap_[0:1, ds(first, n)], engines=[nc.tensor.engine], min_val=0, max_val=NT - 1,
                    skip_runtime_bounds_check_because="it counts up to 24 comparisons")[1]

            def transposed_S(ready, done, slot, par, n):
                pe.wait_ge(ready, n)
                for j in range(G):
                    last = nc.tensor.transpose(bank16(par)[0:NP, j * 128:(j + 1) * 128], S16[:, slot, j, :], ident16[:, :])
                last.then_inc(done, 1)

            def add_up(e, ready, g, at, slot, par, values, sums, width):
                pe.wait_ge(ready, g + 1)
                for u in range(GP):
                    b = bank(4 + u)[0:NP, 0:width]
                    for j in (2 * u, 2 * u + 1):
                        nc.tensor.matmul(b, S[:, slot, j, :], values[:, par, j, :], start=(j == 2 * u), stop=False)
                    pe.wait_ge(e["sum"], g * GP + u + 1)
                    nc.tensor.matmul(b, ident[0:NP, 0:NP], flat(sums[:, ds(at[u], 1), :]), start=False, stop=True).then_inc(e["agg"], 1)

            pe.wait_ge(s_const, 1)
            for i in range(2):
                count_tiles(i)
                deal(i)
            pe.wait_ge(s_w, 16 * N_WEIGHTS)
            nc.tensor.transpose(bank(7)[:, 0:NQ], b1r[:, :], ident[0:NQ, 0:NQ]).then_inc(s_b1, 1)
            for l in range(2):
                node_stage(l)
                meet(pe, 1 + 2 * l)
                e = ES[l]

                def fetch_q(par, at, n):
                    pe.wait_ge(e["ST"], n)
                    for j in range(G):
                        last = nc.tensor.matmul(bank(2 + par)[:, j * 128:(j + 1) * 128], ST[:, par, j, :], flat(Q[:, ds(at[j // 2], 1), :]), start=True, stop=True)
                    last.then_inc(e["q"], 1)

                pe.sem_inc(e["agg"], 2 * GP)
                pe.wait_ge(e["zero"], 1)
                transposed_S(e["S"], e["tr"], 0, 0, 1)
                transposed_S(e["S"], e["tr"], 1, 1, 2)
                fetch_q(0, node_tiles(tmap[0], 0, GP), 1)
                with pe.Fori(0, IT1) as it:
                    for r in range(R1):
                        g = it * R1 + r
                        at = node_tiles(tmap[0], g * GP, 2 * GP)
                        transposed_S(e["S"], e["tr"], (r + 2) % RB1, r % 2, g + 3)
                        fetch_q((r + 1) % 2, at[GP:], g + 2)
                        add_up(e, e["vals"], g, at, r % RB1, r % 2, vals, AGG, DV)
                meet(pe, 2 + 2 * l)
            node_stage(2)
            meet(pe, 5)
            pe.sem_inc(GS["tr"], 2)
            with pe.Fori(0, IT2) as it:
                for k in range(R2):
                    g = it * R2 + k
                    pe.wait_ge(GS["head"], g + 2)
                    pe.wait_ge(GS["red"], g + 1)
                    for j in range(G):
                        for h in range(HG):
                            b = 4 * (k % 2) + 2 * (j // 2) + h // 2
                            last = nc.tensor.transpose(bank(b)[0:NP, (h % 2) * PAIR + (j % 2) * 128:(h % 2) * PAIR + (j % 2 + 1) * 128],
                                                       masks[:, k % 2, j, h, :], ident[:, :])
                    last.then_inc(GS["tr"], 1)
            meet(pe, 6)

            def look_up(par, at, n):
                pe.wait_ge(GS["ST"], n)
                for j in range(G):
                    last = nc.tensor.matmul(bank(2 + par)[:, j * 2 * HG:(j + 1) * 2 * HG], ST[:, par, j, :],
                                            adm[:, ds(at[j // 2], 1), :, :].rearrange("p a b h -> p (a b h)"), start=True, stop=True)
                last.then_inc(GS["look"], 1)

            pe.sem_inc(GS["agg"], 2 * GP)
            pe.wait_ge(GS["zero"], 1)
            transposed_S(GS["S"], GS["tr2"], 0, 0, 1)
            transposed_S(GS["S"], GS["tr2"], 1, 1, 2)
            look_up(0, node_tiles(tmap[1], 0, GP), 1)
            with pe.Fori(0, IT2) as it:
                for k in range(R2):
                    g = it * R2 + k
                    at = node_tiles(tmap[1], g * GP, 2 * GP)
                    transposed_S(GS["S"], GS["tr2"], (k + 2) % RB, k % 2, g + 3)
                    look_up((k + 1) % 2, at[GP:], g + 2)
                    add_up(GS, GS["msg"], g, at, k % RB, k % 2, msg, AGG[:, :, 0:DG], DG)
            meet(pe, 7)
            pe.wait_ge(s_w12, 16 * 3 * NX)
            pe.sem_inc(MS["out"], 2 * CH)
            with pe.Fori(0, NCH) as c:
                def hidden(ex):
                    for f in range(FC):
                        q = ex * FC + f
                        pe.wait_ge(MS["gelu"], c * NQ + q + 1)
                        for h, (at, n) in enumerate(((0, HALF), (HALF, CH * NP - HALF))):
                            for a in range(2):
                                last = nc.tensor.matmul(PS[:, 2 * (q % 2) + h, 0:n], w1_sb[:, a, q * 128:(q + 1) * 128],
                                                        yT[:, a, ds(c * CH * NP + at, n)], start=(a == 0), stop=(a == 1))
                        last.then_inc(MS["hid"], 1)

                def back(ex):
                    pe.wait_ge(MS["gelu"], c * NQ + (ex + 1) * FC + 2)
                    for k in range(CH):
                        pe.wait_ge(MS["acc"], (c * NX + ex) * CH + k + 1)
                        for f in range(FC):
                            last = nc.tensor.matmul(bank(4 + (ex * CH + k) % 4)[0:NP, 0:DM], hid[:, ex % 2, f, k * NP:(k + 1) * NP],
                                                    w2_sb[:, ex * FC + f, :], start=(f == 0), stop=(f == FC - 1))
                        last.then_inc(MS["out"], 1)

                hidden(0)
                for ex in range(NX):
                    if ex + 1 < NX:
                        hidden(ex + 1)
                    back(ex)

        @block.vector
        def _(dve):
            v = nc.vector
            own = Count(dve, s_dve)

            dve.wait_ge(s_iota, 2)
            v.tensor_copy(iota_t[:, :], column_i[:, :])
            v.tensor_copy(iota_l[:, :], column_i[:, 0:128])
            v.tensor_copy(iota_n[:, :], column_i[:, 0:NP])
            v.tensor_scalar(before[:, :], diff_i[:, :], 0.0, None, ALU.is_lt)
            v.tensor_scalar(before256[:, :], diff_i[:, 0:NT], 0.0, float(PAIR), ALU.is_lt, ALU.mult)
            v.tensor_scalar(ident16[:, :], diff_i[:, :], 0.0, None, ALU.is_equal)
            v.tensor_scalar(upto[:, :], diff_i[:, :], 0.0, None, ALU.is_le)
            v.tensor_scalar(ident[:, :], diff_i[:, :], 0.0, None, ALU.is_equal)
            v.memset(zeros16[:, :], 0.0)
            v.memset(cend[:, 0:1], 0.0)
            for i, T in enumerate((T1, T2)):
                v.memset(tmap[i][:, :], 0)
                v.memset(idx[i][:, T:], 0)
                v.memset(loc[i][:, T:], -1.0)
            v.memset(ones[:, :], 1.0).then_inc(s_const, 1)
            dve.wait_ge(s_const, 1)

            def rint(ap):
                own.wait()
                own.did(v.tensor_scalar(ap, ap, RND, RND, ALU.add, ALU.subtract))
                own.wait()

            dve.wait_ge(s_lists, 64)
            for i in range(2):
                P, J, T, s = (P1, P2)[i], (J1, J2)[i], (T1, T2)[i], D_[i]
                key, p_, t_, y_, c_, z_ = (a[0:P, 0:J] for a in (pos, kp, kt, pay, tcol, counts))
                hot_p = hot[0:P, 0:NT * J]
                cnt_p = counts[0:P, 0:NT * J]
                by_tile = lambda a: a.rearrange("p (b j) -> p b j", b=NT)
                own.did(v.tensor_copy(key, key_i[i][:, :]))
                own.wait()
                own.did(v.tensor_scalar(p_, key, -float(NT // 2), 1.0 / NT, ALU.add, ALU.mult))
                rint(p_)
                own.did(v.scalar_tensor_tensor(t_, p_, -float(NT), key, ALU.mult, ALU.add))
                own.wait()
                own.did(v.tensor_tensor(by_tile(hot_p), t_[:, None, :].broadcast_to([P, NT, J]),
                                        iota_n[0:P, 0:NT][:, :, None].broadcast_to([P, NT, J]), ALU.is_equal))
                own.wait()
                own.did(v.tensor_tensor_scan(cnt_p, hot_p, hot_p, 0.0, ALU.add, ALU.max))
                own.wait()
                own.did(v.tensor_copy(cend[0:P, 1:NT + 1], by_tile(cnt_p)[:, :, J - 1]))
                own.wait()
                v.tensor_tensor(cnt[0:P, :], cend[0:P, 1:NT + 1], cend[0:P, 0:NT], ALU.subtract).then_inc(s["cnt"], 1)
                dve.wait_ge(s["total"], 1)
                own.did(v.tensor_scalar(tiles[:, :], bank(4)[0:NT, 0:1], (PAIR - 1) / 2, 1.0 / PAIR, ALU.add, ALU.mult))
                rint(tiles[:, :])
                v.tensor_scalar(tiles_b[:, :], ones[0:NT, :], tiles[:, 0:1], None, ALU.mult).then_inc(s["tiles"], 1)
                dve.wait_ge(s["base"], 1)
                own.did(v.tensor_copy(ends[:, :], bank(5)[0:NT, 0:1]))
                own.did(v.scalar_tensor_tensor(base[0:P, :], bank(6)[0:P, 0:NT], -1.0, cend[0:P, 0:NT], ALU.add, ALU.subtract))
                own.wait()
                v.tensor_scalar(past[:, 0:T // 2], iota_t[0:NT - 1, 0:T // 2], ends[0:NT - 1, 0:1], None, ALU.is_ge).then_inc(s["past"], 1)
                own.did(v.tensor_tensor(by_tile(cnt_p), by_tile(cnt_p), base[0:P, :][:, :, None].broadcast_to([P, NT, J]), ALU.add))
                own.wait()
                own.did(v.tensor_tensor(cnt_p, cnt_p, hot_p, ALU.mult))
                own.wait()
                own.did(v.tensor_reduce(key, cnt_p.rearrange("p (b j) -> p j b", b=NT), AX.X, ALU.add))
                own.wait()
                own.did(v.tensor_scalar(c_, key, -63.5, 1.0 / 128, ALU.add, ALU.mult))
                rint(c_)
                own.did(v.scalar_tensor_tensor(key, c_, -128.0, key, ALU.mult, ALU.add))
                own.did(v.tensor_scalar(y_, pay_i[i][:, :], -float(MID), None, ALU.add))
                own.did(v.tensor_scalar(p_, p_, 1.0, None, ALU.add))
                dve.wait_ge(s["map"], 1)
                own.did(v.tensor_copy(tmap[i][0:1, 0:T // 2], bank(7)[0:1, 0:T // 2]))
                own.wait()
                with dve.Fori(0, J // (2 * U)) as it:
                    for par in range(2):
                        dve.wait_ge(s["dealt"], it * 2 + par + 1)
                        for u in range(U):
                            j = (it * 2 + par) * U + u
                            v.tensor_scalar(hotT[0:P, par, u, 0:T], iota_t[0:P, 0:T], tcol[0:P, ds(j, 1)], None, ALU.is_equal)
                            v.tensor_scalar(hotL[0:P, par, u, 0, :], iota_l[0:P, :], pos[0:P, ds(j, 1)], pay[0:P, ds(j, 1)], ALU.is_equal, ALU.mult)
                            last = v.tensor_scalar(hotL[0:P, par, u, 1, :], iota_l[0:P, :], pos[0:P, ds(j, 1)], kp[0:P, ds(j, 1)], ALU.is_equal, ALU.mult)
                        last.then_inc(s["hot"], 1)
                dve.wait_ge(s["all"], 1)
                own.did(v.tensor_scalar(idx[i][:, 0:T], bank(2 * i)[:, 0:T], float(MID), None, ALU.add))
                own.did(v.tensor_scalar(loc[i][:, 0:T], bank(2 * i + 1)[:, 0:T], -1.0, None, ALU.add))
            own.wait()

            def layer_norm(o, s, var, std_done, source, width, eps, to, norm=None):
                if o.n:
                    o.wait()
                dve.sem_inc(s_held_dve, 1)
                for k in range(CH):
                    o.did(v.bn_stats(st6[:, k, :], source(k)))
                o.wait()
                dve.sem_inc(s_held_dve, 1)
                for k in range(CH):
                    o.did(v.bn_aggr(mv[:, k, :], st6[:, k, :]))
                o.wait()
                v.tensor_scalar(mv[:, :, 1], mv[:, :, 1], eps, None, ALU.add).then_inc(s[var], 1)
                dve.wait_ge(s[std_done], o.round + 1)
                o.did(v.reciprocal(std[:, :], std[:, :]))
                o.wait()
                for k in range(CH):
                    last = v.tensor_scalar(to(k), source(k), mv[:, k, 0:1], std[:, k:k + 1], ALU.subtract, ALU.mult)
                    if norm:
                        last.then_inc(s[norm], 1)
                    else:
                        o.did(last)

            OWN = [11, 4 + 16 + 1, 4 + 16 + 1 + 1 + 11]

            def node_stage(l):
                s = NS[l]
                dve.sem_inc(s["e5"], CREDIT)
                if l == 2:
                    dve.sem_inc(s["projc"], CREDIT)
                    dve.sem_inc(s["hc"], CREDIT)
                with dve.Fori(0, NCH) as c:
                    o = Count(dve, s["own"], c * OWN[l])
                    o.round = c
                    if l == 0:
                        layer_norm(o, s, "var", "std", lambda k: flat(X[:, ds(c * CH + k, 1), :]), DM, 1e-5, lambda k: xn[:, k, :], "norm")
                        dve.wait_ge(s["keep"], c + 1)
                        for k in range(CH):
                            dve.wait_ge(s["emb"], c * CH + k + 1)
                            v.tensor_tensor(e5[:, k, :], bank(2 + k % 2)[0:NP, 0:D], bP[:, :], ALU.add).then_inc(s["e5"], 1)
                    else:
                        sums = AGG[:, ds(c * CH, CH), 0:D].rearrange("p t (h d) -> p t h d", h=H)
                        e5h = e5[:, :, :].rearrange("p t (h d) -> p t h d", h=H)
                        o.did(v.tensor_scalar(rden[:, :, :], AGG[:, ds(c * CH, CH), D:DV], 1e-8, None, ALU.add))
                        o.wait()
                        o.did(v.reciprocal(rden[:, :, :], rden[:, :, :]))
                        o.wait()
                        if l == 1:
                            dve.wait_ge(s["keep"], c + 1)
                        o.did(v.tensor_tensor(e5h, sums, rden[:, :, :][:, :, :, None].broadcast_to([NP, CH, H, HD]), ALU.mult))
                        o.wait()
                        o.did(v.tensor_tensor(e5[:, :, :], e5[:, :, :], EMB[:, ds(c * CH, CH), :], ALU.add))
                        layer_norm(o, s, "var", "std", lambda k: e5[:, k, :], D, 1e-6, lambda k: e5[:, k, :])
                        o.wait()
                        o.did(v.tensor_tensor(e5[:, :, :], e5[:, :, :], ln_s[:, l - 1, :][:, None, :].broadcast_to([NP, CH, D]), ALU.mult))
                        o.wait()
                        v.tensor_tensor(e5[:, :, :], e5[:, :, :], ln_b[:, l - 1, :][:, None, :].broadcast_to([NP, CH, D]), ALU.add).then_inc(s["e5"], CH)
                    if l == 2:
                        for k in range(CH):
                            xk = flat(X[:, ds(c * CH + k, 1), :])
                            dve.wait_ge(s["proj"], c * CH + k + 1)
                            v.tensor_tensor(xk, bank(6 + k % 2)[0:NP, 0:DM], xk, ALU.add).then_inc(s["projc"], 1)
                        dve.wait_ge(s["projc"], (c + 1) * CH + CREDIT)
                        xc = X[:, ds(c * CH, CH), :]
                        o.did(v.tensor_tensor(xc, xc, binv[:, :][:, None, :].broadcast_to([NP, CH, DM]), ALU.add))
                        layer_norm(o, s, "yvar", "ystd", lambda k: flat(X[:, ds(c * CH + k, 1), :]), DM, 1e-5, lambda k: xn[:, k, :], "norm")
                        for k in range(CH):
                            dve.wait_ge(s["h"], c * CH + k + 1)
                            v.tensor_copy(flat(hn[:, ds(c * CH + k, 1), 0:NF]), bank(2 + k % 2)[0:NP, 0:NF]).then_inc(s["hc"], 1)
                    assert o.n == OWN[l], (l, o.n)

            dve.wait_ge(s_x, 16)
            dve.wait_ge(s_w, 16 * N_WEIGHTS)
            own.did(v.tensor_tensor(bP[:, :], bP[:, :], bPos[:, :], ALU.add))
            dve.wait_ge(s_b1, 1)
            own.did(v.tensor_copy(b1c[:, :], bank(7)[:, 0:NQ]))
            own.wait()
            for l in range(2):
                node_stage(l)
                e = ES[l]

                def build_S(par, group):
                    v.tensor_tensor(S[:, par, :, :], iota_n[:, :][:, None, :].broadcast_to([128, G, NP]),
                                    loc[0][:, ds(group * G, G)][:, :, None].broadcast_to([128, G, NP]), ALU.is_equal).then_inc(e["S"], 1)

                def stage_indices(r, group):
                    v.tensor_copy(ix[:, r, :], idx[0][:, ds(group * G, G)]).then_inc(e["slot"], 1)

                meet(dve, 1 + 2 * l)
                v.memset(AGG[:, :, :], 0.0).then_inc(e["zero"], 1)
                for r in range(RB1):
                    stage_indices(r, r)
                build_S(0, 0)
                build_S(1, 1)
                PER = 2
                with dve.Fori(0, IT1) as it:
                    for r in range(R1):
                        g, par, rb = it * R1 + r, r % 2, r % RB1
                        o = Count(dve, e["own"], g * PER)
                        dve.wait_ge(e["q"], g + 1)
                        dve.wait_ge(s_kv[l][rb], (it * (R1 // RB1) + r // RB1 + 1) * 16 * G)
                        o.did(v.tensor_tensor(prod[:, :, :], bank(2 + par).rearrange("p (j d) -> p j d", j=G), kv[:, rb, :, 0:D], ALU.mult))
                        o.wait()
                        o.did(v.tensor_reduce(logit[:, :, :], prod[:, :, :].rearrange("p j (h d) -> p j h d", h=H), AX.X, ALU.add))
                        o.wait()
                        v.tensor_scalar(att[:, par, :, :], logit[:, :, :], 10.0, -10.0, ALU.min, ALU.max).then_inc(e["clip"], 1)
                        dve.wait_ge(e["agg"], g * GP + GP)
                        build_S((r + 2) % RB1, g + 2)
                        dve.wait_ge(e["exp"], g + 1)
                        v.tensor_tensor(vals[:, par, :, 0:D].rearrange("p j (h d) -> p j h d", h=H),
                                        kv[:, rb, :, D:2 * D].rearrange("p j (h d) -> p j h d", h=H),
                                        vals[:, par, :, D:DV][:, :, :, None].broadcast_to([128, G, H, HD]), ALU.mult).then_inc(e["vals"], 1)
                        stage_indices(rb, g + RB1)
                        assert o.n == PER
                meet(dve, 2 + 2 * l)

            node_stage(2)
            h_ = hn[:, :, 0:NF]
            a_src, a_dst, top = hn[:, :, NF:DG], adm[:, :, 0, :], adm[:, :, 1, :]
            over = lambda a, n=NF: a[:, None, :].broadcast_to([NP, NT, n])
            by_head = lambda a: a.rearrange("p t (h e) -> p t h e", h=HG)
            dve.wait_ge(NS[2]["hc"], NT + CREDIT)
            own.did(v.tensor_tensor(t16[:, :, :], h_, over(gvec[:, 0, :]), ALU.mult))
            own.did(v.tensor_tensor(t16b[:, :, :], h_, over(gvec[:, 1, :]), ALU.mult))
            own.wait()
            own.did(v.tensor_reduce(a_dst, by_head(t16b[:, :, :]), AX.X, ALU.add))
            v.tensor_reduce(a_src, by_head(t16[:, :, :]), AX.X, ALU.add).then_inc(GS["diff"], 1)
            dve.wait_ge(GS["diff"], 1)
            own.did(v.tensor_copy(mx[:, :, :], a_src))
            own.wait()
            meet(dve, 5)

            def mask_group(par, group):
                for j in range(G):
                    last = v.tensor_scalar(S[:, par, j, :], iota_n[:, :], loc[1][:, ds(group * G + j, 1)], -BIG, ALU.not_equal, ALU.mult)
                last.then_inc(GS["mask"], 1)

            def stage_rows(k, group):
                v.tensor_copy(ix[:, k, :], idx[1][:, ds(group * G, G)]).then_inc(GS["slot"], 1)

            dve.sem_inc(GS["red"], 2)
            for k in range(RB):
                stage_rows(k, k)
            mask_group(0, 0)
            with dve.Fori(0, IT2) as it:
                for k in range(R2):
                    g, par = it * R2 + k, k % 2
                    o = Count(dve, GS["own"], g * GP)
                    dve.wait_ge(GS["head"], g + 1)
                    mask_group(1 - par, g + 1)
                    dve.wait_ge(GS["tr"], g + 3)
                    v.tensor_reduce(tmx[:, :, :].rearrange("p j h -> p (j h)"),
                                    PS[0:NP, 4 * par:4 * par + G, :].rearrange("p j (h n) -> p (j h) n", n=PAIR), AX.X, ALU.max).then_inc(GS["red"], 1)
                    _, at = nc.values_load_multi_w_load_instructions(
                        tmap[1][0:1, ds(g * GP, GP)], engines=[v.engine], min_val=0, max_val=NT - 1,
                        skip_runtime_bounds_check_because="it counts up to 24 comparisons")
                    dve.wait_ge(GS["red"], g + 3)
                    for j in range(GP):
                        m = flat(mx[:, ds(at[j], 1), :])
                        o.did(v.tensor_tensor(m, tmx[:, j, :], m, ALU.max))
                        o.wait()
                    stage_rows(k % RB, g + RB)
            def leaky_sum(to, a):
                own.did(v.tensor_tensor(t4[:, :, :], a, a_dst, ALU.add))
                own.wait()
                own.did(v.scalar_tensor_tensor(to, t4[:, :, :], 0.2, t4[:, :, :], ALU.mult, ALU.max))
                own.wait()

            leaky_sum(top, mx[:, :, :])
            leaky_sum(selfe[:, :, :], a_src)
            v.tensor_tensor(selfe[:, :, :], selfe[:, :, :], top, ALU.subtract).then_inc(GS["diff"], 1)
            meet(dve, 6)

            GAG = AGG[:, :, 0:DG]
            dve.wait_ge(GS["self"], 1)
            own.did(v.tensor_tensor(by_head(GAG[:, :, 0:NF]), by_head(h_), selfe[:, :, :][:, :, :, None].broadcast_to([NP, NT, HG, NX]), ALU.mult))
            own.did(v.tensor_copy(GAG[:, :, NF:DG], selfe[:, :, :]))
            own.wait()
            dve.sem_inc(GS["zero"], 1)

            def gate_S(par, group):
                v.tensor_tensor(S[:, par, :, :], iota_n[:, :][:, None, :].broadcast_to([128, G, NP]),
                                loc[1][:, ds(group * G, G)][:, :, None].broadcast_to([128, G, NP]), ALU.is_equal).then_inc(GS["S"], 1)

            gate_S(0, 0)
            gate_S(1, 1)
            PER2 = 3
            with dve.Fori(0, IT2) as it:
                for k in range(R2):
                    g, par = it * R2 + k, k % 2
                    o = Count(dve, GS["own2"], g * PER2)
                    got = bank(2 + par)[:, 0:G * 2 * HG].rearrange("p (j a h) -> p j a h", j=G, a=2)
                    dve.wait_ge(GS["look"], g + 1)
                    o.did(v.tensor_tensor(logit[:, :, 0:HG], GAT[:, ds(g * G, G), NF:DG], got[:, :, 0, :], ALU.add))
                    o.wait()
                    o.did(v.scalar_tensor_tensor(logit[:, :, HG:H], logit[:, :, 0:HG], 0.2, logit[:, :, 0:HG], ALU.mult, ALU.max))
                    o.wait()
                    o.did(v.tensor_tensor(logit[:, :, 0:HG], logit[:, :, HG:H], got[:, :, 1, :], ALU.subtract))
                    o.wait()
                    v.tensor_scalar(att[:, par, :, 0:HG], logit[:, :, 0:HG], 0.0, None, ALU.min).then_inc(GS["e"], 1)
                    dve.wait_ge(GS["agg"], g * GP + GP)
                    gate_S((k + 2) % RB, g + 2)
                    dve.wait_ge(GS["exp"], g + 1)
                    v.tensor_tensor(msg[:, par, :, 0:NF].rearrange("p j (h e) -> p j h e", h=HG),
                                    GAT[:, ds(g * G, G), 0:NF].rearrange("p j (h e) -> p j h e", h=HG),
                                    msg[:, par, :, NF:DG][:, :, :, None].broadcast_to([128, G, HG, NX]), ALU.mult).then_inc(GS["msg"], 1)
                    assert o.n == PER2
            dve.wait_ge(GS["sum"], T2 // 2 + 1)

            t, tb = t16[:, :, :], t16b[:, :, :]
            wide = lambda a, n=NF: a[:, :, None].broadcast_to([NP, NT, n])
            own.did(v.tensor_scalar(t4[:, :, :], GAG[:, :, NF:DG], 1e-16, None, ALU.add))
            own.wait()
            own.did(v.reciprocal(t4[:, :, :], t4[:, :, :]))
            own.wait()
            own.did(v.tensor_tensor(by_head(t), by_head(GAG[:, :, 0:NF]), t4[:, :, :][:, :, :, None].broadcast_to([NP, NT, HG, NX]), ALU.mult))
            own.wait()
            own.did(v.tensor_tensor(t, t, over(gvec[:, 2, :]), ALU.add))
            own.wait()
            own.did(v.tensor_reduce(t1[:, :], t, AX.X, ALU.add))
            own.wait()
            own.did(v.tensor_scalar(t1[:, :], t1[:, :], 1.0 / NF, None, ALU.mult))
            own.wait()
            own.did(v.tensor_tensor(t, t, wide(t1[:, :]), ALU.subtract))
            own.wait()
            own.did(v.tensor_tensor(tb, t, t, ALU.mult))
            own.wait()
            own.did(v.tensor_reduce(t1[:, :], tb, AX.X, ALU.add))
            own.wait()
            v.tensor_scalar(t1[:, :], t1[:, :], 1.0 / NF, 1e-5, ALU.mult, ALU.add).then_inc(GS["var"], 1)
            dve.wait_ge(GS["std"], 1)
            own.did(v.reciprocal(t1b[:, :], t1b[:, :]))
            own.wait()
            own.did(v.tensor_tensor(t, t, wide(t1b[:, :]), ALU.mult))
            own.wait()
            own.did(v.tensor_tensor(t, t, over(gvec[:, 3, :]), ALU.mult))
            own.wait()
            own.did(v.tensor_tensor(t, t, over(gvec[:, 4, :]), ALU.add))
            own.wait()
            own.did(v.tensor_reduce(score[:, :, :], t.rearrange("p t (h e) -> p t e h", h=HG), AX.X, ALU.add))
            own.wait()
            own.did(v.tensor_scalar(score[:, :, :], score[:, :, :], 1.0 / HG, None, ALU.mult))
            own.did(v.memset(rank[:, :, :], 0.0))
            own.wait()
            own.did(v.tensor_reduce(t1[:, :], score[:, :, :], AX.X, ALU.max))
            for j in range(NX):
                sj = score[:, :, j]
                own.did(v.tensor_tensor(gate[:, :, :], wide(sj, NX), score[:, :, :], ALU.is_gt))
                own.wait()
                own.did(v.tensor_tensor(rank[:, :, :], rank[:, :, :], gate[:, :, :], ALU.add))
                own.wait()
                if j + 1 < NX:
                    own.did(v.tensor_tensor(gate[:, :, j + 1:], wide(sj, NX - 1 - j), score[:, :, j + 1:], ALU.is_equal))
                    own.wait()
                    own.did(v.tensor_tensor(rank[:, :, j + 1:], rank[:, :, j + 1:], gate[:, :, j + 1:], ALU.add))
                    own.wait()
            v.tensor_tensor(t4[:, :, :], score[:, :, :], wide(t1[:, :], NX), ALU.subtract).then_inc(GS["s"], 1)
            dve.wait_ge(GS["sexp"], 1)
            own.did(v.scalar_tensor_tensor(gate[:, :, :], rank[:, :, :], 1.5, e4[:, :, :], ALU.is_lt, ALU.mult))
            own.wait()
            own.did(v.tensor_reduce(t1[:, :], gate[:, :, :], AX.X, ALU.add))
            own.wait()
            own.did(v.reciprocal(t1[:, :], t1[:, :]))
            own.wait()
            own.did(v.tensor_tensor(gate[:, :, :], gate[:, :, :], wide(t1[:, :], NX), ALU.mult))
            own.wait()
            meet(dve, 7)

            dve.sem_inc(MS["acc"], 4)
            with dve.Fori(0, NCH) as c:
                o = Count(dve, MS["own"], c * NX * CH)
                for ex in range(NX):
                    for k in range(CH):
                        xk = flat(X[:, ds(c * CH + k, 1), :])
                        o.did(v.scalar_tensor_tensor(xk, b2b[:, ex, :], flat(gate[:, ds(c * CH + k, 1), ex:ex + 1]), xk, ALU.mult, ALU.add))
                    o.wait()
                for ex in range(NX):
                    for k in range(CH):
                        xk = flat(X[:, ds(c * CH + k, 1), :])
                        dve.wait_ge(MS["out"], (c * NX + ex) * CH + k + 1 + 2 * CH)
                        v.scalar_tensor_tensor(xk, bank(4 + (ex * CH + k) % 4)[0:NP, 0:DM],
                                               flat(gate[:, ds(c * CH + k, 1), ex:ex + 1]), xk, ALU.mult, ALU.add).then_inc(MS["acc"], 1)
                    dve.wait_ge(MS["acc"], (c * NX + ex + 1) * CH + 4)
                dve.sem_inc(MS["fin"], 1)


_INS = ['x', 'src', 'dst', 'L0_gnn_W_P_w', 'L0_gnn_W_P_b', 'L0_gnn_W_pos', 'L0_gnn_q1', 'L0_gnn_k1', 'L0_gnn_v1',
        'L0_gnn_ln1_s', 'L0_gnn_ln1_b', 'L0_gnn_q2', 'L0_gnn_k2', 'L0_gnn_v2', 'L0_gnn_ln2_s', 'L0_gnn_ln2_b',
        'L0_gnn_inv_w', 'L0_gnn_inv_b', 'L0_ffn_W_gat', 'L0_ffn_att_src', 'L0_ffn_att_dst', 'L0_ffn_b_gat',
        'L0_ffn_ln_gamma', 'L0_ffn_ln_beta', 'L0_ffn_W1', 'L0_ffn_b1', 'L0_ffn_W2', 'L0_ffn_b2', 'L0_ffn_edge_index']


def kernel(**inputs):
    import numpy as np
    import concourse.bacc as bacc
    from concourse.bass_utils import run_bass_kernel_spmd

    nc = bacc.Bacc("TRN2", target_bir_lowering=False, num_devices=1)
    arrays, args = {}, []
    for name in _INS:
        a = np.ascontiguousarray(inputs[name])
        arrays[f"in_{name}"] = a
        args.append(nc.dram_tensor(f"in_{name}", a.shape, mybir.dt.from_np(a.dtype), kind="ExternalInput").ap())
    out = nc.dram_tensor("out", inputs["x"].shape, mybir.dt.float32, kind="ExternalOutput").ap()
    graph_block_kernel(nc, *args, out)
    r = run_bass_kernel_spmd(nc, [arrays], core_ids=[0])
    return r.results[0]["out"]
```

```python
import concourse.bass as bass
from concourse import mybir
from contextlib import ExitStack



def graph_block_kernel(nc, x, src, dst, W_P_w, W_P_b, W_pos, q1, k1, v1, ln1_s, ln1_b,
                       q2, k2, v2, ln2_s, ln2_b, inv_w, inv_b,
                       W_gat, att_src, att_dst, b_gat, ln_gamma, ln_beta, W1, b1, W2, b2,
                       ffn_edges, out):
    f32, f16, bf16, i32 = mybir.dt.float32, mybir.dt.float16, mybir.dt.bfloat16, mybir.dt.int32
    ALU = mybir.AluOpType
    ACT = mybir.ActivationFunctionType
    AX = mybir.AxisListType
    ds = bass.ds

    N, DM = x.shape
    NP, NT = 125, 25
    H, HD = 8, 16
    D = H * HD
    DV = D + H
    CH = 5
    NCH = NT // CH
    G = 4
    GP = G // 2
    R1, RB1 = 10, 5
    R2, RB = 4, 4
    PAIR = 256
    E1, E2 = src.shape[0], ffn_edges.shape[1]
    P1, P2 = 125, 128
    J1, J2 = E1 // P1, E2 // P2
    most = lambda edges, unit: -(-2 * ((edges + NT * (PAIR - 1)) // PAIR) // unit) * unit
    T1, T2 = most(E1, G * R1), most(E2, G * R2)
    IT1, IT2 = T1 // (G * R1), T2 // (G * R2)
    U = 8
    SPREAD = 3
    STEPS = R1 // SPREAD
    NX, HG = 4, 4
    NF = NX * HG
    DG = NF + HG
    NPART = 3
    DR = DG + NPART * HG // 2
    KR = G * NPART * HG
    FF = W1.shape[2]
    FC = FF // 128
    NQ = NX * FC
    MID = N // 2
    RND = 12582912.0
    BIG = 1e30
    NG2 = IT2 * R2
    FAST = NT - IT2
    assert R2 == NX and 0 <= FAST <= IT2
    assert N == NP * NT and J1 % (2 * U) == 0

    node = lambda ap: ap.rearrange("(p t) d -> p t d", t=NT)
    flat = lambda ap: ap.rearrange("p a d -> p (a d)")
    kv_tab = nc.dram_tensor("kv_tab", (N, 2 * D), f32, kind="Internal").ap()
    gate_tab = nc.dram_tensor("gate_tab", (N, DR), f32, kind="Internal").ap()
    expert_tab = nc.dram_tensor("expert_tab", (NT, NP, NX * DM), f32, kind="Internal").ap()

    ctx = ExitStack()
    with ctx:
        def sb(name, shape, dt=f32):
            return ctx.enter_context(nc.sbuf_tensor(name, shape, dt))

        def sem(name):
            return ctx.enter_context(nc.semaphore(name))

        X = sb("X", [NP, NT, DM])
        AGG = sb("AGG", [NP, NT, DV])
        idx = [sb("idx1", [128, T1 + RB1 * G], i32), sb("idx2", [128, T2 + RB * G], i32)]
        loc = [sb("loc1", [128, T1 + 2 * G]), sb("loc2", [128, T2 + 2 * G])]
        tmap = [sb("tmap1", [1, T1 // 2 + 2 * GP], i32), sb("tmap2", [1, T2 // 2 + 2 * GP], i32)]
        ident = sb("ident", [128, 128])
        ident16 = sb("ident16", [128, 128], bf16)
        before = sb("before", [128, 128])
        upto = sb("upto", [128, 128])
        before256 = sb("before256", [128, NT])
        ones = sb("ones", [128, 128])
        zeros16 = sb("zeros16", [128, 128], f16)
        iota_128 = sb("iota_128", [128, 128])
        iota_n = iota_128[:, 0:NP]
        iota_t = sb("iota_t", [128, T1], f16)
        diff_i = sb("diff_i", [128, 128], i32)

        region_a = sb("region_a", [128, NT * J1])
        counts = region_a[:, :]
        w1_sb = region_a[:, 0:2 * NX * FF].rearrange("p (k f) -> p k f", k=2)
        w2_sb = region_a[:, 2 * NX * FF:2 * NX * FF + NQ * DM].rearrange("p (c n) -> p c n", n=DM)
        region_b = sb("region_b", [128, NT * 2 * D])
        hot = region_b[:, 0:NT * J1 // 2].bitcast(f16)
        kv_st = region_b[0:NP, :].rearrange("p (t d) -> p t d", t=NT)
        spilled = region_b[0:NP, 0:CH * NX * DM].rearrange("p (k e n) -> p k e n", k=CH, e=NX)
        yT = region_b[:, 0:2 * N].rearrange("p (k n) -> p k n", k=2)
        region_c = sb("region_c", [128, NT * 2 * D])
        Q = region_c[0:NP, 0:NT * D].rearrange("p (t d) -> p t d", t=NT)
        EMB = region_c[0:NP, NT * D:2 * NT * D].rearrange("p (t d) -> p t d", t=NT)
        GAT = region_c[:, 0:(T2 + G) * DG].rearrange("p (t d) -> p t d", d=DG)
        region_k = sb("region_k", [128, RB1 * G * 2 * D])
        kv = region_k[:, :].rearrange("p (r j d) -> p r j d", r=RB1, j=G)

        def parts(region, *sizes):
            at = 0
            for n in sizes:
                yield region[:, at:at + n]
                at += n

        part_of, kt, pay, pos, tcol, key1, pay1, key2, pay2, column, past = parts(
            region_c, J1, J1, J1, J1, J1, J1, J1, J2, J2, T1, T1)
        key_i = [key1[0:P1, :].bitcast(i32), key2[0:P2, :].bitcast(i32)]
        pay_i = [pay1[0:P1, :].bitcast(i32), pay2[0:P2, :].bitcast(i32)]
        column_i = column.bitcast(i32)
        past = past[0:NT - 1, :]
        cend = sb("cend", [128, NT + 1])
        cnt = sb("cnt", [128, NT])
        base = sb("base", [128, NT])
        tiles = sb("tiles", [NT, 1])
        tiles_b = sb("tiles_b", [NT, 128])
        ends = sb("ends", [NT, 1])
        hotT = region_b[:, 0:U * T1].bitcast(f16).rearrange("p (r u t) -> p r u t", r=2, u=U)
        at_lane, hot_other, hot_part, lane_of = parts(region_k, U * 128, U * 128, U * 128, U * 64)
        at_lane, hot_other = (a.bitcast(f16).rearrange("p (r l u) -> p r l u", r=2, u=U) for a in (at_lane, hot_other))
        hot_part = hot_part.bitcast(f16).rearrange("p (r u l) -> p r u l", r=2, u=U)
        lane_of = lane_of.bitcast(f16).rearrange("p (l u) -> p l u", u=U)
        JD = IT1 * STEPS * U
        assert JD >= J2
        behind_counts = region_a[:, NT * J2:]
        part_of2, tcol2, lane2, pay2_16 = parts(behind_counts, JD, JD, JD // 2, JD // 2)
        hotT2, at_lane2, hot_other2, hot_part2, lane_of2 = parts(region_a[:, 0:NT * J2], U * T2, *[U * 128] * 3, U * 64)
        hotT2 = hotT2.bitcast(f16).rearrange("p (r u t) -> p r u t", r=2, u=U)
        at_lane2, hot_other2 = (a.bitcast(f16).rearrange("p (r l u) -> p r l u", r=2, u=U) for a in (at_lane2, hot_other2))
        hot_part2 = hot_part2.bitcast(f16).rearrange("p (r u l) -> p r u l", r=2, u=U)
        lane_of2 = lane_of2.bitcast(f16).rearrange("p (l u) -> p l u", u=U)
        part_of = [part_of[0:P1, :], part_of2[0:P2, :]]
        tcol = [tcol[0:P1, :], tcol2[0:P2, :]]
        lane = [kt[0:P1, :].bitcast(f16)[:, J1:2 * J1], lane2[0:P2, :].bitcast(f16)]
        other_end = [pay[0:P1, :].bitcast(f16)[:, 0:J1], pay2_16[0:P2, :].bitcast(f16)]

        wP = sb("wP", [128, 2, D])
        wqkv = sb("wqkv", [128, 2, 3 * D])
        winv = sb("winv", [128, DM])
        wgat = sb("wgat", [128, 2, NF])
        bP = sb("bP", [NP, D])
        bPos = sb("bPos", [NP, D])
        ln_s = sb("ln_s", [NP, 2, D])
        ln_b = sb("ln_b", [NP, 2, D])
        binv = sb("binv", [NP, DM])
        gvec = sb("gvec", [NP, 5, NF])
        b1r = sb("b1r", [NQ, 128])
        b1c = sb("b1c", [128, NQ])
        st6 = sb("st6", [NP, CH, 6])
        mv = sb("mv", [NP, NT, 2])
        std = sb("std", [NP, NT])
        mv5 = sb("mv5", [NP, CH, 2])
        behind = 2 * NX * FF + NQ * DM
        xn = region_a[0:NP, behind:behind + CH * DM].rearrange("p (k d) -> p k d", k=CH)
        RS = max(RB1, RB)
        region_s = sb("region_s", [128, RS * G * NP])
        xnT, eT = parts(region_s, 2 * CH * NP, CH * NP)
        e5, rden = parts(region_k[0:NP, :], CH * D, NT * H)
        e5 = e5.rearrange("p (k d) -> p k d", k=CH)
        rden = rden.rearrange("p (t h) -> p t h", t=NT)
        xnT = xnT.rearrange("p (k a n) -> p k a n", k=CH, a=2)
        eT = eT.rearrange("p (k n) -> p k n", k=CH)

        ix = sb("ix", [128, max(RB1, RB), G], i32)
        S = region_s[:, 0:RS * G * NP].rearrange("p (r j n) -> p r j n", r=RS, j=G)
        Sg = region_s[:, 0:RB * G * 64].bitcast(bf16).rearrange("p (r j n) -> p r j n", r=RB, j=G)
        ST = sb("ST", [NP, 2, G, 128])
        prod = region_a[:, behind + CH * DM:behind + CH * DM + G * D].rearrange("p (j d) -> p j d", j=G)
        logit = sb("logit", [128, G, H])
        att = sb("att", [128, 2, G, H])
        vals = sb("vals", [128, 2, G, DV])

        hn = sb("hn", [NP, NT, DR])
        part16 = hn[:, :, DG:DR].bitcast(bf16)
        ident_neg = sb("ident_neg", [128, 128], bf16)
        head_of = sb("head_of", [KR, HG])
        tile_of = sb("tile_of", [KR, G, NP], bf16)
        cols16 = sb("cols16", [128, KR], bf16)
        by_row = sb("by_row", [KR, HG, 128], bf16)
        pcol = sb("pcol", [128, 1])
        low2 = sb("low2", [KR, HG], i32)
        adm = sb("adm", [NP, NT, 2, HG])
        adm16 = sb("adm16", [NP, NT, NPART, 2 * HG], bf16)
        mx = sb("mx", [NP, NT, HG])
        selfe = sb("selfe", [NP, NT, HG])
        tmx = sb("tmx", [NP, GP, HG])
        rows = sb("rows", [128, RB, G, DR])
        msg = sb("msg", [128, 2, G, DG])
        msg16 = sb("msg16", [128, 2, G, NPART, DG], bf16)
        ST16 = ST[:, :, :, 0:64].bitcast(bf16)
        t16, t16b, score, rank, t4, e4, gate, t1, t1b, hid, ob, other, b2_sb = parts(
            region_k[:, :], NT * NF, NT * NF, NT * NX, NT * NX, NT * NX, NT * NX, NT * NX, NT, NT,
            2 * FC * NP, NX * DM, G * NP, NX * DM)
        hid = hid.rearrange("p (r f n) -> p r f n", r=2, f=FC)
        ob, b2_sb = (a[0:NP, :].rearrange("p (e n) -> p e n", e=NX) for a in (ob, b2_sb))
        other = other.bitcast(bf16).rearrange("p (r j n) -> p r j n", r=2, j=G)
        t16, t16b, score, rank, t4, e4, gate, t1, t1b = (
            a[0:NP, :] for a in (t16, t16b, score, rank, t4, e4, gate, t1, t1b))
        t16, t16b = (a.rearrange("p (t d) -> p t d", t=NT) for a in (t16, t16b))
        score, rank, t4, e4, gate = (a.rearrange("p (t d) -> p t d", t=NT) for a in (score, rank, t4, e4, gate))

        PS = ctx.enter_context(nc.psum_tensor("PS", [128, 8, 512], f32))
        bank = lambda i: PS[:, i, :]
        bank16 = lambda i: PS[:, i, :].bitcast(bf16)
        S16 = S[:, :, :, :].bitcast(bf16).rearrange("p r j (n two) -> p r j n two", two=2)[:, :, :, :, 1]

        s_lists, s_x, s_w, s_w12 = sem("s_lists"), sem("s_x"), sem("s_w"), sem("s_w12")
        s_iota = sem("s_iota")
        s_const = sem("s_const")
        s_phase = sem("s_phase")
        s_b1 = sem("s_b1")
        s_held_dve, s_held_pool, s_held_pe = sem("s_held_dve"), sem("s_held_pool"), sem("s_held_pe")
        s_dve = sem("s_dve")
        D_ = [{k: sem(f"s_{k}{i}") for k in ("cnt", "total", "tiles", "base", "past", "map", "lane", "hot", "part", "dealt", "all")}
              for i in range(2)]
        node_sems = ("var", "std", "emb_at", "e5", "eT", "eTc", "proj", "projc", "own")
        NS = [{k: sem(f"s_{k}{i}") for k in node_sems + of_stage}
              for i, of_stage in enumerate((("norm", "xT", "xTc", "emb", "embc", "kvst", "tab"), ("kvst", "tab"),
                                            ("norm", "xT", "xTc", "yvar", "ystd", "h", "hc")))]
        ES = [{k: sem(f"s_e{k}{i}") for k in ("S", "tr", "ST", "q", "clip", "exp", "vals", "agg", "sum", "slot", "own", "zero")}
              for i in range(2)]
        s_kv = [[sem(f"s_kv{i}_{r}") for r in range(RB1)] for i in range(2)]
        GS = {k: sem(f"s_g{k}") for k in ("other", "col", "row", "tr", "unit", "keep", "red", "slot", "own", "S", "tr2", "ST", "look", "e", "exp", "msg",
                                          "agg", "sum", "own2", "zero", "tab", "diff", "self", "var", "std", "s", "sexp")}
        s_rows = [sem(f"s_rows{r}") for r in range(RB)]
        MS = {k: sem(f"s_m{k}") for k in ("hid", "gelu", "out", "evac", "spill", "freed", "acc", "own")}
        s_back = [sem(f"s_back{k}") for k in range(CH)]
        s_out = sem("s_out")

        ENGINES = 5
        N_WEIGHTS = 7 + 2 * 5 + 5

        def meet(eng, n):
            eng.drain()
            eng.sem_inc(s_phase, 1)
            eng.wait_ge(s_phase, ENGINES * n)

        class Count:

            def __init__(self, eng, semaphore, before=0):
                self.eng, self.sem, self.before, self.n = eng, semaphore, before, 0

            def did(self, ins):
                ins.then_inc(self.sem, 1)
                self.n += 1

            def wait(self):
                self.eng.wait_ge(self.sem, self.before + self.n)

        CREDIT = 2
        slot_free = lambda c, k: c * CH + (k + 1 if k >= 2 else 2 - k)

        def work_of(it, k, i, per):
            first = 0 if per == 2 else FAST * NX
            return it * (R2 * per) + first + k * per + i, it * per + (FAST if per == 1 else 0) + (k * per + i) // NX, (k * per + i) % NX

        block = ctx.enter_context(nc.Block())

        @block.sync
        def _(sp):
            for i, (key, other) in enumerate(((src, dst), (ffn_edges[1, :], ffn_edges[0, :]))):
                j = (J1, J2)[i]
                sp.dma_start(key_i[i][:, :], key.rearrange("(p j) -> p j", j=j)).then_inc(s_lists, 16)
                sp.dma_start(pay_i[i][:, :], other.rearrange("(p j) -> p j", j=j)).then_inc(s_lists, 16)
            sp.dma_start(X[:, :, :], node(x)).then_inc(s_x, 16)
            weights = [(wP[:, :, :], W_P_w.rearrange("(k p) n -> p k n", k=2)), (winv[:, :], inv_w),
                       (wgat[:, :, :], W_gat.rearrange("(k p) n -> p k n", k=2)),
                       (bP[:, :], W_P_b[None, :].broadcast_to([NP, D])), (bPos[:, :], W_pos.broadcast_to([NP, D])),
                       (binv[:, :], inv_b[None, :].broadcast_to([NP, DM])),
                       (b1r[:, :], b1.rearrange("e (c p) -> (e c) p", p=128))]
            for l, (q, k, v, s, b) in enumerate(((q1, k1, v1, ln1_s, ln1_b), (q2, k2, v2, ln2_s, ln2_b))):
                weights += [(wqkv[:, l, m * D:(m + 1) * D], w) for m, w in enumerate((q, k, v))]
                weights += [(ln_s[:, l, :], s[None, :].broadcast_to([NP, D])), (ln_b[:, l, :], b[None, :].broadcast_to([NP, D]))]
            weights += [(gvec[:, i, :], v[None, :].broadcast_to([NP, NF])) for i, v in enumerate(
                (att_src.rearrange("h e -> (h e)"), att_dst.rearrange("h e -> (h e)"), b_gat, ln_gamma, ln_beta))]
            assert len(weights) == N_WEIGHTS
            for to, of in weights:
                sp.dma_start(to, of).then_inc(s_w, 16)
            for l in range(2):
                with sp.Fori(0, NCH) as c:
                    sp.wait_ge(NS[l]["kvst"], c + 1)
                    sp.dma_start(node(kv_tab)[:, ds(c * CH, CH), :], kv_st[:, ds(c * CH, CH), :]).then_inc(NS[l]["tab"], 16)
                sp.wait_ge(NS[l]["tab"], 16 * NCH)
                meet(sp, 1 + 2 * l)
                meet(sp, 2 + 2 * l)
            for e in range(NX):
                for k in range(2):
                    sp.dma_start(w1_sb[:, k, e * FF:(e + 1) * FF], W1[e, k * 128:(k + 1) * 128, :]).then_inc(s_w12, 16)
                sp.dma_start(w2_sb[:, e * FC:(e + 1) * FC, :], W2[e, :, :].rearrange("(c p) n -> p c n", p=128)).then_inc(s_w12, 16)
            sp.dma_start(b2_sb.rearrange("p e n -> p (e n)"), b2.rearrange("e n -> (e n)")[None, :].broadcast_to([NP, NX * DM])).then_inc(s_w12, 16)
            sp.wait_ge(GS["diff"], 1)
            sp.dma_start(node(gate_tab), hn[:, :, :]).then_inc(GS["tab"], 16)
            sp.wait_ge(GS["tab"], 16)
            meet(sp, 5)
            sp.sem_inc(MS["freed"], 1)
            with sp.Fori(0, NT) as t:
                sp.wait_ge(MS["evac"], (t + 1) * NX + 1)
                sp.dma_start(expert_tab[ds(t, 1), :, :].rearrange("a p n -> p (a n)"), ob.rearrange("p e n -> p (e n)")).then_inc(MS["spill"], 16)
                sp.wait_ge(MS["spill"], (t + 1) * 16)
                sp.sem_inc(MS["freed"], 1)
            meet(sp, 6)
            meet(sp, 7)
            with sp.Fori(0, NCH) as c:
                for k in range(CH):
                    sp.wait_ge(MS["acc"], c * CH + k + 1)
                    sp.dma_start(spilled[:, k, :, :].rearrange("p e n -> p (e n)"),
                                 expert_tab[ds(c * CH + k, 1), :, :].rearrange("a p n -> p (a n)")).then_inc(s_back[k], 16)

        @block.gpsimd
        def _(pool):
            nc.gpsimd.iota(column_i[:, :], pattern=[[1, T1]], base=0, channel_multiplier=0).then_inc(s_iota, 1)
            nc.gpsimd.iota(diff_i[:, :], pattern=[[-1, 128]], base=0, channel_multiplier=1).then_inc(s_iota, 1)
            for l in range(2):
                meet(pool, 1 + 2 * l)
                with pool.Fori(0, IT1) as it:
                    for r in range(R1):
                        pool.wait_ge(ES[l]["slot"], it * R1 + r + 1)
                        pool.sem_inc(s_held_pool, 1)
                        for j in range(G):
                            nc.gpsimd.indirect_dma_start(
                                out=kv[:, r % RB1, j, :], out_offset=None, in_=kv_tab,
                                in_offset=bass.IndirectOffsetOnAxis(ap=ix[:, r % RB1, j:j + 1], axis=0),
                            ).then_inc(s_kv[l][r % RB1], 16)
                meet(pool, 2 + 2 * l)
            meet(pool, 5)
            def gather_rows(k, n):
                pool.wait_ge(GS["slot"], n)
                pool.sem_inc(s_held_pool, 1)
                for j in range(G):
                    nc.gpsimd.indirect_dma_start(
                        out=rows[:, k, j, :], out_offset=None, in_=gate_tab,
                        in_offset=bass.IndirectOffsetOnAxis(ap=ix[:, k, j:j + 1], axis=0),
                    ).then_inc(s_rows[k], 16)

            with pool.Fori(0, IT2) as it:
                for k in range(R2):
                    gather_rows(k % RB, it * R2 + k + 1)
            gather_rows(NG2 % RB, NG2 + 1)
            meet(pool, 6)
            meet(pool, 7)

        @block.scalar
        def _(act):
            def keep_sums(act, tmap_, g, e, sums, first_bank, width):
                _, at = nc.values_load_multi_w_load_instructions(
                    tmap_[0:1, ds(g * GP, GP)], engines=[nc.scalar.engine], min_val=0, max_val=NT - 1,
                    skip_runtime_bounds_check_because="it counts up to 24 comparisons")
                for u in range(GP):
                    act.wait_ge(e["agg"], g * GP + u + 1 + 2 * GP)
                    nc.scalar.copy(flat(sums[:, ds(at[u], 1), :]), bank(first_bank + u)[0:NP, 0:width]).then_inc(e["sum"], 1)

            def node_stage(l):
                s = NS[l]
                tile = lambda c, k: c * CH + k
                for name in (("xTc", "eTc", "projc"), ("eTc", "projc"), ("xTc", "eTc", "hc"))[l]:
                    act.sem_inc(s[name], CREDIT)
                act.wait_ge(s["var"], 1)
                nc.scalar.activation(std[:, :], mv[:, :, 1], ACT.Sqrt).then_inc(s["std"], 1)

                def transposed_rows(c):
                    for k in range(CH):
                        act.wait_ge(s["xT"], tile(c, k) + 1 + CH)
                        nc.scalar.copy(xnT[:, k, :, :], bank(k % 2)[:, 0:2 * NP].rearrange("p (a n) -> p a n", a=2)).then_inc(s["xTc"], 1)

                def stage_embeddings(c):
                    act.wait_ge(s["emb_at"], (c + 1) * CH)
                    nc.scalar.copy(e5[:, :, :], EMB[:, ds(c * CH, CH), :]).then_inc(s["e5"], 1)

                def transposed_embeddings(c):
                    for k in range(CH):
                        act.wait_ge(s["eT"], tile(c, k) + 1)
                        nc.scalar.copy(eT[:, k, :], bank(4 + k % 2)[:, 0:NP]).then_inc(s["eTc"], 1)

                def keep_projected(c):
                    if l == 2:
                        return
                    for k in range(CH):
                        act.wait_ge(s["proj"], tile(c, k) + 1)
                        nc.scalar.copy(flat(Q[:, ds(tile(c, k), 1), :]), bank(6 + k % 2)[0:NP, 0:D])
                        nc.scalar.copy(flat(kv_st[:, ds(tile(c, k), 1), :]), bank(6 + k % 2)[0:NP, D:3 * D]).then_inc(s["projc"], 1)
                    act.wait_ge(s["projc"], (c + 1) * CH + CREDIT)
                    act.sem_inc(s["kvst"], 1)

                if l == 0:
                    transposed_rows(0)
                stage_embeddings(0)
                with act.Fori(0, NCH - 1) as c:
                    if l == 0:
                        transposed_rows(c + 1)
                    transposed_embeddings(c)
                    if l > 0:
                        stage_embeddings(c + 1)
                    keep_projected(c)
                    if l == 0:
                        stage_embeddings(c + 1)
                transposed_embeddings(NCH - 1)
                keep_projected(NCH - 1)
                if l == 2:
                    act.wait_ge(s["yvar"], 1)
                    nc.scalar.activation(std[:, :], mv[:, :, 1], ACT.Sqrt).then_inc(s["ystd"], 1)
                    with act.Fori(0, NCH) as c:
                        transposed_rows(c)
                        act.wait_ge(s["xTc"], (c + 1) * CH + CREDIT)
                        nc.scalar.copy(yT[:, :, ds(c * CH * NP, CH * NP)].rearrange("p a (k n) -> p k a n", k=CH), xnT[:, :, :, :])
                        for k in range(CH):
                            act.wait_ge(s["h"], tile(c, k) + 1)
                            nc.scalar.copy(flat(hn[:, ds(tile(c, k), 1), 0:NF]), bank(2 + k % 2)[0:NP, 0:NF]).then_inc(s["hc"], 1)

            with act.Fori(0, J1 // (2 * U)) as it:
                for par in range(2):
                    act.wait_ge(D_[0]["lane"], it * 2 + par + 1)
                    for u in range(U):
                        last = nc.scalar.activation(hot_part[0:P1, par, u, :], at_lane[0:P1, par, :, u], ACT.Copy,
                                                    scale=part_of[0][:, ds((it * 2 + par) * U + u, 1)])
                    last.then_inc(D_[0]["part"], 1)

            def deal_beside(it, r):
                i, third = r // SPREAD, r % SPREAD
                if i == STEPS or third == 0:
                    return
                step = it * STEPS + i
                act.wait_ge(D_[1]["lane"], step + 1)
                for u in range(U // 2 * (third - 1), U // 2 * third):
                    last = nc.scalar.activation(hot_part2[0:P2, i % 2, u, :], at_lane2[0:P2, i % 2, :, u], ACT.Copy,
                                                scale=part_of[1][:, ds(step * U + u, 1)])
                if third == 2:
                    last.then_inc(D_[1]["part"], 1)

            for l in range(2):
                node_stage(l)
                meet(act, 1 + 2 * l)
                e = ES[l]

                def keep_transposed(par, n):
                    act.wait_ge(e["tr"], n)
                    nc.scalar.copy(ST[:, par, :, :].rearrange("p j n -> p (j n)"), bank16(par)[0:NP, 0:G * 128]).then_inc(e["ST"], 1)

                act.sem_inc(e["sum"], 1)
                keep_transposed(0, 1)
                keep_transposed(1, 2)
                with act.Fori(0, IT1) as it:
                    for r in range(R1):
                        g = it * R1 + r
                        act.wait_ge(e["clip"], g + 1)
                        nc.scalar.activation(vals[:, r % 2, :, D:DV], att[:, r % 2, :, :], ACT.Exp).then_inc(e["exp"], 1)
                        if l == 0:
                            deal_beside(it, r)
                        keep_transposed(r % 2, g + 3)
                        keep_sums(act, tmap[0], g, e, AGG, 4, DV)
                meet(act, 2 + 2 * l)
            node_stage(2)
            meet(act, 5)
            act.sem_inc(MS["gelu"], 1)
            act.sem_inc(MS["evac"], 1)

            def gelu(m, ex):
                act.wait_ge(MS["hid"], m + 1)
                for f in range(FC):
                    last = nc.scalar.activation(hid[:, ex % 2, f, :], bank(6)[:, f * NP:(f + 1) * NP], ACT.Gelu, bias=b1c[:, ex * FC + f:ex * FC + f + 1])
                last.then_inc(MS["gelu"], 1)

            def keep_rows(k, times, group):
                act.wait_ge(s_rows[k], times * 16 * G)
                nc.scalar.copy(cols16[:, :].rearrange("p (j d) -> p j d", j=G), rows[:, k, :, DG:DR].bitcast(bf16)).then_inc(GS["col"], 1)
                nc.scalar.copy(GAT[:, ds(group * G, G), :], rows[:, k, :, 0:DG]).then_inc(GS["keep"], 1)

            def by_head_rows(n):
                act.wait_ge(GS["tr"], n)
                for h in range(HG):
                    last = nc.scalar.activation(by_row[:, h, :], bank16(4)[0:KR, 0:128], ACT.Copy, scale=head_of[:, h:h + 1])
                last.then_inc(GS["row"], 1)

            keep_rows(0, 1, 0)
            by_head_rows(1)
            for lo, hi, per in ((0, FAST, 2), (FAST, IT2, 1)):
                with act.Fori(lo, hi) as it:
                    for k in range(R2):
                        g = it * R2 + k
                        for i in range(per):
                            m, t, ex = work_of(it, k, i, per)
                            gelu(m, ex)
                            if i == 0:
                                keep_rows((k + 1) % RB, it * (R2 // RB) + (k + 1) // RB + 1, g + 1)
                                by_head_rows(g + 2)
            meet(act, 6)
            act.wait_ge(GS["diff"], 2)
            nc.scalar.activation(selfe[:, :, :], selfe[:, :, :], ACT.Exp).then_inc(GS["self"], 1)

            def keep_transposed2(par, n):
                act.wait_ge(GS["tr2"], n)
                nc.scalar.copy(ST16[:, par, :, :], bank16(par)[0:NP, 0:G * 128].rearrange("p (j n) -> p j n", j=G)).then_inc(GS["ST"], 1)

            def weights2(par, n):
                act.wait_ge(GS["e"], n)
                nc.scalar.activation(msg[:, par, :, NF:DG], att[:, par, :, 0:HG], ACT.Exp).then_inc(GS["exp"], 1)

            act.sem_inc(GS["sum"], 1)
            keep_transposed2(0, 1)
            keep_transposed2(1, 2)
            weights2(0, 1)
            with act.Fori(0, IT2) as it:
                for k in range(R2):
                    g = it * R2 + k
                    keep_transposed2(k % 2, g + 3)
                    weights2((k + 1) % 2, g + 2)
                    keep_sums(act, tmap[1], g, GS, AGG[:, :, 0:DG], 4, DG)
            act.wait_ge(GS["var"], 1)
            nc.scalar.activation(t1b[:, :], t1[:, :], ACT.Sqrt).then_inc(GS["std"], 1)
            act.wait_ge(GS["s"], 1)
            nc.scalar.activation(e4[:, :, :], t4[:, :, :], ACT.Exp).then_inc(GS["sexp"], 1)
            meet(act, 7)
            with act.Fori(0, NCH) as c:
                act.wait_ge(MS["acc"], (c + 2) * CH)
                act.dma_start(node(out)[:, ds(c * CH, CH), :], X[:, ds(c * CH, CH), :]).then_inc(s_out, 16)
            act.wait_ge(s_out, 16 * NCH)

        @block.tensor
        def _(pe):
            def count_tiles(i):
                P, T, s = (P1, P2)[i], (T1, T2)[i], D_[i]
                pe.wait_ge(s["cnt"], 1)
                nc.tensor.matmul(bank(4)[0:NT, 0:1], cnt[0:P, :], ones[0:P, 0:1], start=True, stop=True).then_inc(s["total"], 1)
                pe.wait_ge(s["tiles"], 1)
                nc.tensor.matmul(bank(5)[0:NT, 0:1], upto[0:NT, 0:NT], tiles[:, :], start=True, stop=True)
                nc.tensor.matmul(bank(6)[0:P, 0:NT], before[0:P, 0:P], cnt[0:P, :], start=True, stop=False)
                nc.tensor.matmul(bank(6)[0:P, 0:NT], tiles_b[:, 0:P], before256[0:NT, :], start=False, stop=True).then_inc(s["base"], 1)
                pe.wait_ge(s["past"], 1)
                nc.tensor.matmul(bank(7)[0:1, 0:T // 2], ones[0:NT - 1, 0:1], past[:, 0:T // 2], start=True, stop=True).then_inc(s["map"], 1)

            def open_slots(i, to):
                for a in to:
                    nc.tensor.matmul(a, zeros16[:, :], iota_t[:, 0:a.shape[1]], start=True, stop=False)

            def close_slots(i, to):
                for a in to:
                    last = nc.tensor.matmul(a, zeros16[:, :], iota_t[:, 0:a.shape[1]], start=False, stop=True)
                last.then_inc(D_[i]["all"], 1)

            def deal_step(i, to, other_, part_, hotT_, step):
                pe.wait_ge(D_[i]["hot"], step + 1)
                pe.wait_ge(D_[i]["part"], step + 1)
                for u in range(U):
                    nc.tensor.matmul(to[0], other_[:, :, u], hotT_[:, u, :], start=False, stop=False)
                    last = nc.tensor.matmul(to[1], part_[:, u, :], hotT_[:, u, :], start=False, stop=False)
                last.then_inc(D_[i]["dealt"], 1)

            slots1 = [bank(i)[:, 0:T1] for i in (0, 1)]
            slots2 = [bank(i)[:, 0:T2] for i in (6, 7)]

            def node_stage(l):
                s = NS[l]

                def transposed_rows(c):
                    for k in range(CH):
                        pe.wait_ge(s["norm"], c * CH + k + 1)
                        pe.wait_ge(s["xTc"], slot_free(c, k))
                        for a in range(2):
                            last = nc.tensor.transpose(bank(k % 2)[:, a * NP:(a + 1) * NP], xn[:, k, a * 128:(a + 1) * 128], ident[0:NP, 0:NP])
                        last.then_inc(s["xT"], 1)

                def from_rows(c, w, width, done, taken):
                    for k in range(CH):
                        pe.wait_ge(s["xTc"], c * CH + k + 1 + CREDIT)
                        pe.wait_ge(s[taken], slot_free(c, k))
                        for a in range(2):
                            last = nc.tensor.matmul(bank(2 + k % 2)[0:NP, 0:width], xnT[:, k, a, :], w[:, a, :], start=(a == 0), stop=(a == 1))
                        last.then_inc(s[done], 1)

                def transposed_embeddings(c):
                    pe.wait_ge(s["e5"], c + 1)
                    for k in range(CH):
                        pe.wait_ge(s["eTc"], slot_free(c, k))
                        nc.tensor.transpose(bank(4 + k % 2)[:, 0:NP], e5[:, k, :], ident[0:NP, 0:NP]).then_inc(s["eT"], 1)

                def project(c):
                    w = wqkv[:, l, :] if l < 2 else winv[:, :]
                    for k in range(CH):
                        pe.wait_ge(s["eTc"], c * CH + k + 1 + CREDIT)
                        pe.wait_ge(s["projc"], slot_free(c, k))
                        nc.tensor.matmul(bank(6 + k % 2)[0:NP, 0:w.shape[1]], eT[:, k, :], w, start=True, stop=True).then_inc(s["proj"], 1)

                if l != 1:
                    pe.sem_inc(s["xT"], CH)
                if l == 0:
                    transposed_rows(0)
                    from_rows(0, wP, D, "emb", "embc")
                with pe.Fori(0, NCH - 1) as c:
                    if l == 0:
                        transposed_rows(c + 1)
                    transposed_embeddings(c)
                    if l == 0:
                        from_rows(c + 1, wP, D, "emb", "embc")
                    project(c)
                transposed_embeddings(NCH - 1)
                project(NCH - 1)
                if l == 2:
                    with pe.Fori(0, NCH) as c:
                        transposed_rows(c)
                        from_rows(c, wgat, NF, "h", "hc")

            def node_tiles(tmap_, first, n):
                return nc.values_load_multi_w_load_instructions(
                    tmap_[0:1, ds(first, n)], engines=[nc.tensor.engine], min_val=0, max_val=NT - 1,
                    skip_runtime_bounds_check_because="it counts up to 24 comparisons")[1]

            def transposed_S(ready, done, S_, par, n):
                pe.wait_ge(ready, n)
                for j in range(G):
                    last = nc.tensor.transpose(bank16(par)[0:S_.shape[2], j * 128:(j + 1) * 128], S_[:, j, :], ident16[:, :])
                last.then_inc(done, 1)

            def add_up(e, ready, g, at, stationary, values, sums, width, units=range(GP)):
                pe.wait_ge(ready, g + 1)
                for u in units:
                    b = bank(4 + u)[0:NP, 0:width]
                    for j in (2 * u, 2 * u + 1):
                        for i, part in enumerate(values(j)):
                            nc.tensor.matmul(bank(4 + u)[0:stationary.shape[2], 0:width], stationary[:, j, :], part, start=(j == 2 * u and i == 0), stop=False)
                    pe.wait_ge(e["sum"], g * GP + u + 1)
                    nc.tensor.matmul(b, ident[0:NP, 0:NP], flat(sums[:, ds(at[u], 1), :]), start=False, stop=True).then_inc(e["agg"], 1)

            pe.wait_ge(s_const, 1)
            count_tiles(0)
            pe.sem_inc(D_[0]["dealt"], 2)
            open_slots(0, slots1)
            with pe.Fori(0, J1 // (2 * U)) as it:
                for par in range(2):
                    deal_step(0, slots1, hot_other[0:P1, par, :, :], hot_part[0:P1, par, :, :], hotT[0:P1, par, :, 0:T1], it * 2 + par)
            close_slots(0, slots1)
            count_tiles(1)
            pe.wait_ge(s_w, 16 * N_WEIGHTS)
            nc.tensor.transpose(bank(4)[:, 0:NQ], b1r[:, :], ident[0:NQ, 0:NQ]).then_inc(s_b1, 1)
            for l in range(2):
                node_stage(l)
                meet(pe, 1 + 2 * l)
                e = ES[l]

                def fetch_q(par, at, n):
                    pe.wait_ge(e["ST"], n)
                    for j in range(G):
                        last = nc.tensor.matmul(bank(2 + par)[:, j * 128:(j + 1) * 128], ST[:, par, j, :], flat(Q[:, ds(at[j // 2], 1), :]), start=True, stop=True)
                    last.then_inc(e["q"], 1)

                pe.sem_inc(e["agg"], 2 * GP)
                pe.wait_ge(e["zero"], 1)
                if l == 0:
                    pe.sem_inc(D_[1]["dealt"], 1)
                    open_slots(1, slots2)
                transposed_S(e["S"], e["tr"], S16[:, 0, :, :], 0, 1)
                transposed_S(e["S"], e["tr"], S16[:, 1, :, :], 1, 2)
                fetch_q(0, node_tiles(tmap[0], 0, GP), 1)
                with pe.Fori(0, IT1) as it:
                    for r in range(R1):
                        g = it * R1 + r
                        at = node_tiles(tmap[0], g * GP, 2 * GP)
                        transposed_S(e["S"], e["tr"], S16[:, (r + 2) % RB1, :, :], r % 2, g + 3)
                        fetch_q((r + 1) % 2, at[GP:], g + 2)
                        add_up(e, e["vals"], g, at, S[:, r % RB1, :, :], lambda j: [vals[:, r % 2, j, :]], AGG, DV)
                        if l == 0 and r // SPREAD < STEPS and r % SPREAD == SPREAD - 1:
                            half = r // SPREAD % 2
                            deal_step(1, slots2, hot_other2[0:P2, half, :, :], hot_part2[0:P2, half, :, :], hotT2[0:P2, half, :, :], it * STEPS + r // SPREAD)
                if l == 0:
                    close_slots(1, slots2)
                meet(pe, 2 + 2 * l)
            node_stage(2)
            meet(pe, 5)
            pe.wait_ge(s_w12, 16 * (3 * NX + 1))

            def hidden(m, t, ex):
                pe.wait_ge(MS["gelu"], m + 1)
                for f in range(FC):
                    q = ex * FC + f
                    for a in range(2):
                        last = nc.tensor.matmul(bank(6)[:, f * NP:(f + 1) * NP], w1_sb[:, a, q * 128:(q + 1) * 128], yT[:, a, ds(t * NP, NP)],
                                                start=(a == 0), stop=(a == 1))
                last.then_inc(MS["hid"], 1)

            def back(m, ex):
                pe.wait_ge(MS["evac"], m + 1)
                pe.wait_ge(MS["gelu"], m + 2)
                for f in range(FC):
                    last = nc.tensor.matmul(bank(7)[0:NP, 0:DM], hid[:, ex % 2, f, :], w2_sb[:, ex * FC + f, :], start=(f == 0), stop=(f == FC - 1))
                last.then_inc(MS["out"], 1)

            def transposed_parts(n):
                pe.wait_ge(GS["col"], n)
                pe.sem_inc(s_held_pe, 1)
                nc.tensor.transpose(bank16(4)[0:KR, 0:128], cols16[:, :], ident16[:, :]).then_inc(GS["tr"], 1)

            transposed_parts(1)
            for lo, hi, per in ((0, FAST, 2), (FAST, IT2, 1)):
                with pe.Fori(lo, hi) as it:
                    for k in range(R2):
                        g = it * R2 + k
                        m, t, ex = work_of(it, k, 0, per)
                        hidden(m, t, ex)
                        pe.wait_ge(GS["other"], g + 1)
                        pe.wait_ge(GS["row"], g + 1)
                        for u in range(GP):
                            pe.wait_ge(GS["red"], g * GP + u + 1)
                            for j in (2 * u, 2 * u + 1):
                                for b in range(2):
                                    to = bank(2 * u + b)[0:NP, :].rearrange("p (h n) -> p h n", h=2)[:, :, (j % 2) * 128:(j % 2 + 1) * 128]
                                    nc.tensor.matmul(to, other[:, k % 2, j, :], ident_neg[:, :][:, None, :].broadcast_to([128, 2, 128]), start=True, stop=False)
                                    last = nc.tensor.matmul(to, tile_of[:, j, :], by_row[:, 2 * b:2 * b + 2, :], start=False, stop=True)
                            last.then_inc(GS["unit"], 1)
                        transposed_parts(g + 2)
                        if per == 2:
                            m1, t1_, ex1 = work_of(it, k, 1, per)
                            hidden(m1, t1_, ex1)
                        back(m, ex)
                        if per == 2:
                            back(m1, ex1)
            meet(pe, 6)

            def look_up(par, at, n):
                pe.wait_ge(GS["ST"], n)
                for j in range(G):
                    for i in range(NPART):
                        last = nc.tensor.matmul(bank(2 + par)[:, j * 2 * HG:(j + 1) * 2 * HG], ST16[:, par, j, :],
                                                adm16[:, ds(at[j // 2], 1), i, :].rearrange("p a h -> p (a h)"), start=(i == 0), stop=(i == NPART - 1))
                last.then_inc(GS["look"], 1)

            pe.sem_inc(GS["agg"], 2 * GP)
            pe.wait_ge(GS["zero"], 1)
            transposed_S(GS["S"], GS["tr2"], Sg[:, 0, :, :], 0, 1)
            transposed_S(GS["S"], GS["tr2"], Sg[:, 1, :, :], 1, 2)
            at = node_tiles(tmap[1], 0, 2 * GP)
            look_up(0, at, 1)
            look_up(1, at[GP:], 2)
            with pe.Fori(0, IT2) as it:
                for k in range(R2):
                    g = it * R2 + k
                    transposed_S(GS["S"], GS["tr2"], Sg[:, (k + 2) % RB, :, :], k % 2, g + 3)
                    at = node_tiles(tmap[1], g * GP, 3 * GP)
                    parts_of = lambda j: [msg16[:, k % 2, j, i, :] for i in range(NPART)]
                    add_up(GS, GS["msg"], g, at, Sg[:, k % RB, :, :], parts_of, AGG[:, :, 0:DG], DG, range(0, 1))
                    look_up(k % 2, at[2 * GP:], g + 3)
                    add_up(GS, GS["msg"], g, at, Sg[:, k % RB, :, :], parts_of, AGG[:, :, 0:DG], DG, range(1, GP))
            meet(pe, 7)

        @block.vector
        def _(dve):
            v = nc.vector
            own = Count(dve, s_dve)

            dve.wait_ge(s_iota, 2)
            v.tensor_copy(iota_t[:, :], column_i[:, :])
            v.tensor_copy(lane_of[:, :, :], column_i[:, 0:128][:, :, None].broadcast_to([128, 128, U]))
            v.tensor_copy(iota_128[:, :], column_i[:, 0:128])
            v.tensor_scalar(before[:, :], diff_i[:, :], 0.0, None, ALU.is_lt)
            v.tensor_scalar(before256[:, :], diff_i[:, 0:NT], 0.0, float(PAIR), ALU.is_lt, ALU.mult)
            v.tensor_scalar(ident16[:, :], diff_i[:, :], 0.0, None, ALU.is_equal)
            v.tensor_scalar(upto[:, :], diff_i[:, :], 0.0, None, ALU.is_le)
            v.tensor_scalar(ident[:, :], diff_i[:, :], 0.0, None, ALU.is_equal)
            v.tensor_scalar(ident_neg[:, :], diff_i[:, :], 0.0, -BIG, ALU.is_equal, ALU.mult)
            own.did(v.tensor_scalar(low2[:, :], diff_i[0:KR, 0:HG], HG - 1, None, ALU.bitwise_and))
            own.did(v.tensor_copy(pcol[:, :], diff_i[:, 0:1]))
            own.wait()
            v.tensor_scalar(head_of[:, :], low2[:, :], 0.0, None, ALU.is_equal)
            for j in range(G):
                row = pcol[0:KR, :].broadcast_to([KR, NP])
                own.did(v.tensor_scalar(tile_of[:, j, :], row, float(j * KR // G), None, ALU.is_ge))
                own.wait()
                own.did(v.scalar_tensor_tensor(tile_of[:, j, :], row, float((j + 1) * KR // G), tile_of[:, j, :], ALU.is_lt, ALU.mult))
            v.memset(zeros16[:, :], 0.0)
            v.memset(cend[:, 0:1], 0.0)
            for i, T in enumerate((T1, T2)):
                v.memset(tmap[i][:, :], 0)
                v.memset(idx[i][:, T:], 0)
                v.memset(loc[i][:, T:], -1.0)
            v.memset(ones[:, :], 1.0).then_inc(s_const, 1)
            dve.wait_ge(s_const, 1)

            def rint(ap):
                own.wait()
                own.did(v.tensor_scalar(ap, ap, RND, RND, ALU.add, ALU.subtract))
                own.wait()

            def hot_lanes(i, to, lane_of_, step):
                v.tensor_tensor(to, lane_of_, over_lanes(i, lane[i], step), ALU.is_equal).then_inc(D_[i]["lane"], 1)

            def hot_tiles(i, to, step, u):
                P, T = (P1, P2)[i], (T1, T2)[i]
                v.tensor_scalar(to, iota_t[0:P, 0:T], tcol[i][:, ds(step * U + u, 1)], None, ALU.is_equal)

            def hot_others(i, to, at_lane_, step):
                dve.wait_ge(D_[i]["lane"], step + 1)
                v.tensor_tensor(to, at_lane_, over_lanes(i, other_end[i], step), ALU.mult).then_inc(D_[i]["hot"], 1)

            def over_lanes(i, a, step):
                return a[:, ds(step * U, U)][:, None, :].broadcast_to([(P1, P2)[i], 128, U])

            def keep_slots(i, banks):
                T = (T1, T2)[i]
                dve.wait_ge(D_[i]["all"], 1)
                own.did(v.tensor_scalar(idx[i][:, 0:T], bank(banks[0])[:, 0:T], float(MID), None, ALU.add))
                own.did(v.tensor_scalar(loc[i][:, 0:T], bank(banks[1])[:, 0:T], -1.0, None, ALU.add))

            dve.wait_ge(s_lists, 64)
            for i in range(2):
                P, J, T, s = (P1, P2)[i], (J1, J2)[i], (T1, T2)[i], D_[i]
                key, p_, c_, t_ = pos[0:P, 0:J], part_of[i][:, 0:J], tcol[i][:, 0:J], kt[0:P, :].bitcast(f16)[:, 0:J]
                lane_, other_ = lane[i][:, 0:J], other_end[i][:, 0:J]
                hot_p = hot[0:P, 0:NT * J]
                cnt_p = counts[0:P, 0:NT * J]
                by_tile = lambda a: a.rearrange("p (b j) -> p b j", b=NT)
                own.did(v.tensor_copy(key, key_i[i][:, :]))
                own.wait()
                own.did(v.tensor_scalar(p_, key, -float(NT // 2), 1.0 / NT, ALU.add, ALU.mult))
                rint(p_)
                own.did(v.scalar_tensor_tensor(t_, p_, -float(NT), key, ALU.mult, ALU.add))
                own.wait()
                for b in range(NT):
                    own.did(v.tensor_scalar(hot_p[:, b * J:(b + 1) * J], t_, float(b), None, ALU.is_equal))
                own.wait()
                own.did(v.tensor_tensor_scan(cnt_p, hot_p, hot_p, 0.0, ALU.add, ALU.max))
                own.wait()
                own.did(v.tensor_copy(cend[0:P, 1:NT + 1], by_tile(cnt_p)[:, :, J - 1]))
                own.wait()
                v.tensor_tensor(cnt[0:P, :], cend[0:P, 1:NT + 1], cend[0:P, 0:NT], ALU.subtract).then_inc(s["cnt"], 1)
                dve.wait_ge(s["total"], 1)
                own.did(v.tensor_scalar(tiles[:, :], bank(4)[0:NT, 0:1], (PAIR - 1) / 2, 1.0 / PAIR, ALU.add, ALU.mult))
                rint(tiles[:, :])
                v.tensor_scalar(tiles_b[:, :], ones[0:NT, :], tiles[:, 0:1], None, ALU.mult).then_inc(s["tiles"], 1)
                dve.wait_ge(s["base"], 1)
                own.did(v.tensor_copy(ends[:, :], bank(5)[0:NT, 0:1]))
                own.did(v.scalar_tensor_tensor(base[0:P, :], bank(6)[0:P, 0:NT], -1.0, cend[0:P, 0:NT], ALU.add, ALU.subtract))
                own.wait()
                v.tensor_scalar(past[:, 0:T // 2], iota_t[0:NT - 1, 0:T // 2], ends[0:NT - 1, 0:1], None, ALU.is_ge).then_inc(s["past"], 1)
                for b in range(NT):
                    of_tile = slice(b * J, (b + 1) * J)
                    own.did(v.scalar_tensor_tensor(cnt_p[:, of_tile], cnt_p[:, of_tile], base[0:P, b:b + 1], hot_p[:, of_tile], ALU.add, ALU.mult))
                own.wait()
                own.did(v.tensor_reduce(key, cnt_p.rearrange("p (b j) -> p j b", b=NT), AX.X, ALU.add))
                own.wait()
                own.did(v.tensor_scalar(c_, key, -63.5, 1.0 / 128, ALU.add, ALU.mult))
                rint(c_)
                own.did(v.scalar_tensor_tensor(lane_, c_, -128.0, key, ALU.mult, ALU.add))
                own.did(v.tensor_scalar(other_, pay_i[i][:, :], -float(MID), None, ALU.add))
                own.did(v.tensor_scalar(p_, p_, 1.0, None, ALU.add))
                dve.wait_ge(s["map"], 1)
                own.did(v.tensor_copy(tmap[i][0:1, 0:T // 2], bank(7)[0:1, 0:T // 2]))
                own.wait()
                if i == 0:
                    with dve.Fori(0, J1 // (2 * U)) as it:
                        for par in range(2):
                            step = it * 2 + par
                            dve.wait_ge(s["dealt"], step + 1)
                            hot_lanes(0, at_lane[0:P1, par, :, :], lane_of[0:P1, :, :], step)
                            for u in range(U):
                                hot_tiles(0, hotT[0:P1, par, u, 0:T1], step, u)
                            hot_others(0, hot_other[0:P1, par, :, :], at_lane[0:P1, par, :, :], step)
                    keep_slots(0, (0, 1))
                else:
                    if JD > J2:
                        own.did(v.memset(tcol[1][:, J2:], -1.0))
                        own.did(v.memset(part_of[1][:, J2:], 0.0))
                        own.did(v.memset(lane[1][:, J2:], 0.0))
                        own.did(v.memset(other_end[1][:, J2:], 0.0))
                    own.did(v.tensor_copy(lane_of2[:, :, :], lane_of[:, :, :]))
            own.wait()

            def statistics(o, c, source):
                o.wait()
                dve.sem_inc(s_held_dve, 1)
                for k in range(CH):
                    o.did(v.bn_stats(st6[:, k, :], source(c * CH + k)))
                o.wait()
                dve.sem_inc(s_held_dve, 1)
                for k in range(CH):
                    o.did(v.bn_aggr(mv5[:, k, :], st6[:, k, :]))
                o.wait()
                o.did(v.tensor_copy(mv[:, ds(c * CH, CH), :], mv5[:, :, :]))

            def deviations(s, var, std_done, done, eps):
                dve.wait_ge(s["own"], done)
                v.tensor_scalar(mv[:, :, 1], mv[:, :, 1], eps, None, ALU.add).then_inc(s[var], 1)
                dve.wait_ge(s[std_done], 1)
                own.did(v.reciprocal(std[:, :], std[:, :]))
                own.wait()

            def normalized(to, source, t):
                return v.tensor_scalar(to, source, flat(mv[:, ds(t, 1), 0:1]), std[:, ds(t, 1)], ALU.subtract, ALU.mult)

            x_tile = lambda t: flat(X[:, ds(t, 1), :])
            emb_tile = lambda t: flat(EMB[:, ds(t, 1), :])

            def node_stage(l):
                s = NS[l]
                A, B = 2 * CH + 1, CH + 1
                dve.sem_inc(s["own"], 1)
                if l == 0:
                    dve.sem_inc(s["embc"], CREDIT)
                if l == 0:
                    with dve.Fori(0, NCH) as c:
                        statistics(Count(dve, s["own"], c * A + 1), c, x_tile)
                    deviations(s, "var", "std", NCH * A + 1, 1e-5)
                    with dve.Fori(0, NCH) as c:
                        for k in range(CH):
                            dve.wait_ge(s["xT"], c * CH + k + 1)
                            normalized(xn[:, k, :], x_tile(c * CH + k), c * CH + k).then_inc(s["norm"], 1)
                        for k in range(CH):
                            dve.wait_ge(s["emb"], c * CH + k + 1)
                            v.tensor_tensor(emb_tile(c * CH + k), bank(2 + k % 2)[0:NP, 0:D], bP[:, :], ALU.add).then_inc(s["embc"], 1)
                        dve.wait_ge(s["embc"], (c + 1) * CH + CREDIT)
                        dve.sem_inc(s["emb_at"], CH)
                    return
                own.did(v.tensor_scalar(rden[:, :, :], AGG[:, :, D:DV], 1e-8, None, ALU.add))
                own.wait()
                own.did(v.reciprocal(rden[:, :, :], rden[:, :, :]))
                own.wait()
                agg = AGG[:, :, 0:D]
                by_head_ = agg.rearrange("p t (h d) -> p t h d", h=H)
                own.did(v.tensor_tensor(by_head_, by_head_, rden[:, :, :][:, :, :, None].broadcast_to([NP, NT, H, HD]), ALU.mult))
                own.wait()
                own.did(v.tensor_tensor(EMB[:, :, :], agg, EMB[:, :, :], ALU.add))
                own.wait()
                with dve.Fori(0, NCH) as c:
                    statistics(Count(dve, s["own"], c * A + 1), c, emb_tile)
                deviations(s, "var", "std", NCH * A + 1, 1e-6)

                def embeddings(o, c):
                    emb = EMB[:, ds(c * CH, CH), :]
                    for k in range(CH):
                        o.did(normalized(emb_tile(c * CH + k), emb_tile(c * CH + k), c * CH + k))
                    o.wait()
                    o.did(v.tensor_tensor(emb, emb, ln_s[:, l - 1, :][:, None, :].broadcast_to([NP, CH, D]), ALU.mult))
                    o.wait()
                    v.tensor_tensor(emb, emb, ln_b[:, l - 1, :][:, None, :].broadcast_to([NP, CH, D]), ALU.add).then_inc(s["emb_at"], CH)

                def add_back(c):
                    for k in range(CH):
                        dve.wait_ge(s["proj"], c * CH + k + 1)
                        v.tensor_tensor(x_tile(c * CH + k), bank(6 + k % 2)[0:NP, 0:DM], x_tile(c * CH + k), ALU.add).then_inc(s["projc"], 1)

                before_B = NCH * A + 1
                if l == 1:
                    with dve.Fori(0, NCH) as c:
                        embeddings(Count(dve, s["own"], before_B + c * B), c)
                    own.did(v.tensor_tensor(X[:, :, :], X[:, :, :], binv[:, :][:, None, :].broadcast_to([NP, NT, DM]), ALU.add))
                    return
                dve.sem_inc(s["projc"], CREDIT)
                embeddings(Count(dve, s["own"], before_B), 0)
                with dve.Fori(0, NCH - 1) as c:
                    embeddings(Count(dve, s["own"], before_B + B + c * B), c + 1)
                    add_back(c)
                add_back(NCH - 1)
                dve.wait_ge(s["projc"], NT + CREDIT)
                before_C = before_B + NCH * B
                with dve.Fori(0, NCH) as c:
                    statistics(Count(dve, s["own"], before_C + c * A), c, x_tile)
                deviations(s, "yvar", "ystd", before_C + NCH * A, 1e-5)
                with dve.Fori(0, NCH) as c:
                    for k in range(CH):
                        dve.wait_ge(s["xT"], c * CH + k + 1)
                        normalized(xn[:, k, :], x_tile(c * CH + k), c * CH + k).then_inc(s["norm"], 1)

            dve.wait_ge(s_x, 16)
            dve.wait_ge(s_w, 16 * N_WEIGHTS)
            own.did(v.tensor_tensor(bP[:, :], bP[:, :], bPos[:, :], ALU.add))
            dve.wait_ge(s_b1, 1)
            own.did(v.tensor_copy(b1c[:, :], bank(4)[:, 0:NQ]))
            own.wait()
            for l in range(2):
                node_stage(l)
                e = ES[l]

                def build_S(par, group):
                    v.tensor_tensor(S[:, par, :, :], iota_n[:, :][:, None, :].broadcast_to([128, G, NP]),
                                    loc[0][:, ds(group * G, G)][:, :, None].broadcast_to([128, G, NP]), ALU.is_equal).then_inc(e["S"], 1)

                def stage_indices(r, group):
                    v.tensor_copy(ix[:, r, :], idx[0][:, ds(group * G, G)]).then_inc(e["slot"], 1)

                meet(dve, 1 + 2 * l)
                v.memset(AGG[:, :, :], 0.0).then_inc(e["zero"], 1)
                for r in range(RB1):
                    stage_indices(r, r)
                build_S(0, 0)
                build_S(1, 1)
                PER = 2
                with dve.Fori(0, IT1) as it:
                    for r in range(R1):
                        g, par, rb = it * R1 + r, r % 2, r % RB1
                        o = Count(dve, e["own"], g * PER)
                        beside = l == 0 and r // SPREAD < STEPS
                        step, half, third = it * STEPS + r // SPREAD, r // SPREAD % 2, r % SPREAD
                        columns = iter(range(SPREAD * third, min(SPREAD * third + SPREAD, U)) if beside else ())

                        def some_tiles():
                            for u in columns:
                                hot_tiles(1, hotT2[0:P2, half, u, :], step, u)
                                return

                        if beside and third == 0:
                            dve.wait_ge(D_[1]["dealt"], step + (1 if r == 0 else 0))
                        dve.wait_ge(e["q"], g + 1)
                        dve.wait_ge(s_kv[l][rb], (it * (R1 // RB1) + r // RB1 + 1) * 16 * G)
                        o.did(v.tensor_tensor(prod[:, :, :], bank(2 + par).rearrange("p (j d) -> p j d", j=G), kv[:, rb, :, 0:D], ALU.mult))
                        some_tiles()
                        o.wait()
                        o.did(v.tensor_reduce(logit[:, :, :], prod[:, :, :].rearrange("p j (h d) -> p j h d", h=H), AX.X, ALU.add))
                        some_tiles()
                        o.wait()
                        v.tensor_scalar(att[:, par, :, :], logit[:, :, :], 10.0, -10.0, ALU.min, ALU.max).then_inc(e["clip"], 1)
                        dve.wait_ge(e["agg"], g * GP + GP)
                        build_S((r + 2) % RB1, g + 2)
                        some_tiles()
                        dve.wait_ge(e["exp"], g + 1)
                        v.tensor_tensor(vals[:, par, :, 0:D].rearrange("p j (h d) -> p j h d", h=H),
                                        kv[:, rb, :, D:2 * D].rearrange("p j (h d) -> p j h d", h=H),
                                        vals[:, par, :, D:DV][:, :, :, None].broadcast_to([128, G, H, HD]), ALU.mult).then_inc(e["vals"], 1)
                        stage_indices(rb, g + RB1)
                        if beside and third == 0:
                            hot_lanes(1, at_lane2[0:P2, half, :, :], lane_of2[0:P2, :, :], step)
                        if beside and third == 2:
                            hot_others(1, hot_other2[0:P2, half, :, :], at_lane2[0:P2, half, :, :], step)
                        assert o.n == PER
                if l == 0:
                    keep_slots(1, (6, 7))
                    own.wait()
                meet(dve, 2 + 2 * l)

            node_stage(2)
            h_ = hn[:, :, 0:NF]
            a_src, a_dst, top = hn[:, :, NF:DG], adm[:, :, 0, :], adm[:, :, 1, :]
            over = lambda a, n=NF: a[:, None, :].broadcast_to([NP, NT, n])
            by_head = lambda a: a.rearrange("p t (h e) -> p t h e", h=HG)
            dve.wait_ge(NS[2]["hc"], NT + CREDIT)
            own.did(v.tensor_tensor(t16[:, :, :], h_, over(gvec[:, 0, :]), ALU.mult))
            own.did(v.tensor_tensor(t16b[:, :, :], h_, over(gvec[:, 1, :]), ALU.mult))
            own.wait()
            own.did(v.tensor_reduce(a_dst, by_head(t16b[:, :, :]), AX.X, ALU.add))
            own.did(v.tensor_reduce(a_src, by_head(t16[:, :, :]), AX.X, ALU.add))
            own.wait()
            own.did(v.tensor_copy(part16[:, :, 0:HG], a_src))
            own.wait()
            own.did(v.tensor_tensor(t4[:, :, :], a_src, part16[:, :, 0:HG], ALU.subtract))
            own.wait()
            own.did(v.tensor_copy(part16[:, :, HG:2 * HG], t4[:, :, :]))
            own.wait()
            v.tensor_tensor(part16[:, :, 2 * HG:3 * HG], t4[:, :, :], part16[:, :, HG:2 * HG], ALU.subtract).then_inc(GS["diff"], 1)
            own.did(v.tensor_copy(mx[:, :, :], a_src))
            own.wait()
            meet(dve, 5)

            def not_S(par, group):
                v.tensor_tensor(other[:, par, :, :], iota_n[:, :][:, None, :].broadcast_to([128, G, NP]),
                                loc[1][:, ds(group * G, G)][:, :, None].broadcast_to([128, G, NP]), ALU.not_equal).then_inc(GS["other"], 1)

            def stage_rows(k, group):
                v.tensor_copy(ix[:, k, :], idx[1][:, ds(group * G, G)]).then_inc(GS["slot"], 1)

            dve.sem_inc(GS["red"], 2)
            for k in range(RB):
                stage_rows(k, k)
            not_S(0, 0)
            def keep_expert(m, t, ex):
                if ex == 0:
                    dve.wait_ge(MS["freed"], t + 1)
                dve.wait_ge(MS["out"], m + 1)
                v.tensor_tensor(ob[:, ex, :], bank(7)[0:NP, 0:DM], b2_sb[:, ex, :], ALU.add).then_inc(MS["evac"], 1)

            dve.wait_ge(s_w12, 16 * (3 * NX + 1))
            for lo, hi, per in ((0, FAST, 2), (FAST, IT2, 1)):
                with dve.Fori(lo, hi) as it:
                    for k in range(R2):
                        g, par = it * R2 + k, k % 2
                        o = Count(dve, GS["own"], g * GP)
                        _, at = nc.values_load_multi_w_load_instructions(
                            tmap[1][0:1, ds(g * GP, GP)], engines=[v.engine], min_val=0, max_val=NT - 1,
                            skip_runtime_bounds_check_because="it counts up to 24 comparisons")
                        for u in range(GP):
                            dve.wait_ge(GS["unit"], g * GP + u + 1)
                            v.tensor_reduce(tmx[:, u, :], PS[0:NP, 2 * u:2 * u + 2, :].rearrange("p b (h n) -> p (b h) n", h=2), AX.X, ALU.max).then_inc(GS["red"], 1)
                            if u == 0:
                                not_S(1 - par, g + 1)
                        dve.wait_ge(GS["red"], (g + 1) * GP + 2)
                        for u in range(GP):
                            m = flat(mx[:, ds(at[u], 1), :])
                            o.did(v.tensor_tensor(m, tmx[:, u, :], m, ALU.max))
                            o.wait()
                        dve.wait_ge(GS["keep"], g + 1)
                        stage_rows(k % RB, g + RB)
                        for i in range(per):
                            keep_expert(*work_of(it, k, i, per))
            def leaky_sum(to, a):
                own.did(v.tensor_tensor(t4[:, :, :], a, a_dst, ALU.add))
                own.wait()
                own.did(v.scalar_tensor_tensor(to, t4[:, :, :], 0.2, t4[:, :, :], ALU.mult, ALU.max))
                own.wait()

            leaky_sum(top, mx[:, :, :])
            leaky_sum(selfe[:, :, :], a_src)
            v.tensor_tensor(selfe[:, :, :], selfe[:, :, :], top, ALU.subtract).then_inc(GS["diff"], 1)
            rest = adm[:, :, :, :].rearrange("p t a h -> p t (a h)")
            own.did(v.tensor_copy(adm16[:, :, 0, :], rest))
            dve.wait_ge(GS["diff"], 2)
            for i in range(1, NPART):
                own.wait()
                own.did(v.tensor_tensor(rest, rest, adm16[:, :, i - 1, :], ALU.subtract))
                own.wait()
                own.did(v.tensor_copy(adm16[:, :, i, :], rest))
            meet(dve, 6)

            GAG = AGG[:, :, 0:DG]
            dve.wait_ge(GS["self"], 1)
            own.did(v.tensor_tensor(by_head(GAG[:, :, 0:NF]), by_head(h_), selfe[:, :, :][:, :, :, None].broadcast_to([NP, NT, HG, NX]), ALU.mult))
            own.did(v.tensor_copy(GAG[:, :, NF:DG], selfe[:, :, :]))
            own.wait()
            dve.sem_inc(GS["zero"], 1)

            def gate_S(par, group):
                v.tensor_tensor(Sg[:, par, :, :], iota_128[:, :][:, None, :].broadcast_to([128, G, 128]),
                                loc[1][:, ds(group * G, G)][:, :, None].broadcast_to([128, G, 128]), ALU.is_equal).then_inc(GS["S"], 1)

            gate_S(0, 0)
            gate_S(1, 1)
            def exponents(o, par, group, between=(None,) * 4):
                got = bank(2 + par)[:, 0:G * 2 * HG].rearrange("p (j a h) -> p j a h", j=G, a=2)
                dve.wait_ge(GS["look"], group + 1)
                o.did(v.tensor_tensor(logit[:, :, 0:HG], GAT[:, ds(group * G, G), NF:DG], got[:, :, 0, :], ALU.add))
                if between[0]:
                    between[0]()
                o.wait()
                o.did(v.scalar_tensor_tensor(logit[:, :, HG:H], logit[:, :, 0:HG], 0.2, logit[:, :, 0:HG], ALU.mult, ALU.max))
                if between[1]:
                    between[1]()
                o.wait()
                o.did(v.tensor_tensor(logit[:, :, 0:HG], logit[:, :, HG:H], got[:, :, 1, :], ALU.subtract))
                if between[2]:
                    between[2]()
                o.wait()
                v.tensor_scalar(att[:, par, :, 0:HG], logit[:, :, 0:HG], 0.0, None, ALU.min).then_inc(GS["e"], 1)
                if between[3]:
                    between[3]()

            PER2 = 7
            exponents(own, 0, 0)
            with dve.Fori(0, IT2) as it:
                for k in range(R2):
                    g, par = it * R2 + k, k % 2
                    o = Count(dve, GS["own2"], g * PER2)
                    m, m16 = msg[:, par, :, :], msg16[:, par, :, :, :]

                    def weigh():
                        o.did(v.tensor_tensor(m[:, :, 0:NF].rearrange("p j (h e) -> p j h e", h=HG),
                                              GAT[:, ds(g * G, G), 0:NF].rearrange("p j (h e) -> p j h e", h=HG),
                                              m[:, :, NF:DG][:, :, :, None].broadcast_to([128, G, HG, NX]), ALU.mult))

                    part = lambda i: (lambda: o.did(v.tensor_copy(m16[:, :, i, :], m)))
                    rest = lambda: o.did(v.tensor_tensor(m, m, m16[:, :, 0, :], ALU.subtract))
                    dve.wait_ge(GS["agg"], g * GP + GP)
                    gate_S((k + 2) % RB, g + 2)
                    dve.wait_ge(GS["exp"], g + 1)
                    exponents(o, 1 - par, g + 1, (weigh, part(0), rest, part(1)))
                    o.wait()
                    v.tensor_tensor(m16[:, :, 2, :], m, m16[:, :, 1, :], ALU.subtract).then_inc(GS["msg"], 1)
                    assert o.n == PER2
            dve.wait_ge(GS["sum"], T2 // 2 + 1)

            t, tb = t16[:, :, :], t16b[:, :, :]
            wide = lambda a, n=NF: a[:, :, None].broadcast_to([NP, NT, n])
            own.did(v.tensor_scalar(t4[:, :, :], GAG[:, :, NF:DG], 1e-16, None, ALU.add))
            own.wait()
            own.did(v.reciprocal(t4[:, :, :], t4[:, :, :]))
            own.wait()
            own.did(v.tensor_tensor(by_head(t), by_head(GAG[:, :, 0:NF]), t4[:, :, :][:, :, :, None].broadcast_to([NP, NT, HG, NX]), ALU.mult))
            own.wait()
            own.did(v.tensor_tensor(t, t, over(gvec[:, 2, :]), ALU.add))
            own.wait()
            own.did(v.tensor_reduce(t1[:, :], t, AX.X, ALU.add))
            own.wait()
            own.did(v.tensor_scalar(t1[:, :], t1[:, :], 1.0 / NF, None, ALU.mult))
            own.wait()
            own.did(v.tensor_tensor(t, t, wide(t1[:, :]), ALU.subtract))
            own.wait()
            own.did(v.tensor_tensor(tb, t, t, ALU.mult))
            own.wait()
            own.did(v.tensor_reduce(t1[:, :], tb, AX.X, ALU.add))
            own.wait()
            v.tensor_scalar(t1[:, :], t1[:, :], 1.0 / NF, 1e-5, ALU.mult, ALU.add).then_inc(GS["var"], 1)
            dve.wait_ge(GS["std"], 1)
            own.did(v.reciprocal(t1b[:, :], t1b[:, :]))
            own.wait()
            own.did(v.tensor_tensor(t, t, wide(t1b[:, :]), ALU.mult))
            own.wait()
            own.did(v.tensor_tensor(t, t, over(gvec[:, 3, :]), ALU.mult))
            own.wait()
            own.did(v.tensor_tensor(t, t, over(gvec[:, 4, :]), ALU.add))
            own.wait()
            own.did(v.tensor_reduce(score[:, :, :], t.rearrange("p t (h e) -> p t e h", h=HG), AX.X, ALU.add))
            own.wait()
            own.did(v.tensor_scalar(score[:, :, :], score[:, :, :], 1.0 / HG, None, ALU.mult))
            own.did(v.memset(rank[:, :, :], 0.0))
            own.wait()
            own.did(v.tensor_reduce(t1[:, :], score[:, :, :], AX.X, ALU.max))
            for j in range(NX):
                sj = score[:, :, j]
                own.did(v.tensor_tensor(gate[:, :, :], wide(sj, NX), score[:, :, :], ALU.is_gt))
                own.wait()
                own.did(v.tensor_tensor(rank[:, :, :], rank[:, :, :], gate[:, :, :], ALU.add))
                own.wait()
                if j + 1 < NX:
                    own.did(v.tensor_tensor(gate[:, :, j + 1:], wide(sj, NX - 1 - j), score[:, :, j + 1:], ALU.is_equal))
                    own.wait()
                    own.did(v.tensor_tensor(rank[:, :, j + 1:], rank[:, :, j + 1:], gate[:, :, j + 1:], ALU.add))
                    own.wait()
            v.tensor_tensor(t4[:, :, :], score[:, :, :], wide(t1[:, :], NX), ALU.subtract).then_inc(GS["s"], 1)
            dve.wait_ge(GS["sexp"], 1)
            own.did(v.scalar_tensor_tensor(gate[:, :, :], rank[:, :, :], 1.5, e4[:, :, :], ALU.is_lt, ALU.mult))
            own.wait()
            own.did(v.tensor_reduce(t1[:, :], gate[:, :, :], AX.X, ALU.add))
            own.wait()
            own.did(v.reciprocal(t1[:, :], t1[:, :]))
            own.wait()
            own.did(v.tensor_tensor(gate[:, :, :], gate[:, :, :], wide(t1[:, :], NX), ALU.mult))
            own.wait()
            meet(dve, 7)

            dve.sem_inc(MS["acc"], CH)
            with dve.Fori(0, NCH) as c:
                o = Count(dve, MS["own"], c * (NX - 1) * CH)
                for ex in range(NX):
                    if ex:
                        o.wait()
                    for k in range(CH):
                        xk = flat(X[:, ds(c * CH + k, 1), :])
                        if ex == 0:
                            dve.wait_ge(s_back[k], (c + 1) * 16)
                        added = v.scalar_tensor_tensor(xk, spilled[:, k, ex, :], flat(gate[:, ds(c * CH + k, 1), ex:ex + 1]), xk, ALU.mult, ALU.add)
                        if ex + 1 < NX:
                            o.did(added)
                        else:
                            added.then_inc(MS["acc"], 1)


_INS = ['x', 'src', 'dst', 'L0_gnn_W_P_w', 'L0_gnn_W_P_b', 'L0_gnn_W_pos', 'L0_gnn_q1', 'L0_gnn_k1', 'L0_gnn_v1',
        'L0_gnn_ln1_s', 'L0_gnn_ln1_b', 'L0_gnn_q2', 'L0_gnn_k2', 'L0_gnn_v2', 'L0_gnn_ln2_s', 'L0_gnn_ln2_b',
        'L0_gnn_inv_w', 'L0_gnn_inv_b', 'L0_ffn_W_gat', 'L0_ffn_att_src', 'L0_ffn_att_dst', 'L0_ffn_b_gat',
        'L0_ffn_ln_gamma', 'L0_ffn_ln_beta', 'L0_ffn_W1', 'L0_ffn_b1', 'L0_ffn_W2', 'L0_ffn_b2', 'L0_ffn_edge_index']


def kernel(**inputs):
    import numpy as np
    import concourse.bacc as bacc
    from concourse.bass_utils import run_bass_kernel_spmd

    nc = bacc.Bacc("TRN2", target_bir_lowering=False, num_devices=1)
    arrays, args = {}, []
    for name in _INS:
        a = np.ascontiguousarray(inputs[name])
        arrays[f"in_{name}"] = a
        args.append(nc.dram_tensor(f"in_{name}", a.shape, mybir.dt.from_np(a.dtype), kind="ExternalInput").ap())
    out = nc.dram_tensor("out", inputs["x"].shape, mybir.dt.float32, kind="ExternalOutput").ap()
    graph_block_kernel(nc, *args, out)
    r = run_bass_kernel_spmd(nc, [arrays], core_ids=[0])
    return r.results[0]["out"]
```
